# Optimizing a Trainium2 kernel written in Bass

```python
import numpy as np
import jax
import jax.numpy as jnp

def _softmax(x, axis=-1):
    return jax.nn.softmax(x, axis=axis)

def _gelu(x):
    return jax.nn.gelu(x, approximate=True)

def _silu(x):
    return jax.nn.silu(x)

def _sigmoid(x):
    return jax.nn.sigmoid(x)

def _layernorm(x, axis=-1, eps=1e-05):
    m = jnp.mean(x, axis=axis, keepdims=True)
    v = jnp.var(x, axis=axis, keepdims=True)
    return (x - m) / jnp.sqrt(v + eps)

def _scatter_add(tgt, idx, src, axis=0):
    return tgt.at[idx].add(src)

def _segment_sum(src, seg, n):
    return jax.ops.segment_sum(src, seg, n)
kernel_name = 'mk_macaron_d2_jaxref_r8_976b0c'

def setup_inputs(seed: int=0):
    np.random.seed(seed)
    _w = jnp.asarray

    def _L0_attn_setup():
        import jax, jax.numpy as jnp
        import numpy as np
        B, N, C = (2, 256, 128)
        H = 16
        D = C // H
        key = jax.random.key(seed)
        ks = jax.random.split(key, 5)
        s = 0.02
        return {'x': jax.random.normal(ks[0], (B, N, C), dtype=jnp.float32), 'qkv_w': jax.random.normal(ks[1], (C, 3 * C), dtype=jnp.float32) * s, 'qkv_b': jax.random.normal(ks[2], (3 * C,), dtype=jnp.float32) * s, 'proj_w': jax.random.normal(ks[3], (C, C), dtype=jnp.float32) * s, 'proj_b': jax.random.normal(ks[4], (C,), dtype=jnp.float32) * s}
    _L0_attn_in = _L0_attn_setup()

    def _L0_ffn_setup():
        import jax, jax.numpy as jnp
        import numpy as np
        DIM = 128
        E = 16
        TOPK = 2
        G = 4
        TOPK_G = 2
        INTER = 64
        N_SHARED = 2
        ROUTE_SCALE = 1.0

        def _gate(xf, gate_w, gate_b):
            scores = xf @ gate_w.T
            scores = jax.nn.softmax(scores.astype(jnp.float32), axis=-1)
            orig = scores
            scores = scores + gate_b
            T = xf.shape[0]
            sg = scores.reshape(T, G, E // G)
            group_scores = jax.lax.top_k(sg, 2)[0].sum(-1)
            _, gidx = jax.lax.top_k(group_scores, TOPK_G)
            keep = jax.nn.one_hot(gidx, G).sum(axis=1) > 0
            sg = jnp.where(keep[:, :, None], sg, -jnp.inf)
            scores = sg.reshape(T, E)
            _, idx = jax.lax.top_k(scores, TOPK)
            weights = jnp.take_along_axis(orig, idx, axis=1)
            weights = (weights * ROUTE_SCALE).astype(xf.dtype)
            return (weights, idx)
        key = jax.random.key(seed)
        ks = jax.random.split(key, 16)
        s = lambda fan_in: 1.0 / np.sqrt(fan_in)
        inp = {'x': jax.random.normal(ks[0], (4, 128, DIM), dtype=jnp.float32), 'gate_w': jax.random.normal(ks[1], (E, DIM), dtype=jnp.float32) * s(DIM), 'gate_b': jnp.zeros((E,), dtype=jnp.float32), 'We1': jax.random.normal(ks[2], (E, DIM, INTER), dtype=jnp.float32) * s(DIM), 'be1': jnp.zeros((E, INTER), dtype=jnp.float32), 'We2': jax.random.normal(ks[3], (E, INTER, DIM), dtype=jnp.float32) * s(INTER), 'be2': jnp.zeros((E, DIM), dtype=jnp.float32), 'We3': jax.random.normal(ks[4], (E, DIM, INTER), dtype=jnp.float32) * s(DIM), 'be3': jnp.zeros((E, INTER), dtype=jnp.float32), 'ws1': jax.random.normal(ks[5], (DIM, N_SHARED * INTER), dtype=jnp.float32) * s(DIM), 'bs1': jnp.zeros((N_SHARED * INTER,), dtype=jnp.float32), 'ws2': jax.random.normal(ks[6], (N_SHARED * INTER, DIM), dtype=jnp.float32) * s(N_SHARED * INTER), 'bs2': jnp.zeros((DIM,), dtype=jnp.float32), 'ws3': jax.random.normal(ks[7], (DIM, N_SHARED * INTER), dtype=jnp.float32) * s(DIM), 'bs3': jnp.zeros((N_SHARED * INTER,), dtype=jnp.float32)}
        return inp
    _L0_ffn_in = _L0_ffn_setup()

    def _L1_attn_setup():
        import jax, jax.numpy as jnp
        import numpy as np
        B, N, D = (4, 512, 128)
        H, DH = (16, 64)
        DFF = 512
        M = 64
        EPS_KERN = 1e-06
        EPS_LN = 1e-06

        def _softmax_kernel_feats(data, proj, is_query):
            dn = 1.0 / jnp.sqrt(jnp.sqrt(jnp.float32(data.shape[-1])))
            ratio = 1.0 / jnp.sqrt(jnp.float32(proj.shape[0]))
            data_dash = jnp.einsum('bnhd,md->bnhm', data * dn, proj)
            diag = jnp.sum(jnp.square(data), axis=-1, keepdims=True) * (dn * dn) / 2.0
            if is_query:
                mx = jnp.max(data_dash, axis=-1, keepdims=True)
            else:
                mx = jnp.max(data_dash)
            return ratio * (jnp.exp(data_dash - diag - mx) + EPS_KERN)

        def _layernorm(x, g, b):
            mu = jnp.mean(x, axis=-1, keepdims=True)
            var = jnp.mean(jnp.square(x - mu), axis=-1, keepdims=True)
            return (x - mu) * jax.lax.rsqrt(var + EPS_LN) * g + b

        def _encoder_forward(x, Wq, Wk, Wv, Wo, proj, W1, b1, W2, b2, ln1_g, ln1_b, ln2_g, ln2_b):
            q = jnp.einsum('bnd,dhk->bnhk', x, Wq)
            k = jnp.einsum('bnd,dhk->bnhk', x, Wk)
            v = jnp.einsum('bnd,dhk->bnhk', x, Wv)
            qf = _softmax_kernel_feats(q, proj, True)
            kf = _softmax_kernel_feats(k, proj, False)
            kv = jnp.einsum('bnhm,bnhd->bhmd', kf, v)
            num = jnp.einsum('bnhm,bhmd->bnhd', qf, kv)
            den = jnp.einsum('bnhm,bhm->bnh', qf, jnp.sum(kf, axis=1))
            attn = num / den[..., None]
            attn_out = jnp.einsum('bnhd,hdo->bno', attn, Wo)
            out1 = _layernorm(x + attn_out, ln1_g, ln1_b)
            h = jax.nn.elu(out1 @ W1 + b1)
            ffn_out = h @ W2 + b2
            return _layernorm(out1 + ffn_out, ln2_g, ln2_b)
        key = jax.random.key(seed)
        ks = jax.random.split(key, 12)
        s = 0.02
        inp = {'x': jax.random.normal(ks[0], (B, N, D), jnp.float32), 'Wq': jax.random.normal(ks[1], (D, H, DH), jnp.float32) * s, 'Wk': jax.random.normal(ks[2], (D, H, DH), jnp.float32) * s, 'Wv': jax.random.normal(ks[3], (D, H, DH), jnp.float32) * s, 'Wo': jax.random.normal(ks[4], (H, DH, D), jnp.float32) * s, 'proj': jax.random.normal(ks[5], (M, DH), jnp.float32), 'W1': jax.random.normal(ks[6], (D, DFF), jnp.float32) * s, 'b1': jnp.zeros((DFF,), jnp.float32), 'W2': jax.random.normal(ks[7], (DFF, D), jnp.float32) * s, 'b2': jnp.zeros((D,), jnp.float32), 'ln1_g': jnp.ones((D,), jnp.float32), 'ln1_b': jnp.zeros((D,), jnp.float32), 'ln2_g': jnp.ones((D,), jnp.float32), 'ln2_b': jnp.zeros((D,), jnp.float32)}
        return inp
    _L1_attn_in = _L1_attn_setup()

    def _L1_ffn_setup():
        import jax, jax.numpy as jnp
        import numpy as np
        D_MODEL = 128
        NUM_TILES = 64
        TPC = 8
        NUM_CLUSTERS = NUM_TILES // TPC
        GRID = 16
        COMP_H = 32
        NUM_KNOTS = 8
        EPS_LN = 1e-05

        def _calibrate(scores, knots, temperature):
            K = knots.shape[0]
            normalized = jax.nn.sigmoid(scores / (temperature[0] + 1e-06))
            idx_float = normalized * (K - 1)
            idx_low = jnp.clip(idx_float.astype(jnp.int32), 0, K - 2)
            idx_high = idx_low + 1
            t = idx_float - idx_low.astype(scores.dtype)
            val_low = knots[idx_low]
            val_high = knots[idx_high]
            return val_low + t * (val_high - val_low)

        def _forward(x, signatures_raw, knot_values, temperature, compress_w1, compress_b1, compress_w2, compress_b2, spline_w1, spline_b1, spline_w2, spline_b2, directions, norm_gamma, norm_beta, output_scale):
            B, T, D = x.shape
            xf = x.reshape(-1, D)
            q = jnp.where(signatures_raw > 0.3, 1.0, jnp.where(signatures_raw < -0.3, -1.0, 0.0)).astype(signatures_raw.dtype)
            sigs = signatures_raw + jax.lax.stop_gradient(q - signatures_raw)
            cluster_sigs = jnp.sign(sigs.reshape(NUM_CLUSTERS, TPC, D).mean(axis=1))
            cluster_scores = xf @ cluster_sigs.T
            cluster_gates = _calibrate(cluster_scores, knot_values, temperature)
            cluster_idx = jnp.argmax(cluster_gates, axis=-1)
            tile_scores = xf @ sigs.T
            tile_gates = _calibrate(tile_scores, knot_values, temperature)
            gates_by_cluster = tile_gates.reshape(-1, NUM_CLUSTERS, TPC)
            sel_gates = jnp.take_along_axis(gates_by_cluster, cluster_idx[:, None, None], axis=1)[:, 0, :]
            local_idx = jnp.argmax(sel_gates, axis=-1)
            tile_idx = cluster_idx * TPC + local_idx
            h = jax.nn.gelu(xf @ compress_w1 + compress_b1, approximate=False)
            comp = jnp.tanh(h @ compress_w2 + compress_b2)
            w1 = spline_w1[tile_idx]
            b1 = spline_b1[tile_idx]
            hh = jax.nn.relu(jnp.einsum('ni,nig->ng', comp, w1) + b1)
            w2 = spline_w2[tile_idx]
            b2 = spline_b2[tile_idx]
            mag = jnp.einsum('ng,ngo->no', hh, w2) + b2
            ffn_out = mag * directions[tile_idx] * output_scale[0]
            y = xf + ffn_out
            mu = y.mean(axis=-1, keepdims=True)
            var = ((y - mu) ** 2).mean(axis=-1, keepdims=True)
            y = (y - mu) / jnp.sqrt(var + EPS_LN) * norm_gamma + norm_beta
            return y.reshape(B, T, D)
        key = jax.random.key(seed)
        ks = jax.random.split(key, 12)
        B, T = (4, 512)
        x = jax.random.normal(ks[0], (B, T, D_MODEL), dtype=jnp.float32)
        signatures_raw = jax.random.normal(ks[1], (NUM_TILES, D_MODEL), dtype=jnp.float32) * 0.5
        knot_values = jax.nn.sigmoid(jnp.linspace(-3.0, 3.0, NUM_KNOTS).astype(jnp.float32))
        temperature = jnp.ones((1,), dtype=jnp.float32)
        compress_w1 = jax.random.normal(ks[2], (D_MODEL, COMP_H), dtype=jnp.float32) * (1.0 / np.sqrt(D_MODEL))
        compress_b1 = jnp.zeros((COMP_H,), dtype=jnp.float32)
        compress_w2 = jax.random.normal(ks[3], (COMP_H, 2), dtype=jnp.float32) * (1.0 / np.sqrt(COMP_H))
        compress_b2 = jnp.zeros((2,), dtype=jnp.float32)
        spline_w1 = jax.random.normal(ks[4], (NUM_TILES, 2, GRID), dtype=jnp.float32) * (1.0 / np.sqrt(2.0))
        spline_b1 = jnp.zeros((NUM_TILES, GRID), dtype=jnp.float32)
        spline_w2 = jax.random.normal(ks[5], (NUM_TILES, GRID, 1), dtype=jnp.float32) * (1.0 / np.sqrt(GRID))
        spline_b2 = jnp.zeros((NUM_TILES, 1), dtype=jnp.float32)
        directions = jax.random.normal(ks[6], (NUM_TILES, D_MODEL), dtype=jnp.float32) * 0.02
        norm_gamma = jnp.ones((D_MODEL,), dtype=jnp.float32)
        norm_beta = jnp.zeros((D_MODEL,), dtype=jnp.float32)
        output_scale = jnp.ones((1,), dtype=jnp.float32) * 0.1
        return dict(x=x, signatures_raw=signatures_raw, knot_values=knot_values, temperature=temperature, compress_w1=compress_w1, compress_b1=compress_b1, compress_w2=compress_w2, compress_b2=compress_b2, spline_w1=spline_w1, spline_b1=spline_b1, spline_w2=spline_w2, spline_b2=spline_b2, directions=directions, norm_gamma=norm_gamma, norm_beta=norm_beta, output_scale=output_scale)
    _L1_ffn_in = _L1_ffn_setup()
    _d = {'L0_attn_x': _L0_attn_in['x'], 'L0_attn_qkv_w': _L0_attn_in['qkv_w'], 'L0_attn_qkv_b': _L0_attn_in['qkv_b'], 'L0_attn_proj_w': _L0_attn_in['proj_w'], 'L0_attn_proj_b': _L0_attn_in['proj_b'], 'L0_ffn_gate_w': _L0_ffn_in['gate_w'], 'L0_ffn_gate_b': _L0_ffn_in['gate_b'], 'L0_ffn_We1': _L0_ffn_in['We1'], 'L0_ffn_be1': _L0_ffn_in['be1'], 'L0_ffn_We2': _L0_ffn_in['We2'], 'L0_ffn_be2': _L0_ffn_in['be2'], 'L0_ffn_We3': _L0_ffn_in['We3'], 'L0_ffn_be3': _L0_ffn_in['be3'], 'L0_ffn_ws1': _L0_ffn_in['ws1'], 'L0_ffn_bs1': _L0_ffn_in['bs1'], 'L0_ffn_ws2': _L0_ffn_in['ws2'], 'L0_ffn_bs2': _L0_ffn_in['bs2'], 'L0_ffn_ws3': _L0_ffn_in['ws3'], 'L0_ffn_bs3': _L0_ffn_in['bs3'], 'L1_attn_Wq': _L1_attn_in['Wq'], 'L1_attn_Wk': _L1_attn_in['Wk'], 'L1_attn_Wv': _L1_attn_in['Wv'], 'L1_attn_Wo': _L1_attn_in['Wo'], 'L1_attn_proj': _L1_attn_in['proj'], 'L1_attn_W1': _L1_attn_in['W1'], 'L1_attn_b1': _L1_attn_in['b1'], 'L1_attn_W2': _L1_attn_in['W2'], 'L1_attn_b2': _L1_attn_in['b2'], 'L1_attn_ln1_g': _L1_attn_in['ln1_g'], 'L1_attn_ln1_b': _L1_attn_in['ln1_b'], 'L1_attn_ln2_g': _L1_attn_in['ln2_g'], 'L1_attn_ln2_b': _L1_attn_in['ln2_b'], 'L1_ffn_signatures_raw': _L1_ffn_in['signatures_raw'], 'L1_ffn_knot_values': _L1_ffn_in['knot_values'], 'L1_ffn_temperature': _L1_ffn_in['temperature'], 'L1_ffn_compress_w1': _L1_ffn_in['compress_w1'], 'L1_ffn_compress_b1': _L1_ffn_in['compress_b1'], 'L1_ffn_compress_w2': _L1_ffn_in['compress_w2'], 'L1_ffn_compress_b2': _L1_ffn_in['compress_b2'], 'L1_ffn_spline_w1': _L1_ffn_in['spline_w1'], 'L1_ffn_spline_b1': _L1_ffn_in['spline_b1'], 'L1_ffn_spline_w2': _L1_ffn_in['spline_w2'], 'L1_ffn_spline_b2': _L1_ffn_in['spline_b2'], 'L1_ffn_directions': _L1_ffn_in['directions'], 'L1_ffn_norm_gamma': _L1_ffn_in['norm_gamma'], 'L1_ffn_norm_beta': _L1_ffn_in['norm_beta'], 'L1_ffn_output_scale': _L1_ffn_in['output_scale']}
    _x0 = _d['L0_attn_x']
    _d['L0_attn_x'] = jax.random.normal(jax.random.fold_in(jax.random.key(seed), 1), (16, 512, 128), dtype=_x0.dtype)
    del _x0
    return _d

def reference(L0_attn_x, L0_attn_qkv_w, L0_attn_qkv_b, L0_attn_proj_w, L0_attn_proj_b, L0_ffn_gate_w, L0_ffn_gate_b, L0_ffn_We1, L0_ffn_be1, L0_ffn_We2, L0_ffn_be2, L0_ffn_We3, L0_ffn_be3, L0_ffn_ws1, L0_ffn_bs1, L0_ffn_ws2, L0_ffn_bs2, L0_ffn_ws3, L0_ffn_bs3, L1_attn_Wq, L1_attn_Wk, L1_attn_Wv, L1_attn_Wo, L1_attn_proj, L1_attn_W1, L1_attn_b1, L1_attn_W2, L1_attn_b2, L1_attn_ln1_g, L1_attn_ln1_b, L1_attn_ln2_g, L1_attn_ln2_b, L1_ffn_signatures_raw, L1_ffn_knot_values, L1_ffn_temperature, L1_ffn_compress_w1, L1_ffn_compress_b1, L1_ffn_compress_w2, L1_ffn_compress_b2, L1_ffn_spline_w1, L1_ffn_spline_b1, L1_ffn_spline_w2, L1_ffn_spline_b2, L1_ffn_directions, L1_ffn_norm_gamma, L1_ffn_norm_beta, L1_ffn_output_scale):

    def _L0_attn_ref(x, qkv_w, qkv_b, proj_w, proj_b):
        import jax, jax.numpy as jnp
        import numpy as np
        B, N, C = (2, 256, 128)
        H = 16
        D = C // H
        b, n, c = x.shape
        scale = (c // H) ** (-0.5)
        qkv = x @ qkv_w + qkv_b
        qkv = qkv.reshape(b, n, 3, H, D)
        q, k, v = jnp.moveaxis(qkv, 2, 0)
        attn = jnp.einsum('bnhd,bmhd->bhnm', q, k) * scale
        attn = jax.nn.softmax(attn, axis=-1)
        out = jnp.einsum('bhnm,bmhd->bnhd', attn, v).reshape(b, n, c)
        out = out @ proj_w + proj_b
        return out

    def _L0_ffn_ref(x, gate_w, gate_b, We1, be1, We2, be2, We3, be3, ws1, bs1, ws2, bs2, ws3, bs3):
        import jax, jax.numpy as jnp
        import numpy as np
        DIM = 128
        E = 16
        TOPK = 2
        G = 4
        TOPK_G = 2
        INTER = 64
        N_SHARED = 2
        ROUTE_SCALE = 1.0

        def _gate(xf, gate_w, gate_b):
            scores = xf @ gate_w.T
            scores = jax.nn.softmax(scores.astype(jnp.float32), axis=-1)
            orig = scores
            scores = scores + gate_b
            T = xf.shape[0]
            sg = scores.reshape(T, G, E // G)
            group_scores = jax.lax.top_k(sg, 2)[0].sum(-1)
            _, gidx = jax.lax.top_k(group_scores, TOPK_G)
            keep = jax.nn.one_hot(gidx, G).sum(axis=1) > 0
            sg = jnp.where(keep[:, :, None], sg, -jnp.inf)
            scores = sg.reshape(T, E)
            _, idx = jax.lax.top_k(scores, TOPK)
            weights = jnp.take_along_axis(orig, idx, axis=1)
            weights = (weights * ROUTE_SCALE).astype(xf.dtype)
            return (weights, idx)
        shape = x.shape
        xf = x.reshape(-1, DIM)
        weights, idx = _gate(xf, gate_w, gate_b)
        combine = (jax.nn.one_hot(idx, E, dtype=xf.dtype) * weights[..., None]).sum(1)
        h1 = jnp.einsum('td,edi->tei', xf, We1) + be1
        h3 = jnp.einsum('td,edi->tei', xf, We3) + be3
        h = jax.nn.silu(h1) * h3
        yo = jnp.einsum('tei,eid->ted', h, We2) + be2
        y = jnp.einsum('te,ted->td', combine, yo)
        z = jax.nn.silu(xf @ ws1 + bs1) * (xf @ ws3 + bs3) @ ws2 + bs2
        return (y + z).reshape(shape)

    def _L1_attn_ref(x, Wq, Wk, Wv, Wo, proj, W1, b1, W2, b2, ln1_g, ln1_b, ln2_g, ln2_b):
        import jax, jax.numpy as jnp
        import numpy as np
        B, N, D = (4, 512, 128)
        H, DH = (16, 64)
        DFF = 512
        M = 64
        EPS_KERN = 1e-06
        EPS_LN = 1e-06

        def _softmax_kernel_feats(data, proj, is_query):
            dn = 1.0 / jnp.sqrt(jnp.sqrt(jnp.float32(data.shape[-1])))
            ratio = 1.0 / jnp.sqrt(jnp.float32(proj.shape[0]))
            data_dash = jnp.einsum('bnhd,md->bnhm', data * dn, proj)
            diag = jnp.sum(jnp.square(data), axis=-1, keepdims=True) * (dn * dn) / 2.0
            if is_query:
                mx = jnp.max(data_dash, axis=-1, keepdims=True)
            else:
                mx = jnp.max(data_dash)
            return ratio * (jnp.exp(data_dash - diag - mx) + EPS_KERN)

        def _layernorm(x, g, b):
            mu = jnp.mean(x, axis=-1, keepdims=True)
            var = jnp.mean(jnp.square(x - mu), axis=-1, keepdims=True)
            return (x - mu) * jax.lax.rsqrt(var + EPS_LN) * g + b

        def _encoder_forward(x, Wq, Wk, Wv, Wo, proj, W1, b1, W2, b2, ln1_g, ln1_b, ln2_g, ln2_b):
            q = jnp.einsum('bnd,dhk->bnhk', x, Wq)
            k = jnp.einsum('bnd,dhk->bnhk', x, Wk)
            v = jnp.einsum('bnd,dhk->bnhk', x, Wv)
            qf = _softmax_kernel_feats(q, proj, True)
            kf = _softmax_kernel_feats(k, proj, False)
            kv = jnp.einsum('bnhm,bnhd->bhmd', kf, v)
            num = jnp.einsum('bnhm,bhmd->bnhd', qf, kv)
            den = jnp.einsum('bnhm,bhm->bnh', qf, jnp.sum(kf, axis=1))
            attn = num / den[..., None]
            attn_out = jnp.einsum('bnhd,hdo->bno', attn, Wo)
            out1 = _layernorm(x + attn_out, ln1_g, ln1_b)
            h = jax.nn.elu(out1 @ W1 + b1)
            ffn_out = h @ W2 + b2
            return _layernorm(out1 + ffn_out, ln2_g, ln2_b)
        return _encoder_forward(x, Wq, Wk, Wv, Wo, proj, W1, b1, W2, b2, ln1_g, ln1_b, ln2_g, ln2_b)

    def _L1_ffn_ref(x, signatures_raw, knot_values, temperature, compress_w1, compress_b1, compress_w2, compress_b2, spline_w1, spline_b1, spline_w2, spline_b2, directions, norm_gamma, norm_beta, output_scale):
        import jax, jax.numpy as jnp
        import numpy as np
        D_MODEL = 128
        NUM_TILES = 64
        TPC = 8
        NUM_CLUSTERS = NUM_TILES // TPC
        GRID = 16
        COMP_H = 32
        NUM_KNOTS = 8
        EPS_LN = 1e-05

        def _calibrate(scores, knots, temperature):
            K = knots.shape[0]
            normalized = jax.nn.sigmoid(scores / (temperature[0] + 1e-06))
            idx_float = normalized * (K - 1)
            idx_low = jnp.clip(idx_float.astype(jnp.int32), 0, K - 2)
            idx_high = idx_low + 1
            t = idx_float - idx_low.astype(scores.dtype)
            val_low = knots[idx_low]
            val_high = knots[idx_high]
            return val_low + t * (val_high - val_low)

        def _forward(x, signatures_raw, knot_values, temperature, compress_w1, compress_b1, compress_w2, compress_b2, spline_w1, spline_b1, spline_w2, spline_b2, directions, norm_gamma, norm_beta, output_scale):
            B, T, D = x.shape
            xf = x.reshape(-1, D)
            q = jnp.where(signatures_raw > 0.3, 1.0, jnp.where(signatures_raw < -0.3, -1.0, 0.0)).astype(signatures_raw.dtype)
            sigs = signatures_raw + jax.lax.stop_gradient(q - signatures_raw)
            cluster_sigs = jnp.sign(sigs.reshape(NUM_CLUSTERS, TPC, D).mean(axis=1))
            cluster_scores = xf @ cluster_sigs.T
            cluster_gates = _calibrate(cluster_scores, knot_values, temperature)
            cluster_idx = jnp.argmax(cluster_gates, axis=-1)
            tile_scores = xf @ sigs.T
            tile_gates = _calibrate(tile_scores, knot_values, temperature)
            gates_by_cluster = tile_gates.reshape(-1, NUM_CLUSTERS, TPC)
            sel_gates = jnp.take_along_axis(gates_by_cluster, cluster_idx[:, None, None], axis=1)[:, 0, :]
            local_idx = jnp.argmax(sel_gates, axis=-1)
            tile_idx = cluster_idx * TPC + local_idx
            h = jax.nn.gelu(xf @ compress_w1 + compress_b1, approximate=False)
            comp = jnp.tanh(h @ compress_w2 + compress_b2)
            w1 = spline_w1[tile_idx]
            b1 = spline_b1[tile_idx]
            hh = jax.nn.relu(jnp.einsum('ni,nig->ng', comp, w1) + b1)
            w2 = spline_w2[tile_idx]
            b2 = spline_b2[tile_idx]
            mag = jnp.einsum('ng,ngo->no', hh, w2) + b2
            ffn_out = mag * directions[tile_idx] * output_scale[0]
            y = xf + ffn_out
            mu = y.mean(axis=-1, keepdims=True)
            var = ((y - mu) ** 2).mean(axis=-1, keepdims=True)
            y = (y - mu) / jnp.sqrt(var + EPS_LN) * norm_gamma + norm_beta
            return y.reshape(B, T, D)
        return _forward(x, signatures_raw, knot_values, temperature, compress_w1, compress_b1, compress_w2, compress_b2, spline_w1, spline_b1, spline_w2, spline_b2, directions, norm_gamma, norm_beta, output_scale)
    x = L0_attn_x
    x = x + 0.5 * _L0_ffn_ref(_layernorm(x, axis=-1), L0_ffn_gate_w, L0_ffn_gate_b, L0_ffn_We1, L0_ffn_be1, L0_ffn_We2, L0_ffn_be2, L0_ffn_We3, L0_ffn_be3, L0_ffn_ws1, L0_ffn_bs1, L0_ffn_ws2, L0_ffn_bs2, L0_ffn_ws3, L0_ffn_bs3)
    x = x + _L0_attn_ref(_layernorm(x, axis=-1), L0_attn_qkv_w, L0_attn_qkv_b, L0_attn_proj_w, L0_attn_proj_b)
    x = x + 0.5 * _L0_ffn_ref(_layernorm(x, axis=-1), L0_ffn_gate_w, L0_ffn_gate_b, L0_ffn_We1, L0_ffn_be1, L0_ffn_We2, L0_ffn_be2, L0_ffn_We3, L0_ffn_be3, L0_ffn_ws1, L0_ffn_bs1, L0_ffn_ws2, L0_ffn_bs2, L0_ffn_ws3, L0_ffn_bs3)
    x = x + 0.5 * _L1_ffn_ref(_layernorm(x, axis=-1), L1_ffn_signatures_raw, L1_ffn_knot_values, L1_ffn_temperature, L1_ffn_compress_w1, L1_ffn_compress_b1, L1_ffn_compress_w2, L1_ffn_compress_b2, L1_ffn_spline_w1, L1_ffn_spline_b1, L1_ffn_spline_w2, L1_ffn_spline_b2, L1_ffn_directions, L1_ffn_norm_gamma, L1_ffn_norm_beta, L1_ffn_output_scale)
    x = x + _L1_attn_ref(_layernorm(x, axis=-1), L1_attn_Wq, L1_attn_Wk, L1_attn_Wv, L1_attn_Wo, L1_attn_proj, L1_attn_W1, L1_attn_b1, L1_attn_W2, L1_attn_b2, L1_attn_ln1_g, L1_attn_ln1_b, L1_attn_ln2_g, L1_attn_ln2_b)
    x = x + 0.5 * _L1_ffn_ref(_layernorm(x, axis=-1), L1_ffn_signatures_raw, L1_ffn_knot_values, L1_ffn_temperature, L1_ffn_compress_w1, L1_ffn_compress_b1, L1_ffn_compress_w2, L1_ffn_compress_b2, L1_ffn_spline_w1, L1_ffn_spline_b1, L1_ffn_spline_w2, L1_ffn_spline_b2, L1_ffn_directions, L1_ffn_norm_gamma, L1_ffn_norm_beta, L1_ffn_output_scale)
    return x

_drawn_inputs = setup_inputs


def setup_inputs(seed=0):
    import zlib

    import numpy as np

    out = dict(_drawn_inputs(seed))
    spreads = {'L0_ffn_gate_b': (0.0, 0.1),
     'L0_ffn_be1': (0.0, 0.542),
     'L0_ffn_be2': (0.0, 0.346),
     'L0_ffn_be3': (0.0, 0.555),
     'L0_ffn_bs1': (0.0, 0.1),
     'L0_ffn_bs2': (0.0, 0.1),
     'L0_ffn_bs3': (0.0, 0.1),
     'L1_attn_b1': (0.0, 0.448),
     'L1_attn_b2': (0.0, 0.1),
     'L1_attn_ln1_g': (1.0, 0.2),
     'L1_attn_ln1_b': (0.0, 0.1),
     'L1_attn_ln2_g': (1.0, 0.2),
     'L1_attn_ln2_b': (0.0, 0.1),
     'L1_ffn_compress_b1': (0.0, 0.8),
     'L1_ffn_compress_b2': (0.0, 2.0),
     'L1_ffn_spline_b1': (0.0, 2.0),
     'L1_ffn_spline_b2': (0.0, 2.0),
     'L1_ffn_norm_gamma': (1.0, 0.2),
     'L1_ffn_norm_beta': (0.0, 0.1)}
    factors = {'L0_attn_qkv_w': 8.0,
     'L0_attn_qkv_b': 8.0,
     'L0_attn_proj_w': 8.0,
     'L0_attn_proj_b': 2.789,
     'L1_attn_Wq': 64.0,
     'L1_attn_Wk': 64.0,
     'L1_attn_Wv': 8.0,
     'L1_attn_Wo': 8.0,
     'L1_attn_proj': 64.0,
     'L1_ffn_signatures_raw': 8.0,
     'L1_ffn_knot_values': 8.0,
     'L1_ffn_compress_w1': 8.0,
     'L1_ffn_compress_w2': 8.0,
     'L1_ffn_spline_w1': 8.0,
     'L1_ffn_spline_w2': 8.0,
     'L1_ffn_directions': 8.0}
    for name, (base, spread) in spreads.items():
        noise = np.random.default_rng([zlib.crc32(name.encode()), seed]).standard_normal(out[name].shape)
        drawn = base * np.exp(spread * noise) if base else spread * noise
        out[name] = jnp.asarray(drawn.astype(out[name].dtype))
    for name, factor in factors.items():
        out[name] = (out[name] * factor).astype(out[name].dtype)
    return out
```

```python
from contextlib import ExitStack

import numpy as np

import concourse.bass as bass
from concourse import mybir

F32 = mybir.dt.float32
F32R = mybir.dt.float32r
ALU = mybir.AluOpType
ACT = mybir.ActivationFunctionType
AX = mybir.AxisListType.X

P = 128
C = 128
TILES = 4
GROUP = TILES * P
BIG = 3.0e38


class Queue:

    def __init__(self, nc, engine, name, ctx):
        self.nc, self.engine, self.name = nc, engine, name
        self.sem = ctx.enter_context(nc.semaphore(name))
        self.count = 0
        self.items = []
        self.seen = {}

    def wait(self, *marks):
        for mark in marks:
            if mark is None:
                continue
            if isinstance(mark, list):
                self.wait(*mark)
                continue
            sem, value = mark
            if self.seen.get(id(sem), 0) < value:
                self.seen[id(sem)] = value
                self.items.append(lambda s=sem, v=value: self.engine.wait_ge(s, v))
        return self

    def do(self, build, *args, signal=True, **options):
        if not signal:
            self.items.append(lambda: build(*args, **options))
            return None
        self.count += 1
        self.items.append(lambda: build(*args, **options).then_inc(self.sem, 1))
        return (self.sem, self.count)

    def then(self, build, *args, **options):
        self.wait((self.sem, self.count))
        return self.do(build, *args, **options)

    def replay(self):
        for item in self.items:
            item()


class Slot:

    def __init__(self, ap):
        self.ap = ap
        self.free = []

    @property
    def free(self):
        return self.marks

    @free.setter
    def free(self, marks):
        self.marks, self.held = marks, False

    def claim(self):
        assert not self.held, self.ap
        self.held = True
        return self


class Ring:

    def __init__(self, aps):
        self.slots = [Slot(a) for a in aps]
        self.n = 0

    def open(self):
        return not self.slots[self.n % len(self.slots)].held

    def next(self):
        slot = self.slots[self.n % len(self.slots)]
        self.n += 1
        return slot.claim()


class Stage:

    def __init__(self, nc, name, ctx):
        self.nc, self.name, self.ctx = nc, name, ctx
        self.pe = Queue(nc, nc.tensor, name + "_pe", ctx)
        self.ve = Queue(nc, nc.vector, name + "_ve", ctx)
        self.ac = Queue(nc, nc.scalar, name + "_ac", ctx)
        self.gp = Queue(nc, nc.gpsimd, name + "_gp", ctx)
        self.sp = Queue(nc, nc.sync, name + "_sp", ctx)
        self.buffers = ExitStack()

    def sb(self, name, shape, dt=F32):
        return self.buffers.enter_context(self.nc.sbuf_tensor(f"{self.name}_{name}", shape, dt))

    def ps(self, name, shape):
        return self.buffers.enter_context(self.nc.psum_tensor(f"{self.name}_{name}", shape, F32))

    def run(self):
        with self.nc.Block() as block:
            for deco, q in ((block.sync, self.sp), (block.gpsimd, self.gp), (block.scalar, self.ac),
                            (block.vector, self.ve), (block.tensor, self.pe)):
                deco(lambda _, q=q: q.replay())
        self.buffers.close()


class Loads:

    def __init__(self, stage, name, queue=None):
        self.q = queue or stage.sp
        self.sem = stage.ctx.enter_context(stage.nc.semaphore(f"{stage.name}_{name}"))
        self.count, self.closed = 0, False

    def add(self, out, in_, *after, words=False):
        assert not self.closed
        self.q.wait(*after)
        self.count += 16
        self.q.items.append(lambda: self.q.engine.dma_start(
            out, in_, allow_slow_non_contiguous=words).then_inc(self.sem, 16))

    def all(self):
        self.closed = True
        return (self.sem, self.count)


class DmaLane:

    def __init__(self, stage, name, queue):
        self.q = queue
        self.sem = stage.ctx.enter_context(stage.nc.semaphore(f"{stage.name}_{name}"))
        self.count = 0

    def start(self, out, in_, *after):
        self.q.wait(*after)
        if self.count:
            self.q.wait((self.sem, self.count))
        self.count += 16
        self.q.items.append(lambda: self.q.engine.dma_start(out, in_).then_inc(self.sem, 16))
        return (self.sem, self.count)


def staggered(make, n, live, lead):
    active, started = [], 0
    while active or started < n:
        if started < n and len(active) < live and (not active or active[-1][1] >= lead):
            active.append([make(started), 0])
            started += 1
        for entry in list(active):
            try:
                next(entry[0])
                entry[1] += 1
            except StopIteration:
                active.remove(entry)


def split_pair(q, hi, lo, src, *after):
    q.wait(*after)
    a = q.do(q.engine.tensor_copy, hi, src)
    q.wait(a)
    return q.do(q.engine.tensor_tensor, lo, src, hi.bitcast(F32), ALU.subtract)


def matmul_pairs(pe, out, w, x, start=True, stop=True, signal=True):
    combos = ((w[0], x[0]), (w[0], x[1]), (w[1], x[0]))
    mark = None
    for n, (a, b) in enumerate(combos):
        mark = pe.do(pe.engine.matmul, out, a, b, start=start and n == 0,
                                                           stop=stop and n == 2,
                     signal=signal and n == 2)
    return mark


class Norm:

    def __init__(self, st, consts, depth=2):
        self.st, self.k = st, consts
        self.stats = Ring([st.sb(f"stats{i}", [P, TILES, 6]) for i in range(depth)])
        self.mv = Ring([st.sb(f"mv{i}", [P, TILES, 2]) for i in range(depth)])
        self.rstd = Ring([st.sb(f"rstd{i}", [P, TILES]) for i in range(depth)])

    def begin(self, src, eps, *after):
        st, ve, gp = self.st, self.st.ve, self.st.gp
        stats, mv, rstd = self.stats.next(), self.mv.next(), self.rstd.next()
        ve.wait(*after, stats.free, mv.free, rstd.free)
        marks = [ve.do(ve.engine.bn_stats, stats.ap[:, t, :], src[:, t, :])
                 for t in range(TILES)]
        ve.wait(*marks)
        marks = [ve.do(ve.engine.bn_aggr, mv.ap[:, t, :], stats.ap[:, t, :])
                 for t in range(TILES)]
        stats.free = [marks[-1]]
        ve.wait(*marks)
        m = ve.do(ve.engine.tensor_scalar, rstd.ap[:, :], mv.ap[:, :, 1], eps, None, ALU.add)
        gp.wait(m)
        m = gp.do(gp.engine.tensor_tensor, rstd.ap[:, :], rstd.ap[:, :],
                                                  self.k["minus_half"][:, 0:TILES], ALU.pow)
        return mv, rstd, m

    def apply(self, q, dst, src, handle, *after):
        mv, rstd, m = handle
        q.wait(m, *after)
        for t in range(TILES):
            last = q.do(q.engine.tensor_scalar,
                dst[:, t, :], src[:, t, :], mv.ap[:, t, 0:1], rstd.ap[:, t:t + 1],
                ALU.subtract, ALU.mult)
        mv.free, rstd.free = [last], [last]
        return last


def transpose_tiles(st, bank, src, ident, cols=C, *after):
    st.pe.wait(*after, bank.free)
    for t in range(TILES):
        m = st.pe.do(st.pe.engine.transpose,
            bank.ap[0:cols, t * P:(t + 1) * P], src[:, t, 0:cols], ident[:, :],
            signal=t == TILES - 1)
    return m


def untranspose_tiles(st, bank, src, ident, rows=C, *after):
    st.pe.wait(*after, bank.free)
    for t in range(TILES):
        m = st.pe.do(st.pe.engine.transpose,
            bank.ap[:, t * P:t * P + rows], src[0:rows, t * P:(t + 1) * P], ident[0:rows, 0:rows],
            signal=t == TILES - 1)
    return m


def group(ap):
    return ap.rearrange("p (t c) -> p t c", t=TILES)


def evacuate_pair(st, pair, bank, m):
    hi, lo = pair.ap
    st.ac.wait(m, pair.free)
    a = st.ac.do(st.ac.engine.activation, hi, bank.ap, ACT.Copy)
    st.ve.wait(a)
    b = st.ve.do(st.ve.engine.tensor_tensor, lo, bank.ap, hi.bitcast(F32), ALU.subtract)
    bank.free = [b]
    return b


EXPERTS, INTER = 16, 64
CHUNKS = EXPERTS * INTER // P + 1
GROUPS4, PER_GROUP = 4, 4


def ffn0_tensors(sb):
    pair = lambda name, shape: (sb(name + "_hi", shape, F32R), sb(name + "_lo", shape, F32R))
    return {"w1": pair("w1", [P, CHUNKS, P]), "w3": pair("w3", [P, CHUNKS, P]), "w2": sb("w2", [P, CHUNKS, P]),
            "b13": sb("b13", [P, 2, CHUNKS]), "bs2": sb("bs2", [P, 1]), "b2": pair("b2", [P, P]),
            "gate": pair("gate", [P, EXPERTS]), "gate_b": sb("gate_b", [P, EXPERTS])}


def ffn0_weights(st, d, W, K, bank):
    ve, pe = st.ve, st.pe
    ld = Loads(st, "ffn0_loads")
    raw = {n: st.sb("raw_" + n, [P, CHUNKS, P]) for n in ("w1", "w3")}
    b2, gw = st.sb("raw_b2", [P, P]), st.sb("raw_gw", [EXPERTS, P])
    zero = ve.do(ve.engine.memset, b2[:, :], 0.0)
    for n, e, s in (("w1", "L0_ffn_We1", "L0_ffn_ws1"), ("w3", "L0_ffn_We3", "L0_ffn_ws3")):
        ld.add(raw[n][:, 0:8, :].rearrange("p c (e i) -> p (c e) i", e=2), d[e].rearrange("e d i -> d e i"))
        ld.add(raw[n][:, 8, :], d[s])
    ld.add(W["w2"][:, 0:8, :], d["L0_ffn_We2"].rearrange("e i d -> (e i) d").rearrange("(c p) d -> p c d", p=P))
    ld.add(W["w2"][:, 8, :], d["L0_ffn_ws2"])
    for k, (e, s) in enumerate((("L0_ffn_be1", "L0_ffn_bs1"), ("L0_ffn_be3", "L0_ffn_bs3"))):
        ld.add(W["b13"][:, k, 0:8], d[e].rearrange("e i -> (e i)").rearrange("(c p) -> p c", p=P), words=True)
        ld.add(W["b13"][:, k, 8:9], d[s].rearrange("(p a) -> p a", a=1), words=True)
    ld.add(W["bs2"][:, :], d["L0_ffn_bs2"].rearrange("(p a) -> p a", a=1), words=True)
    ld.add(W["gate_b"][:, :], row(d["L0_ffn_gate_b"]).to_broadcast([P, EXPERTS]))
    ld.add(gw[:, :], d["L0_ffn_gate_w"])
    ld.add(b2[0:EXPERTS, :], d["L0_ffn_be2"], zero)
    ld.add(b2[EXPERTS:2 * EXPERTS, :], d["L0_ffn_be2"])
    ve.wait(ld.all())
    for n in ("w1", "w3"):
        split_pair(ve, W[n][0][:, :, :], W[n][1][:, :, :], raw[n][:, :, :])
    split_pair(ve, W["b2"][0][:, :], W["b2"][1][:, :], b2[:, :])
    ve.do(ve.engine.tensor_scalar, W["bs2"][:, :], W["bs2"][:, :], 0.5, None, ALU.mult)
    pe.wait(ld.all(), K["ready"], bank.free)
    t = pe.do(pe.engine.transpose, bank.ap[:, 0:EXPERTS], gw[:, :], K["ident"][0:EXPERTS, 0:EXPERTS])
    bank.free = [split_pair(ve, W["gate"][0][:, :], W["gate"][1][:, :], bank.ap[:, 0:EXPERTS], t)]


def pick_first(st, out, scores, key, key2, best, order, n):
    ve = st.ve
    T = scores.shape[1]
    bc = lambda a: a.unsqueeze(2).to_broadcast([P, T, n])
    ve.then(ve.engine.tensor_reduce, best, scores, AX, ALU.max)
    ve.then(ve.engine.tensor_tensor, key, scores, bc(best), ALU.is_equal)
    ve.then(ve.engine.tensor_tensor, key2, key, order, ALU.mult)
    ve.then(ve.engine.tensor_reduce, best, key2, AX, ALU.max)
    return ve.then(ve.engine.tensor_tensor, out, key2, bc(best), ALU.is_equal)


def ffn0(nc, ctx, name, X, W, K, groups):
    st = Stage(nc, name, ctx)
    pe, ve, ac, gp = st.pe, st.ve, st.ac, st.gp
    ident = K["ident"]
    norm = Norm(st, K)
    xn = Ring([st.sb(f"xn{i}", [P, GROUP]) for i in range(2)])
    pairs = Ring([(st.sb(f"xh{i}", [P, GROUP], F32R)[:, :], st.sb(f"xl{i}", [P, GROUP], F32R)[:, :])
                  for i in range(2)])
    lgT = Ring([st.sb(f"lgT{i}", [EXPERTS, GROUP]) for i in range(2)])
    h1 = Ring([st.sb(f"h1_{i}", [P, GROUP]) for i in range(4)])
    h3 = Ring([st.sb(f"h3_{i}", [P, GROUP]) for i in range(3)])
    hc = Ring([st.sb(f"hc{i}", [P, GROUP]) for i in range(4)])
    yT = Ring([st.sb(f"yT{i}", [P, GROUP]) for i in range(2)])
    combT = Ring([st.sb(f"combT{i}", [P, GROUP], F32R) for i in range(2)])
    r = {k: st.sb("r_" + k, [P, TILES, n]) for k, n in
         (("logit", 16), ("e", 16), ("prob", 16), ("s", 16), ("pm", 8), ("psum", 8), ("gsum", 4),
          ("alt", 4), ("gs", 4), ("gs2", 4), ("g1", 4), ("g2", 4), ("k1", 4), ("k2", 4), ("pen", 4),
          ("ms", 16), ("ms2", 16), ("o1", 16), ("o2", 16), ("k3", 16), ("k4", 16), ("comb", 16),
          ("pair", 32))}
    col = {k: st.sb("c_" + k, [P, TILES]) for k in ("mx", "sum", "best")}
    pairb = Ring([st.sb(f"pairb{i}", [P, TILES, 32], F32R) for i in range(2)])
    misc = Ring([st.ps(f"misc{i}", [P, 512]) for i in range(1)])
    up = Ring([st.ps(f"up{i}", [P, 512]) for i in range(4)])
    cw = Ring([st.ps(f"cw{i}", [P, 512]) for i in range(2)])
    acc = Slot(st.ps("acc", [P, 512]))
    routed = Slot(None)
    zeros = [ve.do(ve.engine.memset, s.ap[:, :].bitcast(F32), 0.0) for s in combT.slots]

    def one(g):
        xg = X[:, g, :, :]
        h = norm.begin(xg, 1e-5)
        x = xn.next()
        xv = group(x.ap[:, :])
        m = norm.apply(ve, xv, xg, h, x.free)
        yield
        bank = misc.next()
        m = transpose_tiles(st, bank, xv, ident, C, m)
        x.free = [m]
        pair = pairs.next()
        bank_v = bank
        hi, lo = pair.ap
        ac.wait(m, pair.free)
        a = ac.do(ac.engine.activation, hi, bank.ap[:, :], ACT.Copy)
        ve.wait(a)
        pm = ve.do(ve.engine.tensor_tensor, lo, bank.ap[:, :], hi.bitcast(F32), ALU.subtract)
        bank.free = [pm]
        bank = misc.next()
        pe.wait(pm, bank.free)
        m = matmul_pairs(pe, bank.ap[0:EXPERTS, :], [w[:, :] for w in W["gate"]], pair.ap)
        lt = lgT.next()
        ac.wait(m, lt.free)
        m = ac.do(ac.engine.activation, lt.ap[:, :], bank.ap[0:EXPERTS, :], ACT.Copy)
        bank.free = [m]
        bank = misc.next()
        pe.wait(m, bank.free)
        for t in range(TILES):
            m = pe.do(pe.engine.transpose,
                bank.ap[:, t * EXPERTS:(t + 1) * EXPERTS], lt.ap[:, t * P:(t + 1) * P],
                ident[0:EXPERTS, 0:EXPERTS], signal=t == TILES - 1)
        lt.free = [m]
        lg = bank.ap[:, 0:TILES * EXPERTS].rearrange("p (t e) -> p t e", t=TILES)
        bc16 = lambda a: a.unsqueeze(2).to_broadcast([P, TILES, EXPERTS])
        ve.wait(m, routed.claim().free)
        ve.then(ve.engine.tensor_reduce, col["mx"][:, :], lg, AX, ALU.max)
        m = ve.then(ve.engine.tensor_tensor, r["logit"][:, :, :], lg, bc16(col["mx"][:, :]), ALU.subtract)
        bank.free = [m]
        ac.wait(m)
        m = ac.do(ac.engine.activation, r["e"][:, :, :], r["logit"][:, :, :], ACT.Exp)
        yield
        ve.wait(m)
        ve.then(ve.engine.tensor_reduce, col["sum"][:, :], r["e"][:, :, :], AX, ALU.add)
        ve.then(ve.engine.reciprocal, col["sum"][:, :], col["sum"][:, :])
        ve.then(ve.engine.tensor_tensor, r["prob"][:, :, :], r["e"][:, :, :], bc16(col["sum"][:, :]), ALU.mult)
        ve.then(ve.engine.tensor_tensor,
            r["s"][:, :, :], r["prob"][:, :, :],
            W["gate_b"][:, :].unsqueeze(1).to_broadcast([P, TILES, EXPERTS]), ALU.add)
        sv = r["s"][:, :, :].rearrange("p t (g two) -> p t g two", two=2)
        ve.then(ve.engine.tensor_tensor, r["pm"][:, :, :], sv[:, :, :, 0], sv[:, :, :, 1], ALU.max)
        ve.then(ve.engine.tensor_tensor, r["psum"][:, :, :], sv[:, :, :, 0], sv[:, :, :, 1], ALU.add)
        pv = r["pm"][:, :, :].rearrange("p t (g two) -> p t g two", two=2)
        qv = r["psum"][:, :, :].rearrange("p t (g two) -> p t g two", two=2)
        ve.then(ve.engine.tensor_tensor, r["gsum"][:, :, :], pv[:, :, :, 0], pv[:, :, :, 1], ALU.add)
        ve.then(ve.engine.tensor_tensor, r["alt"][:, :, :], qv[:, :, :, 0], qv[:, :, :, 1], ALU.max)
        ve.then(ve.engine.tensor_tensor, r["gs"][:, :, :], r["gsum"][:, :, :], r["alt"][:, :, :], ALU.max)
        order4 = K["order"][:, 0:4].unsqueeze(1).to_broadcast([P, TILES, 4])
        order16 = K["order"][:, :].unsqueeze(1).to_broadcast([P, TILES, 16])
        pick_first(st, r["g1"][:, :, :], r["gs"][:, :, :], r["k1"][:, :, :], r["k2"][:, :, :], col["best"][:, :], order4, 4)
        ve.then(ve.engine.scalar_tensor_tensor, r["gs2"][:, :, :], r["g1"][:, :, :], -BIG, r["gs"][:, :, :], ALU.mult, ALU.add)
        pick_first(st, r["g2"][:, :, :], r["gs2"][:, :, :], r["k1"][:, :, :], r["k2"][:, :, :], col["best"][:, :], order4, 4)
        ve.then(ve.engine.tensor_tensor, r["gsum"][:, :, :], r["g1"][:, :, :], r["g2"][:, :, :], ALU.add)
        ve.then(ve.engine.tensor_scalar, r["pen"][:, :, :], r["gsum"][:, :, :], BIG, -BIG, ALU.mult, ALU.add)
        ve.then(ve.engine.tensor_tensor,
            r["ms"][:, :, :].rearrange("p t (g e) -> p (t g) e", e=4),
            r["s"][:, :, :].rearrange("p t (g e) -> p (t g) e", e=4),
            r["pen"][:, :, :].rearrange("p t g -> p (t g)").unsqueeze(2).to_broadcast([P, TILES * 4, 4]), ALU.add)
        pick_first(st, r["o1"][:, :, :], r["ms"][:, :, :], r["k3"][:, :, :], r["k4"][:, :, :], col["best"][:, :], order16, 16)
        ve.then(ve.engine.scalar_tensor_tensor, r["ms2"][:, :, :], r["o1"][:, :, :], -BIG, r["ms"][:, :, :], ALU.mult, ALU.add)
        pick_first(st, r["o2"][:, :, :], r["ms2"][:, :, :], r["k3"][:, :, :], r["k4"][:, :, :], col["best"][:, :], order16, 16)
        ve.then(ve.engine.tensor_tensor, r["o1"][:, :, :], r["o1"][:, :, :], r["o2"][:, :, :], ALU.add)
        ve.then(ve.engine.tensor_tensor, r["comb"][:, :, :], r["o1"][:, :, :], r["prob"][:, :, :], ALU.mult)
        pb = pairb.next()
        ve.wait(pb.free)
        ve.then(ve.engine.tensor_copy, pb.ap[:, :, 0:16], r["comb"][:, :, :])
        m = ve.then(ve.engine.tensor_tensor, pb.ap[:, :, 16:32], r["comb"][:, :, :], pb.ap[:, :, 0:16].bitcast(F32), ALU.subtract)
        routed.free = [m]
        bank = misc.next()
        pe.wait(m, bank.free)
        for t in range(TILES):
            m = pe.do(pe.engine.transpose,
                bank.ap[0:32, t * P:(t + 1) * P], pb.ap[:, t, :].bitcast(F32), ident[:, :],
                signal=t == TILES - 1)
        pb.free = [m]
        ct = combT.next()
        ac.wait(m, ct.free, *zeros)
        cm = ac.do(ac.engine.activation, ct.ap[0:32, :], bank.ap[0:32, :], ACT.Copy)
        bank.free = [cm]
        yield
        down = []

        def down_proj():
            c, s = down.pop(0)
            pe.wait(s.ready)
            if c == 0:
                pe.wait(acc.claim().free)
            s.free = [pe.do(pe.engine.matmul, acc.ap[:, :], W["w2"][:, c, :], s.ap[:, :], start=c == 0, stop=False)]
            return s.free[0]

        for c in range(CHUNKS):
            b1, b3 = up.next(), up.next()
            pe.wait(b1.free)
            m1 = matmul_pairs(pe, b1.ap[:, :], [w[:, c, :] for w in W["w1"]], pair.ap)
            pe.wait(b3.free)
            m3 = matmul_pairs(pe, b3.ap[:, :], [w[:, c, :] for w in W["w3"]], pair.ap)
            s1, s = h1.next(), hc.next()
            last = s if c == CHUNKS - 1 else h3.next()
            ac.wait(m1, s1.free)
            a = ac.do(ac.engine.activation, s1.ap[:, :], b1.ap[:, :], ACT.Silu, bias=W["b13"][:, 0, c:c + 1])
            b1.free = [a]
            ve.wait(m3, a, last.free)
            b = ve.do(ve.engine.scalar_tensor_tensor, last.ap[:, :], b3.ap[:, :], W["b13"][:, 1, c:c + 1], s1.ap[:, :], ALU.add, ALU.mult)
            b3.free, s1.free = [b], [b]
            s.ready = b
            if c < CHUNKS - 1:
                wb = cw.next()
                pe.wait(cm, wb.free)
                m = pe.do(pe.engine.matmul, wb.ap[:, :], K["spread"][:, c, :], ct.ap[:, :], start=True, stop=True)
                ve.wait(m, b, s.free)
                s.ready = ve.do(ve.engine.tensor_tensor, s.ap[:, :], wb.ap[:, :], last.ap[:, :], ALU.mult)
                wb.free, last.free = [s.ready], [s.ready]
            down.append((c, s))
            if c >= 2:
                down_proj()
            if c % 3 == 2:
                yield
        pair.free = [m3]
        while down:
            down_proj()
        for n in range(2):
            m = pe.do(pe.engine.matmul, acc.ap[:, :], W["b2"][n][:, :], ct.ap[:, :], start=False, stop=n == 1, signal=n == 1)
        ct.free = [m]
        y = yT.next()
        ac.wait(m, y.free)
        m = ac.do(ac.engine.activation, y.ap[:, :], acc.ap[:, :], ACT.Identity, scale=0.5, bias=W["bs2"][:, :])
        acc.free = [m]
        yield
        bank = misc.next()
        m = untranspose_tiles(st, bank, y.ap, ident, C, m)
        y.free = [m]
        ve.wait(m)
        m = ve.do(ve.engine.tensor_tensor, xg, xg, group(bank.ap[:, :]), ALU.add)
        bank.free = [m]
        yield

    staggered(one, groups, 2, 4)
    st.run()


HEADS, HDIM = 16, 8
SETS = 4
BLOCK = P // SETS
MROWS = 2
PRODUCTS = 3
ROWS = MROWS + PRODUCTS * HDIM


class SlotDma:

    def __init__(self, st, name):
        self.q, self.count = st.sp, 0
        self.sem = st.ctx.enter_context(st.nc.semaphore(f"{st.name}_{name}"))

    def start(self, out, in_, *after):
        self.q.wait(*after)
        self.count += 16
        self.q.items.append(lambda: self.q.engine.dma_start(out, in_).then_inc(self.sem, 16))
        return (self.sem, self.count)


def attn0_tensors(sb):
    pair = lambda name, shape: (sb(name + "_hi", shape, F32R), sb(name + "_lo", shape, F32R))
    return {"q": pair("aq", [P, SETS, P]), "k": pair("ak", [P, SETS, P]), "v": pair("av", [P, C]),
            "proj": pair("aproj", [P, C]), "cols": sb("acols", [P, 2 * SETS + 2]),
            "bv": sb("abv", [P, C]), "pb": sb("apb", [P, C])}


def attn0_weights(st, d, A, K, bank):
    ve, pe = st.ve, st.pe
    ld = Loads(st, "attn0_loads")
    qkv, proj = st.sb("raw_qkv", [P, 3 * C]), st.sb("raw_proj", [P, C])
    qkv_b = st.sb("raw_qkv_b", [1, 3 * C])
    rep = st.sb("rep", [P, 2, HEADS, BLOCK])
    rows = st.sb("rows", [1, 2 * SETS + 2, SETS, BLOCK])
    z = [ve.do(ve.engine.memset, rep[:, :, :, :], 0.0), ve.do(ve.engine.memset, rows[:, :, :, :], 0.0)]
    ld.add(qkv[:, :], d["L0_attn_qkv_w"])
    ld.add(proj[:, :], d["L0_attn_proj_w"])
    ld.add(qkv_b[:, :], row(d["L0_attn_qkv_b"]))
    ld.add(A["bv"][:, :], row(d["L0_attn_qkv_b"])[:, 2 * C:3 * C].to_broadcast([P, C]))
    ld.add(A["pb"][:, :], row(d["L0_attn_proj_b"]).to_broadcast([P, C]))
    ve.wait(ld.all(), *z)
    for k in range(2):
        for p in range(PRODUCTS):
            lo = MROWS + p * HDIM
            m = ve.do(ve.engine.tensor_copy, rep[:, k, :, lo:lo + HDIM],
                      qkv[:, k * C:(k + 1) * C].rearrange("p (h d) -> p h d", d=HDIM))
            n = ve.do(ve.engine.tensor_copy,
                      rows[:, k * SETS:(k + 1) * SETS, :, lo:lo + HDIM].rearrange("p s j d -> p (s j) d"),
                      qkv_b[:, k * C:(k + 1) * C].rearrange("p (h d) -> p h d", d=HDIM))
    ve.do(ve.engine.memset, rows[:, SETS:2 * SETS, :, 0:MROWS], 1.0)
    ve.do(ve.engine.memset, rows[:, 2 * SETS, :, MROWS + 2 * HDIM:ROWS], 1.0)
    r = ve.do(ve.engine.memset, rows[:, 2 * SETS + 1, :, MROWS + HDIM:MROWS + 2 * HDIM], 1.0)
    for k, name in enumerate("qk"):
        v = rep[:, k, :, :].rearrange("p (s j) r -> p s (j r)", s=SETS)
        split_pair(ve, A[name][0][:, :, :], A[name][1][:, :, :], v, m)
    split_pair(ve, A["v"][0][:, :], A["v"][1][:, :], qkv[:, 2 * C:3 * C])
    split_pair(ve, A["proj"][0][:, :], A["proj"][1][:, :], proj[:, :])
    pe.wait(r, n, bank.free)
    for i in range(2 * SETS + 2):
        t = pe.do(pe.engine.matmul, bank.ap[:, i:i + 1], rows[:, i, :, :].rearrange("p j r -> p (j r)"),
                  K["ident"][0:1, 0:1], start=True, stop=True)
    ve.wait(t)
    bank.free = [ve.do(ve.engine.tensor_copy, A["cols"][:, :], bank.ap[:, 0:2 * SETS + 2])]


def attn0(nc, ctx, name, X, A, K, groups):
    st = Stage(nc, name, ctx)
    pe, ve, ac, gp = st.pe, st.ve, st.ac, st.gp
    ident = K["ident"]
    scale = float(HDIM) ** -0.5
    norm = Norm(st, K)
    xn = Ring([st.sb(f"xn{i}", [P, GROUP]) for i in range(1)])
    pairs = Ring([(st.sb(f"xh{i}", [P, GROUP], F32R)[:, :], st.sb(f"xl{i}", [P, GROUP], F32R)[:, :]) for i in range(2)])
    raw = Ring([st.sb(f"raw{i}", [P, GROUP]) for i in range(2)])
    hid = Ring([st.sb(f"hid{i}", [P, GROUP], F32R) for i in range(2)])
    qs = Ring([st.sb(f"qs{i}", [P, GROUP], F32R) for i in range(2)])
    ks = Ring([st.sb(f"ks{i}", [P, GROUP], F32R) for i in range(3)])
    qz = [Ring([st.sb(f"qz{i}_{j}", [P, GROUP], F32R) for i in range(3)]) for j in range(SETS)]
    vx = Ring([st.sb(f"vx{i}", [P, TILES, HEADS, BLOCK]) for i in range(2)])
    mx = Ring([st.sb(f"mx{i}", [P, TILES, SETS]) for i in range(2)])
    mt = Ring([st.sb(f"mt{i}", [P, TILES, SETS, BLOCK], F32R) for i in range(2)])
    mrow = Ring([st.sb(f"mrow{i}", [P, GROUP], F32R) for i in range(2)])
    pt = Ring([st.sb(f"pt{i}", [P, GROUP]) for i in range(8)])
    oT = Ring([st.sb(f"oT{i}", [P, GROUP]) for i in range(2)])
    rec = Ring([st.sb(f"rec{i}", [P, TILES, SETS]) for i in range(2)])
    otok = Ring([st.sb(f"otok{i}", [P, GROUP]) for i in range(2)])
    opair = Ring([(st.sb(f"oh{i}", [P, GROUP], F32R)[:, :], st.sb(f"ol{i}", [P, GROUP], F32R)[:, :]) for i in range(1)])
    misc = Ring([st.ps(f"misc{i}", [P, 512])[:, :] for i in range(2)])
    sbank = Ring([st.ps(f"s{i}", [P, 512])[:, :] for i in range(3)])
    tbank = Ring([st.ps(f"t{i}", [P, 512])[:, :] for i in range(2)])
    obank = Slot(st.ps("o", [P, 512])[:, :])
    for ring in qz:
        for i, s in enumerate(ring.slots):
            s.dma = SlotDma(st, f"qz{qz.index(ring)}{i}")
            s.free = [ve.do(ve.engine.memset, s.ap[:, :].bitcast(F32), 0.0)]
    for s in mt.slots:
        s.free = [ve.do(ve.engine.memset, s.ap[:, :, :, :].bitcast(F32), 0.0)]
    for s in vx.slots:
        z = ve.do(ve.engine.memset, s.ap[:, :, :, :], 0.0)
        ve.wait(z)
        s.free = [ve.do(ve.engine.memset, s.ap[:, :, :, HDIM:HDIM + 1], 1.0)]
    batches = {}

    def operand(b, k, s, ring):
        bank = misc.next()
        pe.wait(bank.free, b["pair"].ready)
        m = matmul_pairs(pe, bank.ap, [w[:, s, :] for w in A["qk"[k]]], b["pair"].ap)
        r, h, out = raw.next(), hid.next(), ring.next()
        ac.wait(m, r.free)
        c = k * SETS + s
        m = ac.do(ac.engine.activation, r.ap[:, :], bank.ap, ACT.Identity, bias=A["cols"][:, c:c + 1])
        bank.free = [m]
        a = 2 * SETS + k
        ve.wait(m, h.free)
        m = ve.do(ve.engine.tensor_scalar, h.ap[:, :], r.ap[:, :], A["cols"][:, a:a + 1], None, ALU.mult)
        gp.wait(m, out.free)
        out.ready = gp.do(gp.engine.tensor_tensor, out.ap[:, :], r.ap[:, :], h.ap[:, :].bitcast(F32), ALU.subtract)
        r.free, h.free = [out.ready], [out.ready]
        return out

    def unit(n):
        g, s = divmod(n, SETS)
        xg = X[:, g, :, :]
        if s == 0:
            b = batches[g] = {}
            h = norm.begin(xg, 1e-5)
            x = xn.next()
            xv = group(x.ap[:, :])
            m = norm.apply(ve, xv, xg, h, x.free)
            gp.wait(m)
            b["biased"] = gp.do(gp.engine.tensor_tensor, xg, xg, A["pb"][:, :].unsqueeze(1).to_broadcast([P, TILES, C]), ALU.add)
            yield
            bank = misc.next()
            m = transpose_tiles(st, bank, xv, ident, C, m)
            x.free = [m]
            b["pair"] = pairs.next()
            b["pair"].ready = evacuate_pair(st, b["pair"], bank, m)
            yield
            bank = misc.next()
            pe.wait(bank.free, b["pair"].ready)
            for t in range(TILES):
                m = matmul_pairs(pe, bank.ap[:, t * P:(t + 1) * P], [v[:, t * P:(t + 1) * P] for v in b["pair"].ap],
                                 [w[:, :] for w in A["v"]], signal=t == TILES - 1)
            b["v"] = vx.next()
            ve.wait(m, b["v"].free)
            for t in range(TILES):
                m = ve.do(ve.engine.tensor_tensor, b["v"].ap[:, t, :, 0:HDIM],
                          bank.ap[:, t * P:(t + 1) * P].rearrange("p (h d) -> p h d", d=HDIM),
                          A["bv"][:, :].rearrange("p (h d) -> p h d", d=HDIM), ALU.add)
            b["v"].ready = m
            bank.free = [m]
            b["o"] = otok.next()
            b["v"].used, b["o"].written = [], []
            yield
        b = batches[g]
        while not (ks.open() and qs.open() and all(ring.open() for ring in qz)):
            yield
        k_op = operand(b, 1, s, ks)
        yield
        q_op = operand(b, 0, s, qs)
        if s == SETS - 1:
            b["pair"].free = [q_op.ready, (pe.sem, pe.count)]
        heads = []
        for j in range(SETS):
            z = qz[j].next()
            lo = j * BLOCK
            z.ready = z.dma.start(z.ap[lo:lo + ROWS, :].bitcast(F32), q_op.ap[lo:lo + ROWS, :].bitcast(F32), q_op.ready, z.free)
            heads.append(z)
        q_op.free = [z.ready for z in heads]
        yield
        top = mx.next()
        for j in range(SETS):
            for t in range(TILES):
                bank = sbank.next()
                pe.wait(bank.free, heads[j].ready, k_op.ready)
                m = pe.do(pe.engine.matmul, bank.ap, heads[j].ap[:, t * P:(t + 1) * P], k_op.ap[:, :], start=True, stop=True)
                ve.wait(m, top.free)
                m2 = ve.do(ve.engine.tensor_reduce, top.ap[:, t, j:j + 1], bank.ap, AX, ALU.max)
                bank.free = [m2]
                yield
            heads[j].scored = m
        q = mt.next()
        ve.wait(m2, q.free)
        m = ve.do(ve.engine.tensor_scalar, q.ap[:, :, :, 0], top.ap[:, :, :], -1.0, None, ALU.mult)
        ve.wait(m)
        m = ve.do(ve.engine.scalar_tensor_tensor, q.ap[:, :, :, 1], top.ap[:, :, :], -1.0, q.ap[:, :, :, 0].bitcast(F32), ALU.mult, ALU.subtract)
        top.free = [m]
        bank = misc.next()
        pe.wait(m, bank.free)
        for t in range(TILES):
            m = pe.do(pe.engine.transpose, bank.ap[:, t * P:(t + 1) * P],
                      q.ap[:, t, :, :].rearrange("p j r -> p (j r)").bitcast(F32), ident[:, :], signal=t == TILES - 1)
        q.free = [m]
        r = mrow.next()
        ac.wait(m, r.free)
        m = ac.do(ac.engine.activation, r.ap[:, :], bank.ap, ACT.Copy)
        bank.free = [m]
        for j, z in enumerate(heads):
            lo = j * BLOCK
            z.ready = z.dma.start(z.ap[lo:lo + MROWS, :].bitcast(F32), r.ap[lo:lo + MROWS, :].bitcast(F32), m, z.scored)
        r.free = [z.ready for z in heads]
        yield
        yield
        def weigh(t, probs):
            for j, p in enumerate(probs):
                pe.wait(p.ready, b["v"].ready)
                if t == 0:
                    pe.wait(obank.claim().free if j == 0 else obank.free)
                m = pe.do(pe.engine.matmul, obank.ap[j * BLOCK:(j + 1) * BLOCK, :], b["v"].ap[:, t, s * SETS + j, :],
                          p.ap[:, :], start=t == 0, stop=t == TILES - 1, signal=j == SETS - 1)
            for p in probs:
                p.free = [m]
            return m

        late = None
        for t in range(TILES):
            probs = []
            for j in range(SETS):
                bank = tbank.next()
                pe.wait(bank.free, heads[j].ready)
                m = pe.do(pe.engine.matmul, bank.ap, k_op.ap[:, t * P:(t + 1) * P], heads[j].ap[:, :], start=True, stop=True)
                if t == TILES - 1:
                    heads[j].free = [m]
                p = pt.next()
                ac.wait(m, p.free)
                p.ready = ac.do(ac.engine.activation, p.ap[:, :], bank.ap, ACT.Exp, scale=scale)
                bank.free = [p.ready]
                probs.append(p)
                if j == 1 and late:
                    weigh(*late)
                    late = None
                yield
            late = (t, probs)
        k_op.free = [m]
        yield
        m = weigh(*late)
        b["v"].used.append(m)
        o = oT.next()
        ac.wait(m, o.free)
        m = ac.do(ac.engine.activation, o.ap[:, :], obank.ap, ACT.Copy)
        obank.free = [m]
        yield
        bank = misc.next()
        m = untranspose_tiles(st, bank, o.ap, ident, P, m)
        o.free = [m]
        v = bank.ap.rearrange("p (t j r) -> p t j r", t=TILES, j=SETS)
        rc = rec.next()
        ve.wait(m, rc.free, b["o"].free)
        m = ve.do(ve.engine.reciprocal, rc.ap[:, :, :], v[:, :, :, HDIM])
        ve.wait(m)
        for t in range(TILES):
            lo = t * P + s * SETS * HDIM
            m = ve.do(ve.engine.tensor_tensor, b["o"].ap[:, lo:lo + SETS * HDIM].rearrange("p (j d) -> p j d", d=HDIM),
                      v[:, t, :, 0:HDIM], rc.ap[:, t, :].unsqueeze(2).to_broadcast([P, SETS, HDIM]), ALU.mult)
        bank.free, rc.free = [m], [m]
        b["o"].written.append(m)
        yield
        if s == SETS - 1:
            b["v"].free = b["v"].used
            bank = misc.next()
            m = transpose_tiles(st, bank, group(b["o"].ap[:, :]), ident, C, *b["o"].written)
            b["o"].free = [m]
            pair = opair.next()
            m = evacuate_pair(st, pair, bank, m)
            yield
            bank = misc.next()
            pe.wait(m, bank.free)
            for t in range(TILES):
                m = matmul_pairs(pe, bank.ap[:, t * P:(t + 1) * P], [v[:, t * P:(t + 1) * P] for v in pair.ap],
                                 [w[:, :] for w in A["proj"]], signal=t == TILES - 1)
            pair.free = [m]
            ve.wait(m, b["biased"])
            bank.free = [ve.do(ve.engine.tensor_tensor, xg, xg, group(bank.ap), ALU.add)]
            yield

    staggered(unit, groups * SETS, 4, 18)
    st.run()


CLUSTERS, PER_CLUSTER = 8, 8
NTILES = CLUSTERS * PER_CLUSTER
SCORES = NTILES + CLUSTERS
KNOTS, GRID, COMP_H = 8, 16, 32
COMP0 = 96
COMP_ROWS = COMP0 + 2
PARAM = {"dir": 0, "w1": C, "b1": C + 2 * GRID, "w2": C + 3 * GRID, "b2": C + 4 * GRID}
PARAMS = C + 4 * GRID + 2


def ffn1_tensors(sb):
    pair = lambda name, shape: (sb(name + "_hi", shape, F32R), sb(name + "_lo", shape, F32R))
    return {"score": pair("vscore", [P, P]), "ninv": sb("vninv", [P, 1]), "knots": sb("vknots", [P, KNOTS]),
            "slope": sb("vslope", [P, KNOTS - 1]), "cb1": sb("vcb1", [P, 1]), "cw2": sb("vcw2", [P, 2]),
            "cb2": sb("vcb2", [P, 1]), "params": pair("vparams", [NTILES, PARAMS]),
            "gamma": sb("vgamma", [P, C]), "beta": sb("vbeta", [P, C]), "scale": sb("vscale", [P, 1])}


def ffn1_weights(st, d, V, K, bank):
    ve, pe = st.ve, st.pe
    ld = Loads(st, "ffn1_loads")
    D = lambda name: d["L1_ffn_" + name]
    sig, w, par = st.sb("raw_sig", [NTILES, C]), st.sb("raw_score", [P, P]), st.sb("raw_par", [NTILES, PARAMS])
    t = {n: st.sb("sig_" + n, [P, NTILES]) for n in ("raw", "pos", "neg")}
    cl = {n: st.sb("cl_" + n, [P, CLUSTERS]) for n in ("sum", "pos", "neg")}
    z = [ve.do(ve.engine.memset, w[:, :], 0.0), ve.do(ve.engine.memset, par[:, :], 0.0)]
    ld.add(sig[:, :], D("signatures_raw"), *z)
    ld.add(w[:, COMP0:P], D("compress_w1"))
    ld.add(V["ninv"][:, :], row(D("temperature")).to_broadcast([P, 1]))
    ld.add(V["knots"][:, :], row(D("knot_values")).to_broadcast([P, KNOTS]))
    ld.add(V["scale"][:, :], row(D("output_scale")).to_broadcast([P, 1]))
    ld.add(V["gamma"][:, :], row(D("norm_gamma")).to_broadcast([P, C]))
    ld.add(V["beta"][:, :], row(D("norm_beta")).to_broadcast([P, C]))
    ld.add(V["cb1"][COMP0:P, :], D("compress_b1").rearrange("(p a) -> p a", a=1), words=True)
    ld.add(V["cw2"][COMP0:P, :], D("compress_w2"))
    ld.add(V["cb2"][COMP0:COMP_ROWS, :], D("compress_b2").rearrange("(p a) -> p a", a=1), words=True)
    at = lambda name, n: par[:, PARAM[name]:PARAM[name] + n]
    ld.add(at("dir", C), D("directions"))
    ld.add(at("w1", 2 * GRID), D("spline_w1").rearrange("n i g -> n (i g)"))
    ld.add(at("b1", GRID), D("spline_b1"))
    ld.add(at("w2", GRID), D("spline_w2").rearrange("n g o -> n (g o)"))
    ld.add(at("b2", 1), D("spline_b2"), words=True)
    pe.wait(ld.all(), bank.free)
    m = pe.do(pe.engine.transpose, bank.ap[:, 0:NTILES], sig[:, :], K["ident"][0:NTILES, 0:NTILES])
    ve.wait(m, ld.all())
    ve.do(ve.engine.tensor_copy, t["raw"][:, :], bank.ap[:, 0:NTILES])
    ve.do(ve.engine.tensor_scalar, t["pos"][:, :], bank.ap[:, 0:NTILES], 0.3, None, ALU.is_gt)
    bank.free = [ve.do(ve.engine.tensor_scalar, t["neg"][:, :], bank.ap[:, 0:NTILES], -0.3, None, ALU.is_lt)]
    ve.then(ve.engine.tensor_tensor, t["pos"][:, :], t["pos"][:, :], t["neg"][:, :], ALU.subtract)
    ve.then(ve.engine.tensor_tensor, t["pos"][:, :], t["pos"][:, :], t["raw"][:, :], ALU.subtract)
    ve.then(ve.engine.tensor_tensor, w[:, 0:NTILES], t["pos"][:, :], t["raw"][:, :], ALU.add)
    v = w[:, 0:NTILES].rearrange("p (c l) -> p c l", l=PER_CLUSTER)
    ve.then(ve.engine.tensor_copy, cl["sum"][:, :], v[:, :, 0])
    for k in range(1, PER_CLUSTER):
        ve.then(ve.engine.tensor_tensor, cl["sum"][:, :], cl["sum"][:, :], v[:, :, k], ALU.add)
    ve.then(ve.engine.tensor_scalar, cl["pos"][:, :], cl["sum"][:, :], 0.0, None, ALU.is_gt)
    ve.then(ve.engine.tensor_scalar, cl["neg"][:, :], cl["sum"][:, :], 0.0, None, ALU.is_lt)
    m = ve.then(ve.engine.tensor_tensor, w[:, NTILES:SCORES], cl["pos"][:, :], cl["neg"][:, :], ALU.subtract)
    split_pair(ve, V["score"][0][:, :], V["score"][1][:, :], w[:, :], m)
    split_pair(ve, V["params"][0][:, :], V["params"][1][:, :], par[:, :])
    ve.then(ve.engine.tensor_scalar, V["ninv"][:, :], V["ninv"][:, :], 1e-6, None, ALU.add)
    ve.then(ve.engine.reciprocal, V["ninv"][:, :], V["ninv"][:, :])
    ve.then(ve.engine.tensor_scalar, V["ninv"][:, :], V["ninv"][:, :], -1.0, None, ALU.mult)
    ve.then(ve.engine.tensor_tensor, V["slope"][:, :], V["knots"][:, 1:KNOTS], V["knots"][:, 0:KNOTS - 1], ALU.subtract)
    for name in ("gamma", "beta"):
        ve.then(ve.engine.tensor_scalar, V[name][:, :], V[name][:, :], 0.5, None, ALU.mult)


def ffn1(nc, ctx, name, X, V, K, groups):
    st = Stage(nc, name, ctx)
    pe, ve, ac, gp = st.pe, st.ve, st.ac, st.gp
    ident = K["ident"]
    norm, norm_y = Norm(st, K, 3), None
    xn = Ring([st.sb(f"xn{i}", [P, GROUP]) for i in range(3)])
    pairs = Ring([(st.sb(f"xh{i}", [P, GROUP], F32R)[:, :], st.sb(f"xl{i}", [P, GROUP], F32R)[:, :]) for i in range(2)])
    arg = Ring([st.sb(f"arg{i}", [P, GROUP]) for i in range(2)])
    hT = Ring([st.sb(f"hT{i}", [P, GROUP]) for i in range(2)])
    sT = Ring([st.sb(f"sT{i}", [P, GROUP]) for i in range(2)])
    ohT = Ring([st.sb(f"ohT{i}", [NTILES, GROUP], F32R) for i in range(2)])
    yb = Ring([st.sb(f"y{i}", [P, GROUP]) for i in range(2)])
    W = {k: Ring([st.sb(f"{k}{i}", [P, TILES, n]) for i in range(2)]) for k, n in
         (("u", SCORES), ("clip", SCORES), ("clip2", SCORES), ("piece", SCORES), ("piece2", SCORES), ("gate", SCORES), ("masked", NTILES), ("comp", 2), ("sel", 8), ("oc", 8),
          ("ol", 8), ("k1", 8), ("k2", 8), ("oh", NTILES), ("ha", GRID), ("hb", GRID))}
    cols = {k: Ring([st.sb(f"{k}{i}", [P, TILES]) for i in range(2)]) for k in ("best", "mag")}
    misc = Ring([st.ps(f"misc{i}", [P, 512])[:, :] for i in range(2)])
    sbank = Ring([st.ps(f"s{i}", [P, 512])[:, :] for i in range(2)])
    pbank = Ring([st.ps(f"p{i}", [P, 1024]) for i in range(2)])
    for s in sT.slots:
        s.free = [ve.do(ve.engine.memset, s.ap[:, :], 0.0)]

    def one(g):
        xg = X[:, g, :, :]
        h = norm.begin(xg, 1e-5)
        x = xn.next()
        xv = group(x.ap[:, :])
        m = norm.apply(ve, xv, xg, h, x.free)
        x.ready = m
        gp.wait(m)
        shifted = gp.do(gp.engine.tensor_tensor, xg, xg, V["beta"][:, :].unsqueeze(1).to_broadcast([P, TILES, C]), ALU.add)
        yield
        bank = misc.next()
        m = transpose_tiles(st, bank, xv, ident, C, m)
        pair = pairs.next()
        m = evacuate_pair(st, pair, bank, m)
        yield
        bank = sbank.next()
        pe.wait(bank.free)
        pe.wait(m)
        m = matmul_pairs(pe, bank.ap, [w[:, :] for w in V["score"]], pair.ap)
        pair.free = [m]
        ht, a, s = hT.next(), arg.next(), sT.next()
        ac.wait(m, ht.free)
        m2 = ac.do(ac.engine.activation, ht.ap[COMP0:P, :], bank.ap[COMP0:P, :], ACT.Gelu, bias=V["cb1"][COMP0:P, :])
        ve.wait(m, a.free)
        m1 = ve.do(ve.engine.tensor_scalar, a.ap[0:SCORES, :], bank.ap[0:SCORES, :], V["ninv"][0:SCORES, :], 80.0, ALU.mult, ALU.min)
        bank.free = [m1, m2]
        bank = misc.next()
        pe.wait(m2, bank.free)
        m = pe.do(pe.engine.matmul, bank.ap[COMP0:COMP_ROWS, :], V["cw2"][COMP0:P, :], ht.ap[COMP0:P, :], start=True, stop=True)
        ht.free = [m]
        yield
        ac.wait(m1, s.free)
        m1 = ac.do(ac.engine.activation, s.ap[0:SCORES, :], a.ap[0:SCORES, :], ACT.Exp)
        a.free = [m1]
        ac.wait(m)
        m = ac.do(ac.engine.activation, s.ap[COMP0:COMP_ROWS, :], bank.ap[COMP0:COMP_ROWS, :], ACT.Tanh, bias=V["cb2"][COMP0:COMP_ROWS, :])
        bank.free = [m]
        bank = misc.next()
        m = untranspose_tiles(st, bank, s.ap, ident, COMP_ROWS, m1, m)
        s.free = [m]
        B = {k: ring.next() for k, ring in W.items()}
        Cc = {k: ring.next() for k, ring in cols.items()}
        R = {k: s_.ap[:, :, :] for k, s_ in B.items()}
        col = {k: s_.ap[:, :] for k, s_ in Cc.items()}
        ve.wait(m, *[s_.free for s_ in B.values()], *[s_.free for s_ in Cc.values()])
        v = group(bank.ap)
        ve.do(ve.engine.tensor_copy, R["comp"], v[:, :, COMP0:COMP_ROWS])
        m = ve.do(ve.engine.tensor_scalar, R["u"], v[:, :, 0:SCORES], 1.0, None, ALU.add)
        bank.free = [m]
        ve.then(ve.engine.reciprocal, R["u"], R["u"])
        ve.then(ve.engine.tensor_scalar, R["u"], R["u"], float(KNOTS - 1), None, ALU.mult)
        flat = lambda v: v.rearrange("p t n -> p (t n)")
        knot = lambda j: V["knots"][:, j:j + 1].to_broadcast([P, TILES * SCORES])
        for j in range(KNOTS - 1):
            t, piece = ("clip", "piece") if j % 2 else ("clip2", "piece2")
            if j == 0:
                piece = "gate"
            ve.then(ve.engine.tensor_scalar, R[t], R["u"], float(j), 0.0, ALU.subtract, ALU.max)
            ve.then(ve.engine.scalar_tensor_tensor, flat(R[piece]), flat(R[t]), V["slope"][:, j:j + 1], knot(j), ALU.mult, ALU.add)
            if j:
                ve.then(ve.engine.copy_predicated, flat(R["gate"]), flat(R[t]).bitcast(mybir.dt.uint32), flat(R[piece]))
        yield
        order = K["order"][:, 0:8].unsqueeze(1).to_broadcast([P, TILES, 8])
        pick_first(st, R["oc"], R["gate"][:, :, NTILES:SCORES], R["k1"], R["k2"], col["best"], order, 8)
        for t in range(TILES):
            ve.then(ve.engine.tensor_tensor, R["masked"][:, t, :].rearrange("p (c l) -> p c l", l=8),
                    R["gate"][:, t, 0:NTILES].rearrange("p (c l) -> p c l", l=8),
                    R["oc"][:, t, :].unsqueeze(2).to_broadcast([P, 8, 8]), ALU.mult)
        ve.then(ve.engine.tensor_reduce, R["sel"], R["masked"].rearrange("p t (c l) -> p t l c", l=8), AX, ALU.add)
        pick_first(st, R["ol"], R["sel"], R["k1"], R["k2"], col["best"], order, 8)
        for t in range(TILES):
            m = ve.then(ve.engine.tensor_tensor, R["oh"][:, t, :].rearrange("p (c l) -> p c l", l=8),
                        R["oc"][:, t, :].unsqueeze(2).to_broadcast([P, 8, 8]),
                        R["ol"][:, t, :].unsqueeze(1).to_broadcast([P, 8, 8]), ALU.mult)
        yield
        bank = misc.next()
        m = transpose_tiles(st, bank, R["oh"], ident, NTILES, m)
        o = ohT.next()
        ac.wait(m, o.free)
        m = ac.do(ac.engine.activation, o.ap[:, :], bank.ap[0:NTILES, :], ACT.Copy)
        bank.free = [m]
        yield
        pb = pbank.next()
        pe.wait(m, pb.free)
        par = pb.ap[:, :].rearrange("p (b n) -> p b n", b=2)
        for t in range(TILES):
            dst = par[:, t // 2, (t % 2) * PARAMS:(t % 2 + 1) * PARAMS]
            for k in range(2):
                m = pe.do(pe.engine.matmul, dst, o.ap[:, t * P:(t + 1) * P], V["params"][k][:, :], start=k == 0, stop=k == 1,
                          signal=k == 1)
        o.free = [m]
        par = par[:, :, 0:2 * PARAMS].rearrange("p b (t n) -> p b t n", t=2)
        at = lambda name, n, off=0: par[:, :, :, PARAM[name] + off:PARAM[name] + off + n]
        four = lambda a: a.rearrange("p (b t) g -> p b t g", b=2)
        coord = lambda i: four(R["comp"][:, :, i:i + 1].to_broadcast([P, TILES, GRID]))
        ve.wait(m)
        ve.then(ve.engine.tensor_tensor, four(R["ha"]), at("w1", GRID), coord(0), ALU.mult)
        ve.then(ve.engine.tensor_tensor, four(R["hb"]), at("w1", GRID, GRID), coord(1), ALU.mult)
        ve.then(ve.engine.tensor_tensor, R["ha"], R["ha"], R["hb"], ALU.add)
        ve.then(ve.engine.tensor_tensor, four(R["ha"]), at("b1", GRID), four(R["ha"]), ALU.add)
        ve.then(ve.engine.tensor_scalar, R["ha"], R["ha"], 0.0, None, ALU.max)
        ve.then(ve.engine.tensor_tensor, four(R["hb"]), at("w2", GRID), four(R["ha"]), ALU.mult)
        ve.then(ve.engine.tensor_reduce, col["mag"], R["hb"], AX, ALU.add)
        two = col["mag"].rearrange("p (b t) -> p b t", b=2)
        ve.then(ve.engine.tensor_tensor, two, par[:, :, :, PARAM["b2"]], two, ALU.add)
        m = ve.then(ve.engine.tensor_scalar, col["mag"], col["mag"], V["scale"][:, 0:1], None, ALU.mult)
        y = yb.next()
        yv = group(y.ap[:, :])
        ve.wait(y.free, m)
        for t in range(TILES):
            m = ve.do(ve.engine.scalar_tensor_tensor, yv[:, t, :], par[:, t // 2, t % 2, 0:C], col["mag"][:, t:t + 1], xv[:, t, :], ALU.mult, ALU.add)
        for s_ in list(B.values()) + list(Cc.values()) + [pb, x]:
            s_.free = [m]
        yield
        h = norm.begin(yv, 1e-5, m)
        yield
        m = norm.apply(ve, yv, yv, h)
        gp.wait(m)
        m = gp.do(gp.engine.tensor_tensor, yv, yv, V["gamma"][:, :].unsqueeze(1).to_broadcast([P, TILES, C]), ALU.mult)
        ve.wait(m, shifted)
        y.free = [ve.do(ve.engine.tensor_tensor, xg, xg, yv, ALU.add)]
        yield

    staggered(one, groups, 2, 4)
    st.run()


def setup1(nc, ctx, keep, d, K, stages):
    V = ffn1_tensors(keep)
    T, scratch = None, None
    if stages >= 5:
        T = attn1_tensors(keep)
        scratch = nc.dram_tensor("context", [16, P, 16 * 64], F32, kind="Internal").ap()
    st = Stage(nc, "setup1", ctx)
    bank = Slot(st.ps("bank", [P, 512])[:, :])
    ffn1_weights(st, d, V, K, bank)
    if stages >= 5:
        attn1_weights(st, d, T, K, bank)
    st.run()
    return V, T, scratch


H1, DH, M1, DFF = 16, 64, 64, 512
WIDE = H1 * DH
PAIRS = WIDE // P
DN = float(DH) ** -0.25
EPS_KERNEL = 1e-6


def attn1_tensors(sb):
    pair = lambda name, shape: (sb(name + "_hi", shape, F32R), sb(name + "_lo", shape, F32R))
    T = {"wq": pair("twq", [P, WIDE]), "wk": pair("twk", [P, WIDE]), "gq": pair("tgq", [P, WIDE]),
         "gk": pair("tgk", [P, WIDE]), "vo": sb("tvo", [P, H1, C]), "w1": pair("tw1", [P, DFF]),
         "b1": sb("tb1", [P, DFF // P]), "w2": sb("tw2", [P, DFF // P, C]), "b2": sb("tb2", [P, 1]),
         "ones": sb("tones", [P, P]), "block": sb("tblock", [P, P]),
         "xsum": sb("txsum", [P, 16]), "ksum": sb("tksum", [P, 16, PAIRS]), "nmax": sb("tnmax", [P, 16])}
    for n in ("ln1_g", "ln1_b", "ln2_g", "ln2_b"):
        T[n] = sb("t" + n, [P, C])
    return T


def attn1_weights(st, d, T, K, bank):
    ve, pe, gp = st.ve, st.pe, st.gp
    ld = Loads(st, "attn1_loads")
    D = lambda name: d["L1_attn_" + name]
    raw = {n: st.sb("raw_" + n, [P, WIDE]) for n in ("Wq", "Wk", "Wv")}
    wo, w1, pb, pT = st.sb("raw_wo", [P, PAIRS, C]), st.sb("raw_w1", [P, DFF]), st.sb("raw_proj", [P, P]), st.sb("projT", [P, P])
    turned = st.sb("turned", [P, PAIRS, P])
    z = ve.do(ve.engine.memset, pb[:, :], 0.0)
    for n in raw:
        ld.add(raw[n][:, :], D(n).rearrange("d h k -> d (h k)"), z)
    ld.add(wo[:, :, :], D("Wo").rearrange("h d o -> (h d) o").rearrange("(c p) o -> p c o", p=P))
    ld.add(w1[:, :], D("W1"))
    ld.add(T["w2"][:, :, :], D("W2").rearrange("(c p) o -> p c o", p=P))
    ld.add(T["b1"][:, :], D("b1").rearrange("(c p) -> p c", p=P), words=True)
    ld.add(T["b2"][:, :], D("b2").rearrange("(p a) -> p a", a=1), words=True)
    for n in ("ln1_g", "ln1_b", "ln2_g", "ln2_b"):
        ld.add(T[n][:, :], row(D(n)).to_broadcast([P, C]))
    for e in range(2):
        ld.add(pb[e * M1:(e + 1) * M1, e * DH:(e + 1) * DH], D("proj"))
    ve.do(ve.engine.memset, T["ones"][:, :], 1.0)
    a = ve.do(ve.engine.memset, T["block"][:, :], 0.0)
    ve.wait(a)
    for e in range(2):
        ve.do(ve.engine.memset, T["block"][e * M1:(e + 1) * M1, e * M1:(e + 1) * M1], 1.0)
    ve.wait(ld.all())
    for n, w in (("wq", "Wq"), ("wk", "Wk")):
        split_pair(ve, T[n][0][:, :], T[n][1][:, :], raw[w][:, :])
    split_pair(ve, T["w1"][0][:, :], T["w1"][1][:, :], w1[:, :])
    pe.wait(ld.all(), bank.free)
    m = pe.do(pe.engine.transpose, bank.ap[:, 0:P], pb[:, :], K["ident"][:, :])
    ve.wait(m)
    m = ve.do(ve.engine.tensor_scalar, pT[:, :], bank.ap[:, 0:P], DN, None, ALU.mult)
    pe.wait(m)

    def turn(w):
        for c in range(PAIRS):
            m = pe.do(pe.engine.transpose, bank.ap[:, 0:P], raw[w][:, c * P:(c + 1) * P], K["ident"][:, :])
            ve.wait(m)
            m = ve.do(ve.engine.tensor_copy, turned[:, c, :], bank.ap[:, 0:P])
            pe.wait(m)

    for g, w in (("gq", "Wq"), ("gk", "Wk")):
        turn(w)
        for c in range(PAIRS):
            m = pe.do(pe.engine.matmul, bank.ap[:, 0:P], turned[:, c, :], pT[:, :], start=True, stop=True)
            cut = slice(c * P, (c + 1) * P)
            m = split_pair(ve, T[g][0][:, cut], T[g][1][:, cut], bank.ap[:, 0:P], m)
            pe.wait(m)
    turn("Wv")
    for h in range(H1):
        e = h % 2 * DH
        m = pe.do(pe.engine.matmul, bank.ap[:, 0:C], turned[e:e + DH, h // 2, :], wo[e:e + DH, h // 2, :], start=True, stop=True)
        ve.wait(m)
        m = ve.do(ve.engine.tensor_copy, T["vo"][:, h, :], bank.ap[:, 0:C])
        pe.wait(m)
    bank.free = [m]


def heads_of(ap):
    return ap.rearrange("p (h m) -> p h m", m=M1)


def project_wide(pe, wide, pair, t, w):
    for half in range(2):
        cut = slice(half * 512, (half + 1) * 512)
        m = matmul_pairs(pe, wide.ap[:, cut], [v[:, t * P:(t + 1) * P] for v in pair.ap], [v[:, cut] for v in w], signal=half == 1)
    return m


def attn1_keys(nc, ctx, name, X, T, K, groups, scratch):
    st = Stage(nc, name, ctx)
    pe, ve, ac, gp = st.pe, st.ve, st.ac, st.gp
    ident = K["ident"]
    norm = Norm(st, K)
    xn = Ring([st.sb(f"xn{i}", [P, GROUP]) for i in range(2)])
    pairs = Ring([(st.sb(f"xh{i}", [P, GROUP], F32R)[:, :], st.sb(f"xl{i}", [P, GROUP], F32R)[:, :]) for i in range(2)])
    sq = Ring([st.sb(f"sq{i}", [P, WIDE]) for i in range(2)])
    feats = Ring([st.sb(f"feat{i}", [P, TILES, WIDE]) for i in range(2)])
    esum = Ring([st.sb(f"esum{i}", [P, WIDE]) for i in range(2)])
    out = Ring([st.sb(f"ctx{i}", [P, WIDE]) for i in range(2)])
    diag = Ring([st.sb(f"diag{i}", [P, H1]) for i in range(2)])
    top = Ring([st.sb(f"top{i}", [P, TILES + 2]) for i in range(2)])
    misc = Ring([st.ps(f"misc{i}", [P, 512])[:, :] for i in range(2)])
    wide = Ring([st.ps(f"wide{i}", [P, 1024])[:, :] for i in range(3)])
    dmas = [SlotDma(st, f"out{i}") for i in range(2)]

    def one(g):
        xg = X[:, g, :, :]
        h = norm.begin(xg, 1e-5)
        x = xn.next()
        xv = group(x.ap[:, :])
        m = norm.apply(ve, xv, xg, h, x.free)
        yield
        bank = misc.next()
        m = transpose_tiles(st, bank, xv, ident, C, m)
        pair = pairs.next()
        ready = evacuate_pair(st, pair, bank, m)
        bank.free = [ve.do(ve.engine.tensor_reduce, T["xsum"][:, g:g + 1], bank.ap, AX, ALU.add)]
        yield
        f = feats.next()
        tp = top.next()
        ve.wait(f.free, tp.free)
        for t in range(TILES):
            kb, db = wide.next(), wide.next()
            pe.wait(ready, kb.free)
            m = project_wide(pe, kb, pair, t, T["wk"])
            pe.wait(db.free)
            m2 = project_wide(pe, db, pair, t, T["gk"])
            s = sq.next()
            ac.wait(m, s.free)
            m = ac.do(ac.engine.activation, s.ap[:, :], kb.ap, ACT.Square, scale=0.25)
            kb.free = [m]
            dg = diag.next()
            ve.wait(m2)
            top_t = ve.do(ve.engine.tensor_reduce, tp.ap[:, t:t + 1], db.ap, AX, ALU.max)
            ve.wait(m, dg.free)
            m = ve.do(ve.engine.tensor_reduce, dg.ap[:, :], heads_of(s.ap[:, :]), AX, ALU.add)
            s.free = [m]
            ve.wait(m)
            m = ve.do(ve.engine.tensor_tensor, heads_of(f.ap[:, t, :]), heads_of(db.ap), dg.ap[:, :].unsqueeze(2).to_broadcast([P, H1, M1]), ALU.subtract)
            db.free, dg.free = [m], [m]
            yield
        pair.free = [m2]
        ve.wait(top_t)
        m = ve.do(ve.engine.tensor_reduce, tp.ap[:, TILES:TILES + 1], tp.ap[:, 0:TILES], AX, ALU.max)
        bank = misc.next()
        pe.wait(m, bank.free)
        m = pe.do(pe.engine.transpose, bank.ap[0:1, 0:P], tp.ap[:, TILES:TILES + 1], ident[:, :])
        ve.wait(m)
        one_ = tp.ap[0:1, TILES + 1:TILES + 2]
        m = ve.do(ve.engine.tensor_reduce, one_, bank.ap[0:1, 0:P], AX, ALU.max)
        pe.wait(m)
        m = pe.do(pe.engine.matmul, bank.ap[:, P:P + 1], T["ones"][0:1, :], one_, start=True, stop=True)
        ve.wait(m)
        m = ve.do(ve.engine.tensor_scalar, T["nmax"][:, g:g + 1], bank.ap[:, P:P + 1], -1.0, None, ALU.mult)
        bank.free, tp.free = [m], [m]
        ac.wait(m)
        exps = []
        for t in range(TILES):
            exps.append(ac.do(ac.engine.activation, f.ap[:, t, :], f.ap[:, t, :], ACT.Exp, bias=T["nmax"][:, g:g + 1]))
        yield
        es = esum.next()
        gp.wait(exps[1], es.free)
        m = gp.do(gp.engine.tensor_tensor, es.ap[:, :], f.ap[:, 0, :], f.ap[:, 1, :], ALU.add)
        for t in range(2, TILES):
            gp.wait(exps[t], m)
            m = gp.do(gp.engine.tensor_tensor, es.ap[:, :], es.ap[:, :], f.ap[:, t, :], ALU.add)
        summed = m
        w = wide.next()
        pe.wait(w.free)
        for t in range(TILES):
            pe.wait(exps[t])
            for half in range(2):
                cut = slice(half * 512, (half + 1) * 512)
                m = pe.do(pe.engine.matmul, w.ap[:, cut], xv[:, t, :], f.ap[:, t, cut], start=t == 0, stop=t == TILES - 1)
        x.free, f.free = [m], [m, summed]
        o = out.next()
        dma = dmas[g % 2]
        ac.wait(m, o.free)
        m = ac.do(ac.engine.activation, o.ap[:, :], w.ap, ACT.Copy)
        w.free = [m]
        o.free = [dma.start(scratch[g], o.ap[:, :], m)]
        yield
        bank = misc.next()
        pe.wait(summed, bank.free)
        for c in range(PAIRS):
            m = pe.do(pe.engine.matmul, bank.ap[:, c:c + 1], es.ap[:, c * P:(c + 1) * P], T["ones"][:, 0:1], start=True, stop=True, signal=c == PAIRS - 1)
        es.free = [m]
        ve.wait(m)
        bank.free = [ve.do(ve.engine.tensor_copy, T["ksum"][:, g, :], bank.ap[:, 0:PAIRS])]
        yield

    staggered(one, groups, 2, 5)
    for dma in dmas:
        if dma.count:
            st.sp.wait((dma.sem, dma.count))
    st.run()


def attn1_queries(nc, ctx, name, X, T, K, groups, scratch):
    st = Stage(nc, name, ctx)
    pe, ve, ac, gp = st.pe, st.ve, st.ac, st.gp
    ident = K["ident"]
    norm = Norm(st, K, 3)
    xn = Ring([st.sb(f"xn{i}", [P, GROUP]) for i in range(2)])
    pairs = Ring([(st.sb(f"xh{i}", [P, GROUP], F32R)[:, :], st.sb(f"xl{i}", [P, GROUP], F32R)[:, :]) for i in range(2)])
    pairs2 = Ring([(st.sb(f"yh{i}", [P, GROUP], F32R)[:, :], st.sb(f"yl{i}", [P, GROUP], F32R)[:, :]) for i in range(2)])
    sq = Ring([st.sb(f"sq{i}", [P, WIDE]) for i in range(2)])
    cin = Ring([st.sb(f"cin{i}", [P, WIDE]) for i in range(2)])
    mem = Ring([st.sb(f"mem{i}", [P, PAIRS, C]) for i in range(2)])
    den = Ring([st.sb(f"den{i}", [P, PAIRS, P]) for i in range(2)])
    qf = Ring([st.sb(f"qf{i}", [P, GROUP]) for i in range(3)])
    rc = Ring([st.sb(f"rc{i}", [P, GROUP]) for i in range(2)])
    qn = Ring([st.sb(f"qn{i}", [P, GROUP]) for i in range(3)])
    yT = Ring([st.sb(f"yT{i}", [P, GROUP]) for i in range(2)])
    y1 = Ring([st.sb(f"y1_{i}", [P, GROUP]) for i in range(2)])
    y2 = Ring([st.sb(f"y2_{i}", [P, GROUP]) for i in range(2)])
    neg = Ring([st.sb(f"neg{i}", [P, GROUP]) for i in range(2)])
    pos = Ring([st.sb(f"pos{i}", [P, GROUP]) for i in range(2)])
    hid = Ring([st.sb(f"hid{i}", [P, GROUP]) for i in range(2)])
    bT = Ring([st.sb(f"bT{i}", [P, GROUP], F32R) for i in range(2)])
    top = Ring([st.sb(f"top{i}", [P, TILES, H1]) for i in range(2)])
    dg = Ring([st.sb(f"dg{i}", [P, TILES, H1]) for i in range(2)])
    bp = Ring([st.sb(f"bp{i}", [P, TILES, 2 * H1], F32R) for i in range(2)])
    shift, xeps, ksum, nm = st.sb("shift", [P, 16]), st.sb("xeps", [P, 16]), st.sb("ksum", [P, 16, PAIRS]), st.sb("nm", [P, 1])
    misc = Ring([st.ps("misc0", [P, 512])[:, :]])
    wide = Ring([st.ps(f"wide{i}", [P, 1024])[:, :] for i in range(2)])
    half = Ring([st.ps(f"half{i}", [P, 512])[:, :] for i in range(2)])
    acc = Slot(st.ps("acc", [P, 512])[:, :])
    dmas = [SlotDma(st, f"in{i}") for i in range(2)]
    for s in bT.slots:
        s.free = [ve.do(ve.engine.memset, s.ap[:, :].bitcast(F32), 0.0)]
    m = ve.do(ve.engine.tensor_reduce, nm[:, :], T["nmax"][:, 0:groups], AX, ALU.min)
    ac.wait(m)
    shifted = ac.do(ac.engine.activation, shift[:, 0:groups], T["nmax"][:, 0:groups], ACT.Exp, scale=-1.0, bias=nm[:, :])
    ve.do(ve.engine.tensor_scalar, xeps[:, 0:groups], T["xsum"][:, 0:groups], EPS_KERNEL, None, ALU.mult)
    ve.wait(shifted)
    m = ve.do(ve.engine.tensor_tensor, ksum[:, 0:groups, :], T["ksum"][:, 0:groups, :], shift[:, 0:groups].unsqueeze(2).to_broadcast([P, groups, PAIRS]), ALU.mult)
    ve.wait(m)
    sums = ve.do(ve.engine.tensor_scalar, ksum[:, 0:groups, :], ksum[:, 0:groups, :], GROUP * EPS_KERNEL, None, ALU.add)

    def affine(q, v, gain, bias, *after):
        q.wait(*after)
        m = q.do(q.engine.tensor_tensor, v, v, T[gain][:, :].unsqueeze(1).to_broadcast([P, TILES, C]), ALU.mult)
        q.wait(m)
        return q.do(q.engine.tensor_tensor, v, v, T[bias][:, :].unsqueeze(1).to_broadcast([P, TILES, C]), ALU.add)

    def one(g):
        ci = cin.next()
        loaded = dmas[g % 2].start(ci.ap[:, :], scratch[g], ci.free)
        xg = X[:, g, :, :]
        h = norm.begin(xg, 1e-5)
        x = xn.next()
        xv = group(x.ap[:, :])
        m = norm.apply(ve, xv, xg, h, x.free)
        yield
        bank = misc.next()
        m = transpose_tiles(st, bank, xv, ident, C, m)
        pair = pairs.next()
        ready = evacuate_pair(st, pair, bank, m)
        yield
        gp.wait(loaded, sums)
        m = gp.do(gp.engine.tensor_scalar, ci.ap[:, :], ci.ap[:, :], shift[:, g:g + 1], xeps[:, g:g + 1], ALU.mult, ALU.add)
        dn = den.next()
        gp.wait(dn.free)
        dn.ready = gp.do(gp.engine.tensor_tensor, dn.ap[:, :, :], T["block"][:, :].unsqueeze(1).to_broadcast([P, PAIRS, P]),
                         ksum[:, g, :].unsqueeze(2).to_broadcast([P, PAIRS, P]), ALU.mult)
        tp, d_ = top.next(), dg.next()
        ve.wait(tp.free, d_.free)
        for t in range(TILES):
            kb, db = wide.next(), wide.next()
            pe.wait(ready, kb.free)
            m1 = project_wide(pe, kb, pair, t, T["wq"])
            pe.wait(db.free)
            m2 = project_wide(pe, db, pair, t, T["gq"])
            s = sq.next()
            ac.wait(m1, s.free)
            m1 = ac.do(ac.engine.activation, s.ap[:, :], kb.ap, ACT.Square, scale=0.25)
            kb.free = [m1]
            ve.wait(m2)
            db.free = [ve.do(ve.engine.tensor_reduce, tp.ap[:, t, :], heads_of(db.ap), AX, ALU.max)]
            ve.wait(m1)
            m1 = ve.do(ve.engine.tensor_reduce, d_.ap[:, t, :], heads_of(s.ap[:, :]), AX, ALU.add)
            s.free = [m1]
            yield
        mm = mem.next()
        w = wide.next()
        pe.wait(m, w.free)
        wv = w.ap.rearrange("p (c o) -> p c o", o=C)
        for hd in range(H1):
            e = hd % 2 * M1
            m = pe.do(pe.engine.matmul, wv[e:e + M1, hd // 2, :], ci.ap[:, hd * M1:(hd + 1) * M1], T["vo"][:, hd, :], start=True, stop=True, signal=hd == H1 - 1)
        ci.free = [m]
        ac.wait(m, mm.free)
        mm.ready = ac.do(ac.engine.activation, mm.ap[:, :, :], wv, ACT.Copy)
        w.free = [mm.ready]
        b = bp.next()
        ve.wait(m1, b.free)
        m = ve.do(ve.engine.scalar_tensor_tensor, tp.ap[:, :, :], tp.ap[:, :, :], -1.0, d_.ap[:, :, :], ALU.mult, ALU.subtract)
        ve.wait(m)
        m = ve.do(ve.engine.tensor_copy, b.ap[:, :, 0:H1], tp.ap[:, :, :])
        ve.wait(m)
        m = ve.do(ve.engine.tensor_tensor, b.ap[:, :, H1:2 * H1], tp.ap[:, :, :], b.ap[:, :, 0:H1].bitcast(F32), ALU.subtract)
        tp.free, d_.free = [m], [m]
        bank = misc.next()
        pe.wait(m, bank.free)
        for t in range(TILES):
            m = pe.do(pe.engine.transpose, bank.ap[0:2 * H1, t * P:(t + 1) * P], b.ap[:, t, :].bitcast(F32), ident[:, :], signal=t == TILES - 1)
        b.free = [m]
        bt = bT.next()
        ac.wait(m, bt.free)
        m = ac.do(ac.engine.activation, bt.ap[0:2 * H1, :], bank.ap[0:2 * H1, :], ACT.Copy)
        bank.free = [m]
        biased = m
        yield
        late = []

        def divide():
            c, f = late.pop(0)
            bk = half.next()
            pe.wait(f.ready, dn.ready, bk.free)
            m = pe.do(pe.engine.matmul, bk.ap, dn.ap[:, c, :], f.ap[:, :], start=True, stop=True)
            r, n = rc.next(), qn.next()
            ve.wait(m, r.free)
            m = ve.do(ve.engine.reciprocal, r.ap[:, :], bk.ap)
            bk.free = [m]
            gp.wait(m, n.free)
            n.ready = gp.do(gp.engine.tensor_tensor, n.ap[:, :], f.ap[:, :], r.ap[:, :], ALU.mult)
            f.free, r.free = [n.ready], [n.ready]
            done.append((c, n))

        done = []

        def gather():
            c, n = done.pop(0)
            pe.wait(n.ready, mm.ready)
            if c == 0:
                pe.wait(acc.free)
            m = pe.do(pe.engine.matmul, acc.ap, mm.ap[:, c, :], n.ap[:, :], start=c == 0, stop=c == PAIRS - 1)
            n.free = [m]
            return m

        while acc.held:
            yield
        acc.claim()
        for c in range(PAIRS):
            bk = half.next()
            pe.wait(bk.free, biased)
            matmul_pairs(pe, bk.ap, [v[:, c * P:(c + 1) * P] for v in T["gq"]], pair.ap, stop=False, signal=False)
            m = pe.do(pe.engine.matmul, bk.ap, K["spread"][:, c, :], bt.ap[:, :], start=False, stop=True)
            f = qf.next()
            ac.wait(m, f.free)
            a = ac.do(ac.engine.activation, f.ap[:, :], bk.ap, ACT.Exp)
            bk.free = [a]
            ve.wait(a)
            f.ready = ve.do(ve.engine.tensor_scalar, f.ap[:, :], f.ap[:, :], EPS_KERNEL, None, ALU.add)
            late.append((c, f))
            if c >= 1:
                divide()
            if c >= 3:
                gather()
            yield
        pair.free, bt.free = [m], [m]
        divide()
        while done:
            m = gather()
        dn.free, mm.free = [m], [m]
        y = yT.next()
        ac.wait(m, y.free)
        m = ac.do(ac.engine.activation, y.ap[:, :], acc.ap, ACT.Copy)
        acc.free = [m]
        yield
        bank = misc.next()
        m = untranspose_tiles(st, bank, y.ap, ident, C, m)
        y.free = [m]
        o = y1.next()
        ov = group(o.ap[:, :])
        ve.wait(m, o.free)
        m = ve.do(ve.engine.tensor_tensor, ov, group(bank.ap), xv, ALU.add)
        bank.free, x.free = [m], [m]
        h = norm.begin(ov, 1e-6, m)
        yield
        m = norm.apply(ve, ov, ov, h)
        m = affine(gp, ov, "ln1_g", "ln1_b", m)
        yield
        bank = misc.next()
        m = transpose_tiles(st, bank, ov, ident, C, m)
        pair = pairs2.next()
        m = evacuate_pair(st, pair, bank, m)
        yield
        pe.wait(m)
        up = []

        def down():
            c, s = up.pop(0)
            pe.wait(s.ready)
            if c == 0:
                pe.wait(acc.free)
            m = pe.do(pe.engine.matmul, acc.ap, T["w2"][:, c, :], s.ap[:, :], start=c == 0, stop=c == DFF // P - 1)
            s.free = [m]
            return m

        while acc.held:
            yield
        acc.claim()
        for c in range(DFF // P):
            bk = half.next()
            pe.wait(bk.free)
            m = matmul_pairs(pe, bk.ap, [v[:, c * P:(c + 1) * P] for v in T["w1"]], pair.ap)
            last = m
            n, p, s = neg.next(), pos.next(), hid.next()
            ve.wait(m, n.free)
            m1 = ve.do(ve.engine.tensor_scalar, n.ap[:, :], bk.ap, T["b1"][:, c:c + 1], 0.0, ALU.add, ALU.min)
            ac.wait(m1, p.free)
            m = ac.do(ac.engine.activation, p.ap[:, :], bk.ap, ACT.Relu, bias=T["b1"][:, c:c + 1])
            bk.free = [m]
            m = ac.do(ac.engine.activation, n.ap[:, :], n.ap[:, :], ACT.Exp)
            ve.wait(m, s.free)
            s.ready = ve.do(ve.engine.scalar_tensor_tensor, s.ap[:, :], n.ap[:, :], -1.0, p.ap[:, :], ALU.add, ALU.add)
            n.free, p.free = [s.ready], [s.ready]
            up.append((c, s))
            if c >= 1:
                down()
            yield
        pair.free = [last]
        m = down()
        y = yT.next()
        ac.wait(m, y.free)
        m = ac.do(ac.engine.activation, y.ap[:, :], acc.ap, ACT.Identity, bias=T["b2"][:, :])
        acc.free = [m]
        yield
        bank = misc.next()
        m = untranspose_tiles(st, bank, y.ap, ident, C, m)
        y.free = [m]
        r = y2.next()
        rv = group(r.ap[:, :])
        ve.wait(m, r.free)
        m = ve.do(ve.engine.tensor_tensor, rv, group(bank.ap), ov, ALU.add)
        bank.free, o.free = [m], [m]
        h = norm.begin(rv, 1e-6, m)
        yield
        m = norm.apply(ve, rv, rv, h)
        m = affine(gp, rv, "ln2_g", "ln2_b", m)
        ve.wait(m)
        r.free = [ve.do(ve.engine.tensor_tensor, xg, xg, rv, ALU.add)]
        yield

    staggered(one, groups, 2, 12)
    st.run()


def attn1(nc, ctx, name, X, T, K, groups, scratch):
    attn1_keys(nc, ctx, name + "k", X, T, K, groups, scratch)
    attn1_queries(nc, ctx, name + "q", X, T, K, groups, scratch)


def row(vector):
    return vector.rearrange("(a n) -> a n", a=1)


def constant_tensors(sb):
    return {"ident": sb("ident", [P, P]), "order": sb("order", [P, 16]), "minus_half": sb("minus_half", [P, 16]),
            "spread": sb("spread", [P, CHUNKS - 1, P], F32R)}


def constants(st, K):
    gp, ve = st.gp, st.ve
    select = lambda ap, **kw: gp.then(gp.engine.affine_select,
        out=ap, in_=ap, compare_op=ALU.not_equal, fill=1.0, **kw)
    gp.do(gp.engine.memset, K["ident"][:, :], 0.0)
    select(K["ident"][:, :], base=0, pattern=[[-1, P]], channel_multiplier=1)
    gp.do(gp.engine.memset, K["minus_half"][:, :], -0.5)
    for j in range(16):
        last = gp.do(gp.engine.memset, K["order"][:, j:j + 1], float(16 - j))
    raw = st.sb("spread_raw", [P, CHUNKS - 1, P])
    gp.do(gp.engine.memset, raw[:, :, :], 0.0)
    view = raw[:, :, :].rearrange("p c (e i) -> p c e i", e=2)
    for half in range(2):
        last = select(view, base=-EXPERTS * half, pattern=[[-2, CHUNKS - 1], [-1, 2], [0, INTER]], channel_multiplier=1)
    ve.wait(last)
    K["ready"] = [last, ve.do(ve.engine.tensor_copy, K["spread"][:, :, :], raw[:, :, :])]


def macaron(nc, d, out, groups, stages):
    with ExitStack() as ctx:
        keep = lambda name, shape, dt=F32: ctx.enter_context(nc.sbuf_tensor(name, shape, dt))
        X = keep("X", [P, groups, TILES, C])
        K = constant_tensors(keep)
        layer0 = ExitStack()
        keep0 = lambda name, shape, dt=F32: layer0.enter_context(nc.sbuf_tensor(name, shape, dt))
        W = ffn0_tensors(keep0)
        if stages >= 2:
            A = attn0_tensors(keep0)
        st = Stage(nc, "setup", ctx)
        for g in range(0, groups, 2):
            lane = Loads(st, f"x{g}", st.ac)
            n = min(2, groups - g)
            lane.add(X[:, g:g + n, :, :].rearrange("p b t c -> p b (t c)"),
                     d["L0_attn_x"][g:g + n].rearrange("b (p t) c -> p b (t c)", p=P))
            st.ve.wait(lane.all())
        bank = Slot(st.ps("bank", [P, 512])[:, :])
        constants(st, K)
        ffn0_weights(st, d, W, K, bank)
        if stages >= 2:
            attn0_weights(st, d, A, K, bank)
        st.run()
        if stages >= 1:
            ffn0(nc, ctx, "ffnA", X, W, K, groups)
        if stages >= 2:
            attn0(nc, ctx, "att0", X, A, K, groups)
        if stages >= 3:
            ffn0(nc, ctx, "ffnB", X, W, K, groups)
        layer0.close()
        if stages >= 4:
            layer1 = ExitStack()
            keep1 = lambda name, shape, dt=F32: layer1.enter_context(nc.sbuf_tensor(name, shape, dt))
            V, T, scratch = setup1(nc, ctx, keep1, d, K, stages)
            ffn1(nc, ctx, "ffnC", X, V, K, groups)
            if stages >= 5:
                attn1(nc, ctx, "att1", X, T, K, groups, scratch)
            if stages >= 6:
                ffn1(nc, ctx, "ffnD", X, V, K, groups)
            layer1.close()
        st = Stage(nc, "store", ctx)
        lane = Loads(st, "out")
        for g in range(0, groups, 2):
            n = min(2, groups - g)
            lane.add(out[g:g + n].rearrange("b (p t) c -> p b (t c)", p=P),
                     X[:, g:g + n, :, :].rearrange("p b t c -> p b (t c)"))
        st.sp.wait(lane.all())
        st.run()


NAMES = ["L0_attn_x", "L0_attn_qkv_w", "L0_attn_qkv_b", "L0_attn_proj_w", "L0_attn_proj_b",
         "L0_ffn_gate_w", "L0_ffn_gate_b", "L0_ffn_We1", "L0_ffn_be1", "L0_ffn_We2", "L0_ffn_be2",
         "L0_ffn_We3", "L0_ffn_be3", "L0_ffn_ws1", "L0_ffn_bs1", "L0_ffn_ws2", "L0_ffn_bs2",
         "L0_ffn_ws3", "L0_ffn_bs3", "L1_attn_Wq", "L1_attn_Wk", "L1_attn_Wv", "L1_attn_Wo",
         "L1_attn_proj", "L1_attn_W1", "L1_attn_b1", "L1_attn_W2", "L1_attn_b2", "L1_attn_ln1_g",
         "L1_attn_ln1_b", "L1_attn_ln2_g", "L1_attn_ln2_b", "L1_ffn_signatures_raw",
         "L1_ffn_knot_values", "L1_ffn_temperature", "L1_ffn_compress_w1", "L1_ffn_compress_b1",
         "L1_ffn_compress_w2", "L1_ffn_compress_b2", "L1_ffn_spline_w1", "L1_ffn_spline_b1",
         "L1_ffn_spline_w2", "L1_ffn_spline_b2", "L1_ffn_directions", "L1_ffn_norm_gamma",
         "L1_ffn_norm_beta", "L1_ffn_output_scale"]


def kernel(**inputs):
    import concourse.bacc as bacc
    from concourse.bass_utils import run_bass_kernel_spmd

    nc = bacc.Bacc("TRN2", target_bir_lowering=False, num_devices=1)
    arrays, dram = {}, {}
    for name in NAMES:
        arrays[name] = np.ascontiguousarray(inputs[name])
        dram[name] = nc.dram_tensor(name, arrays[name].shape, F32, kind="ExternalInput").ap()
    shape = arrays["L0_attn_x"].shape
    out = nc.dram_tensor("out", shape, F32, kind="ExternalOutput").ap()
    macaron(nc, dram, out, 16, 6)
    result = run_bass_kernel_spmd(nc, [arrays], core_ids=[0])
    return result.results[0]["out"]
```

```python
from contextlib import ExitStack

import numpy as np

import concourse.bass as bass
from concourse import mybir

F32 = mybir.dt.float32
F32R = mybir.dt.float32r
ALU = mybir.AluOpType
ACT = mybir.ActivationFunctionType
AX = mybir.AxisListType.X

P = 128
C = 128
TILES = 4
GROUP = TILES * P
BIG = 3.0e38


class Queue:

    def __init__(self, nc, engine, name, ctx):
        self.nc, self.engine, self.name = nc, engine, name
        self.sem = ctx.enter_context(nc.semaphore(name))
        self.count = 0
        self.items = []
        self.seen = {}

    def wait(self, *marks):
        for mark in marks:
            if mark is None:
                continue
            if isinstance(mark, list):
                self.wait(*mark)
                continue
            sem, value = mark
            if self.seen.get(id(sem), 0) < value:
                self.seen[id(sem)] = value
                self.items.append(lambda s=sem, v=value: self.engine.wait_ge(s, v))
        return self

    def do(self, build, *args, signal=True, **options):
        if not signal:
            self.items.append(lambda: build(*args, **options))
            return None
        self.count += 1
        self.items.append(lambda: build(*args, **options).then_inc(self.sem, 1))
        return (self.sem, self.count)

    def then(self, build, *args, **options):
        self.wait((self.sem, self.count))
        return self.do(build, *args, **options)

    def chain(self, *after):
        return Chain(self, *after)

    def replay(self):
        for item in self.items:
            item()


class Chain:

    def __init__(self, queue, *after):
        self.queue, self.last = queue, list(after)

    def then(self, build, *args, **options):
        self.queue.wait(*self.last)
        self.last = [self.queue.do(build, *args, **options)]
        return self.last[0]


class Slot:

    def __init__(self, ap):
        self.ap = ap
        self.free = []

    @property
    def free(self):
        return self.marks

    @free.setter
    def free(self, marks):
        self.marks, self.held = marks, False

    def claim(self):
        assert not self.held, self.ap
        self.held = True
        return self


class Ring:

    def __init__(self, aps):
        self.slots = [Slot(a) for a in aps]
        self.n = 0

    def open(self):
        return not self.slots[self.n % len(self.slots)].held

    def next(self):
        slot = self.slots[self.n % len(self.slots)]
        self.n += 1
        return slot.claim()


class Stage:

    def __init__(self, nc, name, ctx):
        self.nc, self.name, self.ctx = nc, name, ctx
        self.pe = Queue(nc, nc.tensor, name + "_pe", ctx)
        self.ve = Queue(nc, nc.vector, name + "_ve", ctx)
        self.ac = Queue(nc, nc.scalar, name + "_ac", ctx)
        self.gp = Queue(nc, nc.gpsimd, name + "_gp", ctx)
        self.sp = Queue(nc, nc.sync, name + "_sp", ctx)
        self.buffers = ExitStack()

    def sb(self, name, shape, dt=F32):
        return self.buffers.enter_context(self.nc.sbuf_tensor(f"{self.name}_{name}", shape, dt))

    def ps(self, name, shape):
        return self.buffers.enter_context(self.nc.psum_tensor(f"{self.name}_{name}", shape, F32))

    def run(self):
        with self.nc.Block() as block:
            for deco, q in ((block.sync, self.sp), (block.gpsimd, self.gp), (block.scalar, self.ac),
                            (block.vector, self.ve), (block.tensor, self.pe)):
                deco(lambda _, q=q: q.replay())
        self.buffers.close()


class Loads:

    def __init__(self, stage, name, queue=None):
        self.q = queue or stage.sp
        self.sem = stage.ctx.enter_context(stage.nc.semaphore(f"{stage.name}_{name}"))
        self.count, self.closed = 0, False

    def add(self, out, in_, *after, words=False):
        assert not self.closed
        self.q.wait(*after)
        self.count += 16
        self.q.items.append(lambda: self.q.engine.dma_start(
            out, in_, allow_slow_non_contiguous=words).then_inc(self.sem, 16))

    def all(self):
        self.closed = True
        return (self.sem, self.count)


def opened(ring):
    while not ring.open():
        yield


def rest(steps):
    for _ in range(steps):
        yield


def staggered(make, n, live, lead):
    active, started, rounds = [], 0, 0
    while active or started < n:
        rounds += 1
        assert rounds < 1000 * n, "the pipelines wait for each other's buffers"
        if started < n and len(active) < live and (not active or active[-1][1] >= lead):
            active.append([make(started), 0])
            started += 1
        for entry in list(active):
            try:
                next(entry[0])
                entry[1] += 1
            except StopIteration:
                active.remove(entry)


def split_pair(q, hi, lo, src, *after):
    q.wait(*after)
    a = q.do(q.engine.tensor_copy, hi, src)
    q.wait(a)
    return q.do(q.engine.tensor_tensor, lo, src, hi.bitcast(F32), ALU.subtract)


def matmul_pairs(pe, out, w, x, start=True, stop=True, signal=True):
    combos = ((w[0], x[0]), (w[0], x[1]), (w[1], x[0]))
    mark = None
    for n, (a, b) in enumerate(combos):
        mark = pe.do(pe.engine.matmul, out, a, b, start=start and n == 0,
                                                           stop=stop and n == 2,
                     signal=signal and n == 2)
    return mark


class Norm:

    def __init__(self, st, consts, depth=2):
        self.st, self.k = st, consts
        self.stats = Ring([st.sb(f"stats{i}", [P, TILES, 6]) for i in range(depth)])
        self.mv = Ring([st.sb(f"mv{i}", [P, TILES, 2]) for i in range(depth)])
        self.rstd = Ring([st.sb(f"rstd{i}", [P, TILES]) for i in range(depth)])

    def begin(self, src, eps, *after):
        st, ve, gp = self.st, self.st.ve, self.st.gp
        stats, mv, rstd = self.stats.next(), self.mv.next(), self.rstd.next()
        ve.wait(*after, stats.free, mv.free, rstd.free)
        marks = [ve.do(ve.engine.bn_stats, stats.ap[:, t, :], src[:, t, :])
                 for t in range(TILES)]
        ve.wait(*marks)
        marks = [ve.do(ve.engine.bn_aggr, mv.ap[:, t, :], stats.ap[:, t, :])
                 for t in range(TILES)]
        stats.free = [marks[-1]]
        ve.wait(*marks)
        m = ve.do(ve.engine.tensor_scalar, rstd.ap[:, :], mv.ap[:, :, 1], eps, None, ALU.add)
        gp.wait(m)
        m = gp.do(gp.engine.tensor_tensor, rstd.ap[:, :], rstd.ap[:, :],
                                                  self.k["minus_half"][:, 0:TILES], ALU.pow)
        return mv, rstd, m

    def apply(self, q, dst, src, handle, *after):
        mv, rstd, m = handle
        q.wait(m, *after)
        for t in range(TILES):
            last = q.do(q.engine.tensor_scalar,
                dst[:, t, :], src[:, t, :], mv.ap[:, t, 0:1], rstd.ap[:, t:t + 1],
                ALU.subtract, ALU.mult)
        mv.free, rstd.free = [last], [last]
        return last


def transpose_tiles(st, bank, src, ident, cols=C, *after):
    st.pe.wait(*after, bank.free)
    for t in range(TILES):
        m = st.pe.do(st.pe.engine.transpose,
            bank.ap[0:cols, t * P:(t + 1) * P], src[:, t, 0:cols], ident[:, :],
            signal=t == TILES - 1)
    return m


def untranspose_tiles(st, bank, src, ident, rows=C, *after):
    st.pe.wait(*after, bank.free)
    for t in range(TILES):
        m = st.pe.do(st.pe.engine.transpose,
            bank.ap[:, t * P:t * P + rows], src[0:rows, t * P:(t + 1) * P], ident[0:rows, 0:rows],
            signal=t == TILES - 1)
    return m


def group(ap):
    return ap.rearrange("p (t c) -> p t c", t=TILES)


def evacuate_pair(st, pair, bank, m):
    hi, lo = pair.ap
    st.ac.wait(m, pair.free)
    a = st.ac.do(st.ac.engine.activation, hi, bank.ap, ACT.Copy)
    st.ve.wait(a)
    b = st.ve.do(st.ve.engine.tensor_tensor, lo, bank.ap, hi.bitcast(F32), ALU.subtract)
    bank.free = [b]
    return b


EXPERTS, INTER = 16, 64
CHUNKS = EXPERTS * INTER // P + 1
GROUPS4, PER_GROUP = 4, 4


def ffn0_tensors(sb):
    pair = lambda name, shape: (sb(name + "_hi", shape, F32R), sb(name + "_lo", shape, F32R))
    return {"w1": pair("w1", [P, CHUNKS, P]), "w3": pair("w3", [P, CHUNKS, P]), "w2": sb("w2", [P, CHUNKS, P]),
            "b13": sb("b13", [P, 2, CHUNKS]), "bs2": sb("bs2", [P, 1]), "b2": pair("b2", [P, P]),
            "gate": pair("gate", [P, EXPERTS]), "gate_b": sb("gate_b", [P, EXPERTS])}


def ffn0_weights(st, d, W, K, bank):
    ve, pe = st.ve, st.pe
    ld = Loads(st, "ffn0_loads")
    raw = {n: st.sb("raw_" + n, [P, CHUNKS, P]) for n in ("w1", "w3")}
    b2, gw = st.sb("raw_b2", [P, P]), st.sb("raw_gw", [EXPERTS, P])
    zero = ve.do(ve.engine.memset, b2[:, :], 0.0)
    for n, e, s in (("w1", "L0_ffn_We1", "L0_ffn_ws1"), ("w3", "L0_ffn_We3", "L0_ffn_ws3")):
        ld.add(raw[n][:, 0:8, :].rearrange("p c (e i) -> p (c e) i", e=2), d[e].rearrange("e d i -> d e i"))
        ld.add(raw[n][:, 8, :], d[s])
    ld.add(W["w2"][:, 0:8, :], d["L0_ffn_We2"].rearrange("e i d -> (e i) d").rearrange("(c p) d -> p c d", p=P))
    ld.add(W["w2"][:, 8, :], d["L0_ffn_ws2"])
    for k, (e, s) in enumerate((("L0_ffn_be1", "L0_ffn_bs1"), ("L0_ffn_be3", "L0_ffn_bs3"))):
        ld.add(W["b13"][:, k, 0:8], d[e].rearrange("e i -> (e i)").rearrange("(c p) -> p c", p=P), words=True)
        ld.add(W["b13"][:, k, 8:9], d[s].rearrange("(p a) -> p a", a=1), words=True)
    ld.add(W["bs2"][:, :], d["L0_ffn_bs2"].rearrange("(p a) -> p a", a=1), words=True)
    ld.add(W["gate_b"][:, :], row(d["L0_ffn_gate_b"]).to_broadcast([P, EXPERTS]))
    ld.add(gw[:, :], d["L0_ffn_gate_w"])
    ld.add(b2[0:EXPERTS, :], d["L0_ffn_be2"], zero)
    ld.add(b2[EXPERTS:2 * EXPERTS, :], d["L0_ffn_be2"])
    ve.wait(ld.all())
    for n in ("w1", "w3"):
        split_pair(ve, W[n][0][:, :, :], W[n][1][:, :, :], raw[n][:, :, :])
    split_pair(ve, W["b2"][0][:, :], W["b2"][1][:, :], b2[:, :])
    ve.do(ve.engine.tensor_scalar, W["bs2"][:, :], W["bs2"][:, :], 0.5, None, ALU.mult)
    pe.wait(ld.all(), K["ready"], bank.free)
    t = pe.do(pe.engine.transpose, bank.ap[:, 0:EXPERTS], gw[:, :], K["ident"][0:EXPERTS, 0:EXPERTS])
    bank.free = [split_pair(ve, W["gate"][0][:, :], W["gate"][1][:, :], bank.ap[:, 0:EXPERTS], t)]


def pick_first(chain, out, scores, key, key2, best, order):
    ve = chain.queue.engine
    bc = lambda a: a.unsqueeze(2).to_broadcast(list(scores.shape))
    chain.then(ve.tensor_reduce, best, scores, AX, ALU.max)
    yield
    chain.then(ve.tensor_tensor, key, scores, bc(best), ALU.is_equal)
    yield
    chain.then(ve.tensor_tensor, key2, key, order, ALU.mult)
    yield
    chain.then(ve.tensor_reduce, best, key2, AX, ALU.max)
    yield
    chain.then(ve.tensor_tensor, out, key2, bc(best), ALU.is_equal)
    yield


def ffn0(nc, ctx, name, X, W, K, groups):
    st = Stage(nc, name, ctx)
    pe, ve, ac, gp = st.pe, st.ve, st.ac, st.gp
    ident = K["ident"]
    norm = Norm(st, K)
    xn = Ring([st.sb(f"xn{i}", [P, GROUP]) for i in range(2)])
    pairs = Ring([(st.sb(f"xh{i}", [P, GROUP], F32R)[:, :], st.sb(f"xl{i}", [P, GROUP], F32R)[:, :])
                  for i in range(3)])
    lgT = Ring([st.sb(f"lgT{i}", [EXPERTS, GROUP]) for i in range(2)])
    h1 = Ring([st.sb(f"h1_{i}", [P, GROUP]) for i in range(4)])
    h3 = Ring([st.sb(f"h3_{i}", [P, GROUP]) for i in range(3)])
    hc = Ring([st.sb(f"hc{i}", [P, GROUP]) for i in range(4)])
    yT = Ring([st.sb(f"yT{i}", [P, GROUP]) for i in range(2)])
    combT = Ring([st.sb(f"combT{i}", [P, GROUP], F32R) for i in range(2)])
    routing = Ring([{**{k: st.sb(f"r{i}_" + k, [P, TILES, n])[:, :, :] for k, n in
                        (("e", 16), ("prob", 16), ("s", 16), ("pm", 8), ("psum", 8), ("gsum", 4), ("alt", 4),
                         ("gs", 4), ("g1", 4), ("g2", 4), ("k1", 4), ("k2", 4), ("pen", 4), ("ms", 16),
                         ("o1", 16), ("o2", 16), ("k3", 16), ("k4", 16), ("comb", 16))},
                     **{k: st.sb(f"c{i}_" + k, [P, TILES])[:, :] for k in ("mx", "sum", "best")}}
                    for i in range(2)])
    pairb = Ring([st.sb(f"pairb{i}", [P, TILES, 32], F32R) for i in range(2)])
    misc = Ring([st.ps(f"misc{i}", [P, 512]) for i in range(1)])
    up = Ring([st.ps(f"up{i}", [P, 512]) for i in range(4)])
    cw = Ring([st.ps(f"cw{i}", [P, 512]) for i in range(2)])
    acc = Slot(st.ps("acc", [P, 512]))
    zeros = [ve.do(ve.engine.memset, s.ap[:, :].bitcast(F32), 0.0) for s in combT.slots]

    def one(g):
        xg = X[:, g, :, :]
        h = norm.begin(xg, 1e-5)
        yield from rest(4)
        x = xn.next()
        xv = group(x.ap[:, :])
        m = norm.apply(ve, xv, xg, h, x.free)
        yield from rest(3)
        yield from opened(misc)
        bank = misc.next()
        m = transpose_tiles(st, bank, xv, ident, C, m)
        x.free = [m]
        yield from opened(pairs)
        pair = pairs.next()
        hi, lo = pair.ap
        ac.wait(m, pair.free)
        yield from rest(2)
        a = ac.do(ac.engine.activation, hi, bank.ap[:, :], ACT.Copy)
        yield from rest(2)
        ve.wait(a)
        pm = ve.do(ve.engine.tensor_tensor, lo, bank.ap[:, :], hi.bitcast(F32), ALU.subtract)
        bank.free = [pm]
        yield from rest(2)
        yield from opened(misc)
        bank = misc.next()
        pe.wait(pm, bank.free)
        m = matmul_pairs(pe, bank.ap[0:EXPERTS, :], [w[:, :] for w in W["gate"]], pair.ap)
        yield from opened(lgT)
        lt = lgT.next()
        yield from rest(3)
        ac.wait(m, lt.free)
        m = ac.do(ac.engine.activation, lt.ap[:, :], bank.ap[0:EXPERTS, :], ACT.Copy)
        bank.free = [m]
        yield from rest(2)
        yield from opened(misc)
        bank = misc.next()
        pe.wait(m, bank.free)
        for t in range(TILES):
            m = pe.do(pe.engine.transpose,
                bank.ap[:, t * EXPERTS:(t + 1) * EXPERTS], lt.ap[:, t * P:(t + 1) * P],
                ident[0:EXPERTS, 0:EXPERTS], signal=t == TILES - 1)
        lt.free = [m]
        lg = bank.ap[:, 0:TILES * EXPERTS].rearrange("p (t e) -> p t e", t=TILES)
        bc16 = lambda a: a.unsqueeze(2).to_broadcast([P, TILES, EXPERTS])
        yield from rest(2)
        yield from opened(routing)
        slot = routing.next()
        r = slot.ap
        ch = ve.chain(m, slot.free)
        E = ve.engine
        ch.then(E.tensor_reduce, r["mx"], lg, AX, ALU.max)
        yield
        m = ch.then(E.tensor_tensor, r["e"], lg, bc16(r["mx"]), ALU.subtract)
        bank.free = [m]
        yield
        ac.wait(m)
        ch.last = [ac.do(ac.engine.activation, r["e"], r["e"], ACT.Exp)]
        yield
        yield
        ch.then(E.tensor_reduce, r["sum"], r["e"], AX, ALU.add)
        yield
        ch.then(E.reciprocal, r["sum"], r["sum"])
        yield
        ch.then(E.tensor_tensor, r["prob"], r["e"], bc16(r["sum"]), ALU.mult)
        yield
        ch.then(E.tensor_tensor, r["s"], r["prob"],
                W["gate_b"][:, :].unsqueeze(1).to_broadcast([P, TILES, EXPERTS]), ALU.add)
        yield
        halves = lambda a: (a.rearrange("p t (g two) -> p t g two", two=2)[:, :, :, 0],
                            a.rearrange("p t (g two) -> p t g two", two=2)[:, :, :, 1])
        ch.then(E.tensor_tensor, r["pm"], *halves(r["s"]), ALU.max)
        yield
        ch.then(E.tensor_tensor, r["psum"], *halves(r["s"]), ALU.add)
        yield
        ch.then(E.tensor_tensor, r["gsum"], *halves(r["pm"]), ALU.add)
        yield
        ch.then(E.tensor_tensor, r["alt"], *halves(r["psum"]), ALU.max)
        yield
        ch.then(E.tensor_tensor, r["gs"], r["gsum"], r["alt"], ALU.max)
        yield
        order4 = K["order"][:, 0:4].unsqueeze(1).to_broadcast([P, TILES, 4])
        order16 = K["order"][:, :].unsqueeze(1).to_broadcast([P, TILES, 16])
        yield from pick_first(ch, r["g1"], r["gs"], r["k1"], r["k2"], r["best"], order4)
        ch.then(E.scalar_tensor_tensor, r["gs"], r["g1"], -BIG, r["gs"], ALU.mult, ALU.add)
        yield
        yield from pick_first(ch, r["g2"], r["gs"], r["k1"], r["k2"], r["best"], order4)
        ch.then(E.tensor_tensor, r["gsum"], r["g1"], r["g2"], ALU.add)
        yield
        ch.then(E.tensor_scalar, r["pen"], r["gsum"], BIG, -BIG, ALU.mult, ALU.add)
        yield
        by_group = lambda a: a.rearrange("p t (g e) -> p (t g) e", e=PER_GROUP)
        ch.then(E.tensor_tensor, by_group(r["ms"]), by_group(r["s"]),
                r["pen"].rearrange("p t g -> p (t g)").unsqueeze(2).to_broadcast([P, TILES * GROUPS4, PER_GROUP]), ALU.add)
        yield
        yield from pick_first(ch, r["o1"], r["ms"], r["k3"], r["k4"], r["best"], order16)
        ch.then(E.scalar_tensor_tensor, r["ms"], r["o1"], -BIG, r["ms"], ALU.mult, ALU.add)
        yield
        yield from pick_first(ch, r["o2"], r["ms"], r["k3"], r["k4"], r["best"], order16)
        ch.then(E.tensor_tensor, r["o1"], r["o1"], r["o2"], ALU.add)
        yield
        ch.then(E.tensor_tensor, r["comb"], r["o1"], r["prob"], ALU.mult)
        yield
        yield from opened(pairb)
        pb = pairb.next()
        ve.wait(pb.free)
        ch.then(E.tensor_copy, pb.ap[:, :, 0:16], r["comb"])
        yield
        m = ch.then(E.tensor_tensor, pb.ap[:, :, 16:32], r["comb"], pb.ap[:, :, 0:16].bitcast(F32), ALU.subtract)
        slot.free = [m]
        yield
        yield from opened(misc)
        bank = misc.next()
        pe.wait(m, bank.free)
        for t in range(TILES):
            m = pe.do(pe.engine.transpose,
                bank.ap[0:32, t * P:(t + 1) * P], pb.ap[:, t, :].bitcast(F32), ident[:, :],
                signal=t == TILES - 1)
        pb.free = [m]
        yield from rest(2)
        yield from opened(combT)
        ct = combT.next()
        ac.wait(m, ct.free, *zeros)
        cm = ac.do(ac.engine.activation, ct.ap[0:32, :], bank.ap[0:32, :], ACT.Copy)
        bank.free = [cm]
        yield from rest(2)
        down = []

        def down_proj():
            c, s = down.pop(0)
            pe.wait(s.ready)
            if c == 0:
                pe.wait(acc.free)
            s.free = [pe.do(pe.engine.matmul, acc.ap[:, :], W["w2"][:, c, :], s.ap[:, :], start=c == 0, stop=False)]
            return s.free[0]

        while acc.held:
            yield
        acc.claim()
        for c in range(CHUNKS):
            b1, b3 = up.next(), up.next()
            pe.wait(b1.free)
            m1 = matmul_pairs(pe, b1.ap[:, :], [w[:, c, :] for w in W["w1"]], pair.ap)
            pe.wait(b3.free)
            m3 = matmul_pairs(pe, b3.ap[:, :], [w[:, c, :] for w in W["w3"]], pair.ap)
            yield
            s1, s = h1.next(), hc.next()
            last = s if c == CHUNKS - 1 else h3.next()
            ac.wait(m1, s1.free)
            a = ac.do(ac.engine.activation, s1.ap[:, :], b1.ap[:, :], ACT.Silu, bias=W["b13"][:, 0, c:c + 1])
            b1.free = [a]
            yield
            ve.wait(m3, a, last.free)
            b = ve.do(ve.engine.scalar_tensor_tensor, last.ap[:, :], b3.ap[:, :], W["b13"][:, 1, c:c + 1], s1.ap[:, :], ALU.add, ALU.mult)
            b3.free, s1.free = [b], [b]
            s.ready = b
            yield
            if c < CHUNKS - 1:
                wb = cw.next()
                pe.wait(cm, wb.free)
                m = pe.do(pe.engine.matmul, wb.ap[:, :], K["spread"][:, c, :], ct.ap[:, :], start=True, stop=True)
                ve.wait(m, b, s.free)
                s.ready = ve.do(ve.engine.tensor_tensor, s.ap[:, :], wb.ap[:, :], last.ap[:, :], ALU.mult)
                wb.free, last.free = [s.ready], [s.ready]
            down.append((c, s))
            if c >= 2:
                down_proj()
            yield
        pair.free = [m3]
        while down:
            down_proj()
        for n in range(2):
            m = pe.do(pe.engine.matmul, acc.ap[:, :], W["b2"][n][:, :], ct.ap[:, :], start=False, stop=n == 1, signal=n == 1)
        ct.free = [m]
        y = yT.next()
        ac.wait(m, y.free)
        m = ac.do(ac.engine.activation, y.ap[:, :], acc.ap[:, :], ACT.Identity, scale=0.5, bias=W["bs2"][:, :])
        acc.free = [m]
        yield from rest(3)
        yield from opened(misc)
        bank = misc.next()
        m = untranspose_tiles(st, bank, y.ap, ident, C, m)
        y.free = [m]
        yield from rest(2)
        ve.wait(m)
        m = ve.do(ve.engine.tensor_tensor, xg, xg, group(bank.ap[:, :]), ALU.add)
        bank.free = [m]
        yield

    staggered(one, groups, 3, 38)
    st.run()


HEADS, HDIM = 16, 8
SETS = 4
BLOCK = P // SETS
MROWS = 2
PRODUCTS = 3
ROWS = MROWS + PRODUCTS * HDIM


class SlotDma:

    def __init__(self, st, name):
        self.q, self.count = st.sp, 0
        self.sem = st.ctx.enter_context(st.nc.semaphore(f"{st.name}_{name}"))

    def start(self, out, in_, *after):
        self.q.wait(*after)
        self.count += 16
        self.q.items.append(lambda: self.q.engine.dma_start(out, in_).then_inc(self.sem, 16))
        return (self.sem, self.count)


def attn0_tensors(sb):
    pair = lambda name, shape: (sb(name + "_hi", shape, F32R), sb(name + "_lo", shape, F32R))
    return {"q": pair("aq", [P, SETS, P]), "k": pair("ak", [P, SETS, P]), "v": pair("av", [P, C]),
            "proj": pair("aproj", [P, C]), "cols": sb("acols", [P, 2 * SETS + 2]),
            "bv": sb("abv", [P, C]), "pb": sb("apb", [P, C])}


def attn0_weights(st, d, A, K, bank):
    ve, pe = st.ve, st.pe
    ld = Loads(st, "attn0_loads")
    qkv, proj = st.sb("raw_qkv", [P, 3 * C]), st.sb("raw_proj", [P, C])
    qkv_b = st.sb("raw_qkv_b", [1, 3 * C])
    rep = st.sb("rep", [P, 2, HEADS, BLOCK])
    rows = st.sb("rows", [1, 2 * SETS + 2, SETS, BLOCK])
    z = [ve.do(ve.engine.memset, rep[:, :, :, :], 0.0), ve.do(ve.engine.memset, rows[:, :, :, :], 0.0)]
    ld.add(qkv[:, :], d["L0_attn_qkv_w"])
    ld.add(proj[:, :], d["L0_attn_proj_w"])
    ld.add(qkv_b[:, :], row(d["L0_attn_qkv_b"]))
    ld.add(A["bv"][:, :], row(d["L0_attn_qkv_b"])[:, 2 * C:3 * C].to_broadcast([P, C]))
    ld.add(A["pb"][:, :], row(d["L0_attn_proj_b"]).to_broadcast([P, C]))
    ve.wait(ld.all(), *z)
    for k in range(2):
        for p in range(PRODUCTS):
            lo = MROWS + p * HDIM
            m = ve.do(ve.engine.tensor_copy, rep[:, k, :, lo:lo + HDIM],
                      qkv[:, k * C:(k + 1) * C].rearrange("p (h d) -> p h d", d=HDIM))
            n = ve.do(ve.engine.tensor_copy,
                      rows[:, k * SETS:(k + 1) * SETS, :, lo:lo + HDIM].rearrange("p s j d -> p (s j) d"),
                      qkv_b[:, k * C:(k + 1) * C].rearrange("p (h d) -> p h d", d=HDIM))
    ve.do(ve.engine.memset, rows[:, SETS:2 * SETS, :, 0:MROWS], 1.0)
    ve.do(ve.engine.memset, rows[:, 2 * SETS, :, MROWS + 2 * HDIM:ROWS], 1.0)
    r = ve.do(ve.engine.memset, rows[:, 2 * SETS + 1, :, MROWS + HDIM:MROWS + 2 * HDIM], 1.0)
    for k, name in enumerate("qk"):
        v = rep[:, k, :, :].rearrange("p (s j) r -> p s (j r)", s=SETS)
        split_pair(ve, A[name][0][:, :, :], A[name][1][:, :, :], v, m)
    split_pair(ve, A["v"][0][:, :], A["v"][1][:, :], qkv[:, 2 * C:3 * C])
    split_pair(ve, A["proj"][0][:, :], A["proj"][1][:, :], proj[:, :])
    pe.wait(r, n, bank.free)
    for i in range(2 * SETS + 2):
        t = pe.do(pe.engine.matmul, bank.ap[:, i:i + 1], rows[:, i, :, :].rearrange("p j r -> p (j r)"),
                  K["ident"][0:1, 0:1], start=True, stop=True)
    ve.wait(t)
    bank.free = [ve.do(ve.engine.tensor_copy, A["cols"][:, :], bank.ap[:, 0:2 * SETS + 2])]


HOP = 2


def attn0(nc, ctx, name, X, A, K, groups):
    st = Stage(nc, name, ctx)
    pe, ve, ac, gp = st.pe, st.ve, st.ac, st.gp
    ident = K["ident"]
    scale = float(HDIM) ** -0.5
    norm = Norm(st, K)
    xn = Ring([st.sb(f"xn{i}", [P, GROUP]) for i in range(1)])
    pairs = Ring([(st.sb(f"xh{i}", [P, GROUP], F32R)[:, :], st.sb(f"xl{i}", [P, GROUP], F32R)[:, :]) for i in range(2)])
    raw = Ring([st.sb(f"raw{i}", [P, GROUP]) for i in range(2)])
    hid = Ring([st.sb(f"hid{i}", [P, GROUP], F32R) for i in range(2)])
    qs = Ring([st.sb(f"qs{i}", [P, GROUP], F32R) for i in range(2)])
    ks = Ring([st.sb(f"ks{i}", [P, GROUP], F32R) for i in range(3)])
    qz = [Ring([st.sb(f"qz{i}_{j}", [P, GROUP], F32R) for i in range(3)]) for j in range(SETS)]
    vx = Ring([st.sb(f"vx{i}", [P, TILES, HEADS, BLOCK]) for i in range(2)])
    mx = Ring([st.sb(f"mx{i}", [P, TILES, SETS]) for i in range(2)])
    mt = Ring([st.sb(f"mt{i}", [P, TILES, SETS, BLOCK], F32R) for i in range(2)])
    mrow = Ring([st.sb(f"mrow{i}", [P, GROUP], F32R) for i in range(2)])
    pt = Ring([st.sb(f"pt{i}", [P, GROUP]) for i in range(8)])
    oT = Ring([st.sb(f"oT{i}", [P, GROUP]) for i in range(2)])
    rec = Ring([st.sb(f"rec{i}", [P, TILES, SETS]) for i in range(2)])
    otok = Ring([st.sb(f"otok{i}", [P, GROUP]) for i in range(2)])
    opair = Ring([(st.sb(f"oh{i}", [P, GROUP], F32R)[:, :], st.sb(f"ol{i}", [P, GROUP], F32R)[:, :]) for i in range(1)])
    misc = Ring([st.ps(f"misc{i}", [P, 512])[:, :] for i in range(2)])
    sbank = Ring([st.ps(f"s{i}", [P, 512])[:, :] for i in range(3)])
    tbank = Ring([st.ps(f"t{i}", [P, 512])[:, :] for i in range(2)])
    obank = Slot(st.ps("o", [P, 512])[:, :])
    for ring in qz:
        for i, s in enumerate(ring.slots):
            s.dma = SlotDma(st, f"qz{qz.index(ring)}{i}")
            s.free = [ve.do(ve.engine.memset, s.ap[:, :].bitcast(F32), 0.0)]
    for s in mt.slots:
        s.free = [ve.do(ve.engine.memset, s.ap[:, :, :, :].bitcast(F32), 0.0)]
    for s in vx.slots:
        z = ve.do(ve.engine.memset, s.ap[:, :, :, :], 0.0)
        ve.wait(z)
        s.free = [ve.do(ve.engine.memset, s.ap[:, :, :, HDIM:HDIM + 1], 1.0)]
    batches = {}

    def operand(b, k, s, out):
        yield from opened(misc)
        bank = misc.next()
        pe.wait(bank.free, b["pair"].ready)
        m = matmul_pairs(pe, bank.ap, [w[:, s, :] for w in A["qk"[k]]], b["pair"].ap)
        b["pair"].used.append(m)
        yield from rest(HOP)
        yield from opened(raw)
        r = raw.next()
        yield from opened(hid)
        h = hid.next()
        ac.wait(m, r.free)
        c = k * SETS + s
        m = ac.do(ac.engine.activation, r.ap[:, :], bank.ap, ACT.Identity, bias=A["cols"][:, c:c + 1])
        bank.free = [m]
        a = 2 * SETS + k
        yield from rest(HOP)
        ve.wait(m, h.free)
        m = ve.do(ve.engine.tensor_scalar, h.ap[:, :], r.ap[:, :], A["cols"][:, a:a + 1], None, ALU.mult)
        gp.wait(m, out.free)
        out.ready = gp.do(gp.engine.tensor_tensor, out.ap[:, :], r.ap[:, :], h.ap[:, :].bitcast(F32), ALU.subtract)
        r.free, h.free = [out.ready], [out.ready]
        yield

    def unit(n):
        g, s = divmod(n, SETS)
        xg = X[:, g, :, :]
        if s == 0:
            b = batches[g] = {}
            h = norm.begin(xg, 1e-5)
            yield from rest(4)
            yield from opened(xn)
            x = xn.next()
            xv = group(x.ap[:, :])
            m = norm.apply(ve, xv, xg, h, x.free)
            gp.wait(m)
            b["biased"] = gp.do(gp.engine.tensor_tensor, xg, xg, A["pb"][:, :].unsqueeze(1).to_broadcast([P, TILES, C]), ALU.add)
            yield from rest(HOP)
            yield from opened(misc)
            bank = misc.next()
            m = transpose_tiles(st, bank, xv, ident, C, m)
            x.free = [m]
            yield from rest(1)
            yield from opened(pairs)
            b["pair"] = pairs.next()
            b["pair"].ready = evacuate_pair(st, b["pair"], bank, m)
            b["pair"].used = []
            yield from rest(HOP)
            yield from opened(misc)
            bank = misc.next()
            pe.wait(bank.free, b["pair"].ready)
            for t in range(TILES):
                m = matmul_pairs(pe, bank.ap[:, t * P:(t + 1) * P], [v[:, t * P:(t + 1) * P] for v in b["pair"].ap],
                                 [w[:, :] for w in A["v"]], signal=t == TILES - 1)
                yield
            b["pair"].used.append(m)
            yield from opened(vx)
            b["v"] = vx.next()
            ve.wait(m, b["v"].free)
            for t in range(TILES):
                m = ve.do(ve.engine.tensor_tensor, b["v"].ap[:, t, :, 0:HDIM],
                          bank.ap[:, t * P:(t + 1) * P].rearrange("p (h d) -> p h d", d=HDIM),
                          A["bv"][:, :].rearrange("p (h d) -> p h d", d=HDIM), ALU.add)
            b["v"].ready = m
            bank.free = [m]
            yield from opened(otok)
            b["o"] = otok.next()
            b["v"].used, b["o"].written = [], []
            yield
            b["prepared"] = True
        b = batches[g]
        while "prepared" not in b:
            yield
        while not (ks.open() and qs.open() and all(ring.open() for ring in qz)):
            yield
        k_op, q_op, zs = ks.next(), qs.next(), [ring.next() for ring in qz]
        yield from operand(b, 0, s, q_op)
        yield from operand(b, 1, s, k_op)
        if s == SETS - 1:
            b["pair"].free = b["pair"].used
        heads = []
        for j in range(SETS):
            z = zs[j]
            lo = j * BLOCK
            z.ready = z.dma.start(z.ap[lo:lo + ROWS, :].bitcast(F32), q_op.ap[lo:lo + ROWS, :].bitcast(F32), q_op.ready, z.free)
            heads.append(z)
        q_op.free = [z.ready for z in heads]
        yield from rest(4)
        yield from opened(mx)
        top = mx.next()
        for j in range(SETS):
            for t in range(TILES):
                bank = sbank.next()
                pe.wait(bank.free, heads[j].ready, k_op.ready)
                m = pe.do(pe.engine.matmul, bank.ap, heads[j].ap[:, t * P:(t + 1) * P], k_op.ap[:, :], start=True, stop=True)
                ve.wait(m, top.free)
                m2 = ve.do(ve.engine.tensor_reduce, top.ap[:, t, j:j + 1], bank.ap, AX, ALU.max)
                bank.free = [m2]
                yield
            heads[j].scored = m
        yield from opened(mt)
        q = mt.next()
        ve.wait(m2, q.free)
        m = ve.do(ve.engine.tensor_scalar, q.ap[:, :, :, 0], top.ap[:, :, :], -1.0, None, ALU.mult)
        ve.wait(m)
        m = ve.do(ve.engine.scalar_tensor_tensor, q.ap[:, :, :, 1], top.ap[:, :, :], -1.0, q.ap[:, :, :, 0].bitcast(F32), ALU.mult, ALU.subtract)
        top.free = [m]
        yield from rest(1)
        yield from opened(misc)
        bank = misc.next()
        pe.wait(m, bank.free)
        for t in range(TILES):
            m = pe.do(pe.engine.transpose, bank.ap[:, t * P:(t + 1) * P],
                      q.ap[:, t, :, :].rearrange("p j r -> p (j r)").bitcast(F32), ident[:, :], signal=t == TILES - 1)
        q.free = [m]
        yield from rest(1)
        yield from opened(mrow)
        r = mrow.next()
        ac.wait(m, r.free)
        m = ac.do(ac.engine.activation, r.ap[:, :], bank.ap, ACT.Copy)
        bank.free = [m]
        for j, z in enumerate(heads):
            lo = j * BLOCK
            z.ready = z.dma.start(z.ap[lo:lo + MROWS, :].bitcast(F32), r.ap[lo:lo + MROWS, :].bitcast(F32), m, z.scored)
        r.free = [z.ready for z in heads]
        yield from rest(4)
        while obank.held:
            yield
        obank.claim()
        def weigh(t, probs):
            for j, p in enumerate(probs):
                pe.wait(p.ready, b["v"].ready)
                if t == 0:
                    pe.wait(obank.free)
                m = pe.do(pe.engine.matmul, obank.ap[j * BLOCK:(j + 1) * BLOCK, :], b["v"].ap[:, t, s * SETS + j, :],
                          p.ap[:, :], start=t == 0, stop=t == TILES - 1, signal=j == SETS - 1)
            for p in probs:
                p.free = [m]
            return m

        late = None
        for t in range(TILES):
            probs = []
            for j in range(SETS):
                bank = tbank.next()
                pe.wait(bank.free, heads[j].ready)
                m = pe.do(pe.engine.matmul, bank.ap, k_op.ap[:, t * P:(t + 1) * P], heads[j].ap[:, :], start=True, stop=True)
                if t == TILES - 1:
                    heads[j].free = [m]
                p = pt.next()
                ac.wait(m, p.free)
                p.ready = ac.do(ac.engine.activation, p.ap[:, :], bank.ap, ACT.Exp, scale=scale)
                bank.free = [p.ready]
                probs.append(p)
                if j == 1 and late:
                    weigh(*late)
                    late = None
                yield
            late = (t, probs)
        k_op.free = [m]
        yield
        m = weigh(*late)
        b["v"].used.append(m)
        yield from opened(oT)
        o = oT.next()
        ac.wait(m, o.free)
        m = ac.do(ac.engine.activation, o.ap[:, :], obank.ap, ACT.Copy)
        obank.free = [m]
        yield from rest(1)
        yield from opened(misc)
        bank = misc.next()
        m = untranspose_tiles(st, bank, o.ap, ident, P, m)
        o.free = [m]
        v = bank.ap.rearrange("p (t j r) -> p t j r", t=TILES, j=SETS)
        yield from rest(1)
        yield from opened(rec)
        rc = rec.next()
        ve.wait(m, rc.free, b["o"].free)
        m = ve.do(ve.engine.reciprocal, rc.ap[:, :, :], v[:, :, :, HDIM])
        ve.wait(m)
        for t in range(TILES):
            lo = t * P + s * SETS * HDIM
            m = ve.do(ve.engine.tensor_tensor, b["o"].ap[:, lo:lo + SETS * HDIM].rearrange("p (j d) -> p j d", d=HDIM),
                      v[:, t, :, 0:HDIM], rc.ap[:, t, :].unsqueeze(2).to_broadcast([P, SETS, HDIM]), ALU.mult)
        bank.free, rc.free = [m], [m]
        b["o"].written.append(m)
        yield
        if s == SETS - 1:
            b["v"].free = b["v"].used
            yield from opened(misc)
            bank = misc.next()
            m = transpose_tiles(st, bank, group(b["o"].ap[:, :]), ident, C, *b["o"].written)
            b["o"].free = [m]
            yield from rest(1)
            yield from opened(opair)
            pair = opair.next()
            m = evacuate_pair(st, pair, bank, m)
            yield from rest(HOP)
            yield from opened(misc)
            bank = misc.next()
            pe.wait(m, bank.free)
            for t in range(TILES):
                m = matmul_pairs(pe, bank.ap[:, t * P:(t + 1) * P], [v[:, t * P:(t + 1) * P] for v in pair.ap],
                                 [w[:, :] for w in A["proj"]], signal=t == TILES - 1)
                yield
            pair.free = [m]
            ve.wait(m, b["biased"])
            bank.free = [ve.do(ve.engine.tensor_tensor, xg, xg, group(bank.ap), ALU.add)]
            yield

    staggered(unit, groups * SETS, 5, 16)
    st.run()


CLUSTERS, PER_CLUSTER = 8, 8
NTILES = CLUSTERS * PER_CLUSTER
SCORES = NTILES + CLUSTERS
KNOTS, GRID, COMP_H = 8, 16, 32
COMP0 = 96
COMP_ROWS = COMP0 + 2
PARAM = {"dir": 0, "w1": C, "b1": C + 2 * GRID, "w2": C + 3 * GRID, "b2": C + 4 * GRID}
PARAMS = C + 4 * GRID + 2


def ffn1_tensors(sb):
    pair = lambda name, shape: (sb(name + "_hi", shape, F32R), sb(name + "_lo", shape, F32R))
    return {"score": pair("vscore", [P, P]), "ninv": sb("vninv", [P, 1]), "knots": sb("vknots", [P, KNOTS]),
            "slope": sb("vslope", [P, KNOTS - 1]), "cb1": sb("vcb1", [P, 1]), "cw2": sb("vcw2", [P, 2]),
            "cb2": sb("vcb2", [P, 1]), "params": pair("vparams", [NTILES, PARAMS]),
            "gamma": sb("vgamma", [P, C]), "beta": sb("vbeta", [P, C]), "scale": sb("vscale", [P, 1])}


def ffn1_weights(st, d, V, K, bank):
    ve, pe = st.ve, st.pe
    ld = Loads(st, "ffn1_loads")
    D = lambda name: d["L1_ffn_" + name]
    sig, w, par = st.sb("raw_sig", [NTILES, C]), st.sb("raw_score", [P, P]), st.sb("raw_par", [NTILES, PARAMS])
    t = {n: st.sb("sig_" + n, [P, NTILES]) for n in ("raw", "pos", "neg")}
    cl = {n: st.sb("cl_" + n, [P, CLUSTERS]) for n in ("sum", "pos", "neg")}
    z = [ve.do(ve.engine.memset, w[:, :], 0.0), ve.do(ve.engine.memset, par[:, :], 0.0)]
    ld.add(sig[:, :], D("signatures_raw"), *z)
    ld.add(w[:, COMP0:P], D("compress_w1"))
    ld.add(V["ninv"][:, :], row(D("temperature")).to_broadcast([P, 1]))
    ld.add(V["knots"][:, :], row(D("knot_values")).to_broadcast([P, KNOTS]))
    ld.add(V["scale"][:, :], row(D("output_scale")).to_broadcast([P, 1]))
    ld.add(V["gamma"][:, :], row(D("norm_gamma")).to_broadcast([P, C]))
    ld.add(V["beta"][:, :], row(D("norm_beta")).to_broadcast([P, C]))
    ld.add(V["cb1"][COMP0:P, :], D("compress_b1").rearrange("(p a) -> p a", a=1), words=True)
    ld.add(V["cw2"][COMP0:P, :], D("compress_w2"))
    ld.add(V["cb2"][COMP0:COMP_ROWS, :], D("compress_b2").rearrange("(p a) -> p a", a=1), words=True)
    at = lambda name, n: par[:, PARAM[name]:PARAM[name] + n]
    ld.add(at("dir", C), D("directions"))
    ld.add(at("w1", 2 * GRID), D("spline_w1").rearrange("n i g -> n (i g)"))
    ld.add(at("b1", GRID), D("spline_b1"))
    ld.add(at("w2", GRID), D("spline_w2").rearrange("n g o -> n (g o)"))
    ld.add(at("b2", 1), D("spline_b2"), words=True)
    pe.wait(ld.all(), bank.free)
    m = pe.do(pe.engine.transpose, bank.ap[:, 0:NTILES], sig[:, :], K["ident"][0:NTILES, 0:NTILES])
    ve.wait(m, ld.all())
    ve.do(ve.engine.tensor_copy, t["raw"][:, :], bank.ap[:, 0:NTILES])
    ve.do(ve.engine.tensor_scalar, t["pos"][:, :], bank.ap[:, 0:NTILES], 0.3, None, ALU.is_gt)
    bank.free = [ve.do(ve.engine.tensor_scalar, t["neg"][:, :], bank.ap[:, 0:NTILES], -0.3, None, ALU.is_lt)]
    ve.then(ve.engine.tensor_tensor, t["pos"][:, :], t["pos"][:, :], t["neg"][:, :], ALU.subtract)
    ve.then(ve.engine.tensor_tensor, t["pos"][:, :], t["pos"][:, :], t["raw"][:, :], ALU.subtract)
    ve.then(ve.engine.tensor_tensor, w[:, 0:NTILES], t["pos"][:, :], t["raw"][:, :], ALU.add)
    v = w[:, 0:NTILES].rearrange("p (c l) -> p c l", l=PER_CLUSTER)
    ve.then(ve.engine.tensor_copy, cl["sum"][:, :], v[:, :, 0])
    for k in range(1, PER_CLUSTER):
        ve.then(ve.engine.tensor_tensor, cl["sum"][:, :], cl["sum"][:, :], v[:, :, k], ALU.add)
    ve.then(ve.engine.tensor_scalar, cl["pos"][:, :], cl["sum"][:, :], 0.0, None, ALU.is_gt)
    ve.then(ve.engine.tensor_scalar, cl["neg"][:, :], cl["sum"][:, :], 0.0, None, ALU.is_lt)
    m = ve.then(ve.engine.tensor_tensor, w[:, NTILES:SCORES], cl["pos"][:, :], cl["neg"][:, :], ALU.subtract)
    split_pair(ve, V["score"][0][:, :], V["score"][1][:, :], w[:, :], m)
    split_pair(ve, V["params"][0][:, :], V["params"][1][:, :], par[:, :])
    ve.then(ve.engine.tensor_scalar, V["ninv"][:, :], V["ninv"][:, :], 1e-6, None, ALU.add)
    ve.then(ve.engine.reciprocal, V["ninv"][:, :], V["ninv"][:, :])
    ve.then(ve.engine.tensor_scalar, V["ninv"][:, :], V["ninv"][:, :], -1.0, None, ALU.mult)
    ve.then(ve.engine.tensor_tensor, V["slope"][:, :], V["knots"][:, 1:KNOTS], V["knots"][:, 0:KNOTS - 1], ALU.subtract)
    for name in ("gamma", "beta"):
        ve.then(ve.engine.tensor_scalar, V[name][:, :], V[name][:, :], 0.5, None, ALU.mult)


AHEAD = (2, 4, 6)
LIVE = 4


def ffn1(nc, ctx, name, X, V, K, groups):
    st = Stage(nc, name, ctx)
    pe, ve, ac, gp = st.pe, st.ve, st.ac, st.gp
    ident = K["ident"]
    norm = Norm(st, K, 2 * LIVE)
    xn = Ring([st.sb(f"xn{i}", [P, GROUP]) for i in range(LIVE)])
    pairs = Ring([(st.sb(f"xh{i}", [P, GROUP], F32R)[:, :], st.sb(f"xl{i}", [P, GROUP], F32R)[:, :]) for i in range(2)])
    arg = Ring([st.sb(f"arg{i}", [P, GROUP]) for i in range(2)])
    hT = Ring([st.sb(f"hT{i}", [P, GROUP]) for i in range(2)])
    sT = Ring([st.sb(f"sT{i}", [P, GROUP]) for i in range(2)])
    ohT = Ring([st.sb(f"ohT{i}", [NTILES, GROUP], F32R) for i in range(2)])
    yb = Ring([st.sb(f"y{i}", [P, GROUP]) for i in range(LIVE)])
    W = {k: Ring([st.sb(f"{k}{i}", [P, TILES, n]) for i in range(LIVE)]) for k, n in
         (("u", SCORES), ("piece", SCORES), ("gate", SCORES), ("masked", NTILES), ("comp", 2), ("sel", 8), ("oc", 8),
          ("ol", 8), ("k1", 8), ("k2", 8), ("oh", NTILES), ("ha", GRID), ("hb", GRID))}
    W["past"] = Ring([st.sb(f"past{i}", [P, TILES, KNOTS - 1, SCORES]) for i in range(LIVE)])
    cols = {k: Ring([st.sb(f"{k}{i}", [P, TILES]) for i in range(LIVE)]) for k in ("best", "mag")}
    misc = Ring([st.ps(f"misc{i}", [P, 512])[:, :] for i in range(2)])
    sbank = Ring([st.ps(f"s{i}", [P, 512])[:, :] for i in range(2)])
    pbank = Ring([st.ps(f"p{i}", [P, 1024]) for i in range(2)])
    for s in sT.slots:
        s.free = [ve.do(ve.engine.memset, s.ap[:, :], 0.0)]

    def one(g):
        xg = X[:, g, :, :]
        h = norm.begin(xg, 1e-5)
        yield from rest(4)
        x = xn.next()
        xv = group(x.ap[:, :])
        m = norm.apply(ve, xv, xg, h, x.free)
        x.ready = m
        gp.wait(m)
        shifted = gp.do(gp.engine.tensor_tensor, xg, xg, V["beta"][:, :].unsqueeze(1).to_broadcast([P, TILES, C]), ALU.add)
        yield from rest(2)
        yield from opened(misc)
        bank = misc.next()
        m = transpose_tiles(st, bank, xv, ident, C, m)
        yield from opened(pairs)
        pair = pairs.next()
        m = evacuate_pair(st, pair, bank, m)
        yield from rest(3)
        yield from opened(sbank)
        bank = sbank.next()
        pe.wait(bank.free)
        pe.wait(m)
        m = matmul_pairs(pe, bank.ap, [w[:, :] for w in V["score"]], pair.ap)
        pair.free = [m]
        yield from rest(2)
        yield from opened(hT)
        ht, a, s = hT.next(), arg.next(), sT.next()
        ac.wait(m, ht.free)
        m2 = ac.do(ac.engine.activation, ht.ap[COMP0:P, :], bank.ap[COMP0:P, :], ACT.Gelu, bias=V["cb1"][COMP0:P, :])
        ve.wait(m, a.free)
        m1 = ve.do(ve.engine.tensor_scalar, a.ap[0:SCORES, :], bank.ap[0:SCORES, :], V["ninv"][0:SCORES, :], 80.0, ALU.mult, ALU.min)
        bank.free = [m1, m2]
        yield from opened(misc)
        bank = misc.next()
        pe.wait(m2, bank.free)
        m = pe.do(pe.engine.matmul, bank.ap[COMP0:COMP_ROWS, :], V["cw2"][COMP0:P, :], ht.ap[COMP0:P, :], start=True, stop=True)
        ht.free = [m]
        yield from rest(2)
        ac.wait(m1, s.free)
        m1 = ac.do(ac.engine.activation, s.ap[0:SCORES, :], a.ap[0:SCORES, :], ACT.Exp)
        a.free = [m1]
        ac.wait(m)
        m = ac.do(ac.engine.activation, s.ap[COMP0:COMP_ROWS, :], bank.ap[COMP0:COMP_ROWS, :], ACT.Tanh, bias=V["cb2"][COMP0:COMP_ROWS, :])
        bank.free = [m]
        yield from opened(misc)
        bank = misc.next()
        m = untranspose_tiles(st, bank, s.ap, ident, COMP_ROWS, m1, m)
        s.free = [m]
        yield from rest(2)
        B = {k: ring.next() for k, ring in W.items()}
        Cc = {k: ring.next() for k, ring in cols.items()}
        R = {k: s_.ap[:, :, :] for k, s_ in B.items() if k != "past"}
        R["past"] = B["past"].ap[:, :, :, :]
        col = {k: s_.ap[:, :] for k, s_ in Cc.items()}
        v = group(bank.ap)
        used = [s_.free for s_ in list(B.values()) + list(Cc.values())]
        ch = ve.chain(m, *used)
        ch.then(ve.engine.tensor_copy, R["comp"], v[:, :, COMP0:COMP_ROWS])
        yield
        bank.free = [ch.then(ve.engine.tensor_scalar, R["u"], v[:, :, 0:SCORES], 1.0, None, ALU.add)]
        yield
        ch.then(ve.engine.reciprocal, R["u"], R["u"])
        yield
        u_ready = ch.then(ve.engine.tensor_scalar, R["u"], R["u"], float(KNOTS - 1), None, ALU.mult)
        yield
        gp.wait(*used, u_ready)
        ahead = {j: gp.do(gp.engine.tensor_scalar, R["past"][:, :, j, :], R["u"], float(j), 0.0, ALU.subtract, ALU.max)
                 for j in AHEAD}
        for j in range(KNOTS - 1):
            past = R["past"][:, :, j, :]
            if j in ahead:
                ve.wait(ahead[j])
            else:
                ch.then(ve.engine.tensor_scalar, past, R["u"], float(j), 0.0, ALU.subtract, ALU.max)
                yield
            piece = R["gate" if j == 0 else "piece"]
            ch.then(ve.engine.scalar_tensor_tensor, piece, past, V["slope"][:, j:j + 1],
                    V["knots"][:, j:j + 1].unsqueeze(1).to_broadcast([P, TILES, SCORES]), ALU.mult, ALU.add)
            yield
            if j:
                ch.then(ve.engine.copy_predicated, R["gate"], past.bitcast(mybir.dt.uint32), piece)
                yield
        order = K["order"][:, 0:8].unsqueeze(1).to_broadcast([P, TILES, 8])
        yield from pick_first(ch, R["oc"], R["gate"][:, :, NTILES:SCORES], R["k1"], R["k2"], col["best"], order)
        for t in range(TILES):
            ve.wait(*ch.last)
            m = ve.do(ve.engine.tensor_tensor, R["masked"][:, t, :].rearrange("p (c l) -> p c l", l=8),
                      R["gate"][:, t, 0:NTILES].rearrange("p (c l) -> p c l", l=8),
                      R["oc"][:, t, :].unsqueeze(2).to_broadcast([P, 8, 8]), ALU.mult)
        ch.last = [m]
        yield
        ch.then(ve.engine.tensor_reduce, R["sel"], R["masked"].rearrange("p t (c l) -> p t l c", l=8), AX, ALU.add)
        yield
        yield from pick_first(ch, R["ol"], R["sel"], R["k1"], R["k2"], col["best"], order)
        ve.wait(*ch.last)
        for t in range(TILES):
            m = ve.do(ve.engine.tensor_tensor, R["oh"][:, t, :].rearrange("p (c l) -> p c l", l=8),
                      R["oc"][:, t, :].unsqueeze(2).to_broadcast([P, 8, 8]),
                      R["ol"][:, t, :].unsqueeze(1).to_broadcast([P, 8, 8]), ALU.mult)
        yield
        yield from rest(2)
        yield from opened(misc)
        bank = misc.next()
        m = transpose_tiles(st, bank, R["oh"], ident, NTILES, m)
        yield from opened(ohT)
        o = ohT.next()
        ac.wait(m, o.free)
        m = ac.do(ac.engine.activation, o.ap[:, :], bank.ap[0:NTILES, :], ACT.Copy)
        bank.free = [m]
        yield from rest(2)
        yield from opened(pbank)
        pb = pbank.next()
        pe.wait(m, pb.free)
        par = pb.ap[:, :].rearrange("p (b n) -> p b n", b=2)
        for t in range(TILES):
            dst = par[:, t // 2, (t % 2) * PARAMS:(t % 2 + 1) * PARAMS]
            for k in range(2):
                m = pe.do(pe.engine.matmul, dst, o.ap[:, t * P:(t + 1) * P], V["params"][k][:, :], start=k == 0, stop=k == 1,
                          signal=k == 1)
        o.free = [m]
        yield from rest(2)
        par = par[:, :, 0:2 * PARAMS].rearrange("p b (t n) -> p b t n", t=2)
        at = lambda name, n, off=0: par[:, :, :, PARAM[name] + off:PARAM[name] + off + n]
        four = lambda a: a.rearrange("p (b t) g -> p b t g", b=2)
        coord = lambda i: four(R["comp"][:, :, i:i + 1].to_broadcast([P, TILES, GRID]))
        ch = ve.chain(m)
        ch.then(ve.engine.tensor_tensor, four(R["ha"]), at("w1", GRID), coord(0), ALU.mult)
        yield
        ch.then(ve.engine.tensor_tensor, four(R["hb"]), at("w1", GRID, GRID), coord(1), ALU.mult)
        yield
        ch.then(ve.engine.tensor_tensor, R["ha"], R["ha"], R["hb"], ALU.add)
        yield
        ch.then(ve.engine.tensor_tensor, four(R["ha"]), at("b1", GRID), four(R["ha"]), ALU.add)
        yield
        ch.then(ve.engine.tensor_scalar, R["ha"], R["ha"], 0.0, None, ALU.max)
        yield
        ch.then(ve.engine.tensor_tensor, four(R["hb"]), at("w2", GRID), four(R["ha"]), ALU.mult)
        yield
        ch.then(ve.engine.tensor_reduce, col["mag"], R["hb"], AX, ALU.add)
        yield
        two = col["mag"].rearrange("p (b t) -> p b t", b=2)
        ch.then(ve.engine.tensor_tensor, two, par[:, :, :, PARAM["b2"]], two, ALU.add)
        yield
        m = ch.then(ve.engine.tensor_scalar, col["mag"], col["mag"], V["scale"][:, 0:1], None, ALU.mult)
        yield
        y = yb.next()
        yv = group(y.ap[:, :])
        ve.wait(y.free, m)
        for t in range(TILES):
            m = ve.do(ve.engine.scalar_tensor_tensor, yv[:, t, :], par[:, t // 2, t % 2, 0:C], col["mag"][:, t:t + 1], xv[:, t, :], ALU.mult, ALU.add)
        for s_ in list(B.values()) + list(Cc.values()) + [pb, x]:
            s_.free = [m]
        yield
        yield from rest(2)
        h = norm.begin(yv, 1e-5, m)
        yield from rest(4)
        m = norm.apply(ve, yv, yv, h)
        gp.wait(m)
        m = gp.do(gp.engine.tensor_tensor, yv, yv, V["gamma"][:, :].unsqueeze(1).to_broadcast([P, TILES, C]), ALU.mult)
        yield from rest(4)
        ve.wait(m, shifted)
        y.free = [ve.do(ve.engine.tensor_tensor, xg, xg, yv, ALU.add)]
        yield

    staggered(one, groups, LIVE, 16)
    st.run()


def setup1(nc, ctx, keep, d, K):
    V = ffn1_tensors(keep)
    T = attn1_tensors(keep)
    scratch = nc.dram_tensor("context", [16, P, 16 * 64], F32, kind="Internal").ap()
    st = Stage(nc, "setup1", ctx)
    bank = Slot(st.ps("bank", [P, 512])[:, :])
    banks = Ring([st.ps(f"bank{i}", [P, 512])[:, 0:P] for i in range(4)])
    ffn1_weights(st, d, V, K, bank)
    attn1_weights(st, d, T, K, bank, banks)
    st.run()
    return V, T, scratch


H1, DH, M1, DFF = 16, 64, 64, 512
WIDE = H1 * DH
PAIRS = WIDE // P
STRIP = 32
DN = float(DH) ** -0.25
EPS_KERNEL = 1e-6


def attn1_tensors(sb):
    pair = lambda name, shape: (sb(name + "_hi", shape, F32R), sb(name + "_lo", shape, F32R))
    T = {"wq": pair("twq", [P, WIDE]), "wk": pair("twk", [P, WIDE]), "gq": pair("tgq", [P, WIDE]),
         "gk": pair("tgk", [P, WIDE]), "vo": sb("tvo", [P, H1, C]), "w1": pair("tw1", [P, DFF]),
         "b1": sb("tb1", [P, DFF // P]), "w2": sb("tw2", [P, DFF // P, C]), "b2": sb("tb2", [P, 1]),
         "ones": sb("tones", [P, P]), "mask": sb("tmask", [P, PAIRS, STRIP]),
         "xsum": sb("txsum", [P, 16]), "ksum": sb("tksum", [P, 16, PAIRS]), "nmax": sb("tnmax", [P, 16])}
    for n in ("ln1_g", "ln1_b", "ln2_g", "ln2_b"):
        T[n] = sb("t" + n, [P, C])
    return T


def attn1_weights(st, d, T, K, bank, banks):
    ve, pe, gp = st.ve, st.pe, st.gp
    ld = Loads(st, "attn1_loads")
    D = lambda name: d["L1_attn_" + name]
    raw = {n: st.sb("raw_" + n, [P, WIDE]) for n in ("Wq", "Wk", "Wv")}
    wo, w1, pb, pT = st.sb("raw_wo", [P, PAIRS, C]), st.sb("raw_w1", [P, DFF]), st.sb("raw_proj", [P, P]), st.sb("projT", [P, P])
    turned = st.sb("turned", [P, PAIRS, P])
    z = ve.do(ve.engine.memset, pb[:, :], 0.0)
    for n in raw:
        ld.add(raw[n][:, :], D(n).rearrange("d h k -> d (h k)"), z)
    ld.add(wo[:, :, :], D("Wo").rearrange("h d o -> (h d) o").rearrange("(c p) o -> p c o", p=P))
    ld.add(w1[:, :], D("W1"))
    ld.add(T["w2"][:, :, :], D("W2").rearrange("(c p) o -> p c o", p=P))
    ld.add(T["b1"][:, :], D("b1").rearrange("(c p) -> p c", p=P), words=True)
    ld.add(T["b2"][:, :], D("b2").rearrange("(p a) -> p a", a=1), words=True)
    for n in ("ln1_g", "ln1_b", "ln2_g", "ln2_b"):
        ld.add(T[n][:, :], row(D(n)).to_broadcast([P, C]))
    for e in range(2):
        ld.add(pb[e * M1:(e + 1) * M1, e * DH:(e + 1) * DH], D("proj"))
    ve.do(ve.engine.memset, T["ones"][:, :], 1.0)
    a = ve.do(ve.engine.memset, T["mask"][:, :, :], 0.0)
    ve.wait(a)
    for e in range(2):
        for part in range(2):
            n = 2 * part + e
            ve.do(ve.engine.memset, T["mask"][e * M1:(e + 1) * M1, part * 4:part * 4 + 4, n:n + 1], 1.0)
    ve.wait(ld.all())
    for n, w in (("wq", "Wq"), ("wk", "Wk")):
        split_pair(ve, T[n][0][:, :], T[n][1][:, :], raw[w][:, :])
    split_pair(ve, T["w1"][0][:, :], T["w1"][1][:, :], w1[:, :])
    pe.wait(ld.all(), bank.free)
    m = pe.do(pe.engine.transpose, bank.ap[:, 0:P], pb[:, :], K["ident"][:, :])
    ve.wait(m)
    m = ve.do(ve.engine.tensor_scalar, pT[:, :], bank.ap[:, 0:P], DN, None, ALU.mult)
    pe.wait(m)
    bank.free = [m]

    def turn(w, after):
        for c in range(PAIRS):
            slot = banks.next()
            pe.wait(slot.free)
            m = pe.do(pe.engine.transpose, slot.ap, raw[w][:, c * P:(c + 1) * P], K["ident"][:, :])
            ve.wait(m, after)
            m = ve.do(ve.engine.tensor_copy, turned[:, c, :], slot.ap)
            slot.free = [m]
        return m

    product = None
    for g, w in (("gq", "Wq"), ("gk", "Wk")):
        turned_all = turn(w, product)
        for c in range(PAIRS):
            slot = banks.next()
            pe.wait(turned_all, slot.free)
            product = pe.do(pe.engine.matmul, slot.ap, turned[:, c, :], pT[:, :], start=True, stop=True)
            cut = slice(c * P, (c + 1) * P)
            slot.free = [split_pair(ve, T[g][0][:, cut], T[g][1][:, cut], slot.ap, product)]
    turned_all = turn("Wv", product)
    for h in range(H1):
        e = h % 2 * DH
        slot = banks.next()
        pe.wait(turned_all, slot.free)
        m = pe.do(pe.engine.matmul, slot.ap, turned[e:e + DH, h // 2, :], wo[e:e + DH, h // 2, :], start=True, stop=True)
        ve.wait(m)
        slot.free = [ve.do(ve.engine.tensor_copy, T["vo"][:, h, :], slot.ap)]


def heads_of(ap):
    return ap.rearrange("p (h m) -> p h m", m=M1)


def project_wide(pe, wide, pair, t, w):
    for half in range(2):
        cut = slice(half * 512, (half + 1) * 512)
        m = matmul_pairs(pe, wide.ap[:, cut], [v[:, t * P:(t + 1) * P] for v in pair.ap], [v[:, cut] for v in w], signal=half == 1)
    return m


def attn1_keys(nc, ctx, name, X, T, K, groups, scratch):
    st = Stage(nc, name, ctx)
    pe, ve, ac, gp = st.pe, st.ve, st.ac, st.gp
    ident = K["ident"]
    norm = Norm(st, K, 3)
    xn = Ring([st.sb(f"xn{i}", [P, GROUP]) for i in range(3)])
    pairs = Ring([(st.sb(f"xh{i}", [P, GROUP], F32R)[:, :], st.sb(f"xl{i}", [P, GROUP], F32R)[:, :]) for i in range(2)])
    sq = Ring([st.sb(f"sq{i}", [P, WIDE]) for i in range(2)])
    feats = Ring([st.sb(f"feat{i}", [P, TILES, WIDE]) for i in range(2)])
    esum = Ring([st.sb(f"esum{i}", [P, WIDE]) for i in range(2)])
    out = Ring([st.sb(f"ctx{i}", [P, WIDE]) for i in range(2)])
    diag = Ring([st.sb(f"diag{i}", [P, H1]) for i in range(2)])
    top = Ring([st.sb(f"top{i}", [P, TILES + 2]) for i in range(2)])
    misc = Ring([st.ps(f"misc{i}", [P, 512])[:, :] for i in range(2)])
    wide = Ring([st.ps(f"wide{i}", [P, 1024])[:, :] for i in range(3)])
    dmas = [SlotDma(st, f"out{i}") for i in range(2)]

    def one(g):
        xg = X[:, g, :, :]
        h = norm.begin(xg, 1e-5)
        yield from rest(3)
        yield from opened(xn)
        x = xn.next()
        xv = group(x.ap[:, :])
        m = norm.apply(ve, xv, xg, h, x.free)
        yield from rest(2)
        yield from opened(misc)
        bank = misc.next()
        m = transpose_tiles(st, bank, xv, ident, C, m)
        yield from opened(pairs)
        pair = pairs.next()
        ready = evacuate_pair(st, pair, bank, m)
        bank.free = [ve.do(ve.engine.tensor_reduce, T["xsum"][:, g:g + 1], bank.ap, AX, ALU.add)]
        yield from rest(2)
        yield from opened(feats)
        f = feats.next()
        yield from opened(top)
        tp = top.next()
        ve.wait(f.free, tp.free)
        for t in range(TILES):
            yield from opened(wide)
            kb = wide.next()
            yield from opened(wide)
            db = wide.next()
            pe.wait(ready, kb.free)
            m = project_wide(pe, kb, pair, t, T["wk"])
            pe.wait(db.free)
            m2 = project_wide(pe, db, pair, t, T["gk"])
            yield
            yield from opened(sq)
            s = sq.next()
            ac.wait(m, s.free)
            m = ac.do(ac.engine.activation, s.ap[:, :], kb.ap, ACT.Square, scale=0.25)
            kb.free = [m]
            yield from opened(diag)
            dg = diag.next()
            ve.wait(m2)
            top_t = ve.do(ve.engine.tensor_reduce, tp.ap[:, t:t + 1], db.ap, AX, ALU.max)
            yield
            ve.wait(m, dg.free)
            m = ve.do(ve.engine.tensor_reduce, dg.ap[:, :], heads_of(s.ap[:, :]), AX, ALU.add)
            s.free = [m]
            ve.wait(m)
            m = ve.do(ve.engine.tensor_tensor, heads_of(f.ap[:, t, :]), heads_of(db.ap), dg.ap[:, :].unsqueeze(2).to_broadcast([P, H1, M1]), ALU.subtract)
            db.free, dg.free = [m], [m]
            yield
        pair.free = [m2]
        ve.wait(top_t)
        m = ve.do(ve.engine.tensor_reduce, tp.ap[:, TILES:TILES + 1], tp.ap[:, 0:TILES], AX, ALU.max)
        yield
        yield from opened(misc)
        bank = misc.next()
        pe.wait(m, bank.free)
        m = pe.do(pe.engine.transpose, bank.ap[0:1, 0:P], tp.ap[:, TILES:TILES + 1], ident[:, :])
        yield
        ve.wait(m)
        one_ = tp.ap[0:1, TILES + 1:TILES + 2]
        m = ve.do(ve.engine.tensor_reduce, one_, bank.ap[0:1, 0:P], AX, ALU.max)
        yield
        pe.wait(m)
        m = pe.do(pe.engine.matmul, bank.ap[:, P:P + 1], T["ones"][0:1, :], one_, start=True, stop=True)
        yield
        ve.wait(m)
        m = ve.do(ve.engine.tensor_scalar, T["nmax"][:, g:g + 1], bank.ap[:, P:P + 1], -1.0, None, ALU.mult)
        bank.free, tp.free = [m], [m]
        yield
        ac.wait(m)
        exps = []
        for t in range(TILES):
            exps.append(ac.do(ac.engine.activation, f.ap[:, t, :], f.ap[:, t, :], ACT.Exp, bias=T["nmax"][:, g:g + 1]))
            yield
        yield from opened(esum)
        es = esum.next()
        gp.wait(exps[1], es.free)
        m = gp.do(gp.engine.tensor_tensor, es.ap[:, :], f.ap[:, 0, :], f.ap[:, 1, :], ALU.add)
        for t in range(2, TILES):
            gp.wait(exps[t], m)
            m = gp.do(gp.engine.tensor_tensor, es.ap[:, :], es.ap[:, :], f.ap[:, t, :], ALU.add)
        summed = m
        yield from opened(wide)
        w = wide.next()
        pe.wait(w.free)
        for t in range(TILES):
            pe.wait(exps[t])
            for half in range(2):
                cut = slice(half * 512, (half + 1) * 512)
                m = pe.do(pe.engine.matmul, w.ap[:, cut], xv[:, t, :], f.ap[:, t, cut], start=t == 0, stop=t == TILES - 1)
            yield
        x.free, f.free = [m], [m, summed]
        yield from opened(out)
        o = out.next()
        dma = dmas[g % 2]
        ac.wait(m, o.free)
        m = ac.do(ac.engine.activation, o.ap[:, :], w.ap, ACT.Copy)
        w.free = [m]
        o.free = [dma.start(scratch[g], o.ap[:, :], m)]
        yield
        yield from opened(misc)
        bank = misc.next()
        pe.wait(summed, bank.free)
        for c in range(PAIRS):
            m = pe.do(pe.engine.matmul, bank.ap[:, c:c + 1], es.ap[:, c * P:(c + 1) * P], T["ones"][:, 0:1], start=True, stop=True, signal=c == PAIRS - 1)
        es.free = [m]
        ve.wait(m)
        bank.free = [ve.do(ve.engine.tensor_copy, T["ksum"][:, g, :], bank.ap[:, 0:PAIRS])]
        yield

    staggered(one, groups, 3, 12)
    for dma in dmas:
        if dma.count:
            st.sp.wait((dma.sem, dma.count))
    st.run()


def attn1_queries(nc, ctx, name, X, T, K, groups, scratch):
    st = Stage(nc, name, ctx)
    pe, ve, ac, gp = st.pe, st.ve, st.ac, st.gp
    ident = K["ident"]
    norm = Norm(st, K, 4)
    xn = Ring([st.sb(f"xn{i}", [P, GROUP]) for i in range(3)])
    pairs = Ring([(st.sb(f"xh{i}", [P, GROUP], F32R)[:, :], st.sb(f"xl{i}", [P, GROUP], F32R)[:, :]) for i in range(2)])
    pairs2 = Ring([(st.sb(f"yh{i}", [P, GROUP], F32R)[:, :], st.sb(f"yl{i}", [P, GROUP], F32R)[:, :]) for i in range(2)])
    sq = Ring([st.sb(f"sq{i}", [P, WIDE]) for i in range(2)])
    cin = Ring([st.sb(f"cin{i}", [P, WIDE]) for i in range(2)])
    mem = Ring([st.sb(f"mem{i}", [P, PAIRS, C]) for i in range(2)])
    den = Ring([st.sb(f"den{i}", [P, PAIRS, STRIP]) for i in range(2)])
    denT = Ring([st.sb("denT", [P, GROUP])])
    rec = Ring([st.sb(f"rec{i}", [P, TILES, H1]) for i in range(2)])
    qf = Ring([st.sb(f"qf{i}", [P, GROUP]) for i in range(12)])
    yT = Ring([st.sb(f"yT{i}", [P, GROUP]) for i in range(2)])
    y1 = Ring([st.sb(f"y1_{i}", [P, GROUP]) for i in range(2)])
    y2 = Ring([st.sb(f"y2_{i}", [P, GROUP]) for i in range(2)])
    neg = Ring([st.sb(f"neg{i}", [P, GROUP]) for i in range(2)])
    pos = Ring([st.sb(f"pos{i}", [P, GROUP]) for i in range(2)])
    hid = Ring([st.sb(f"hid{i}", [P, GROUP]) for i in range(2)])
    bT = Ring([st.sb(f"bT{i}", [P, GROUP], F32R) for i in range(2)])
    rT = Ring([st.sb("rT", [P, GROUP], F32R)])
    top = Ring([st.sb(f"top{i}", [P, TILES, H1]) for i in range(2)])
    dg = Ring([st.sb(f"dg{i}", [P, TILES, H1]) for i in range(2)])
    bp = Ring([st.sb(f"bp{i}", [P, TILES, 2 * H1], F32R) for i in range(2)])
    shift, xeps, ksum, nm = st.sb("shift", [P, 16]), st.sb("xeps", [P, 16]), st.sb("ksum", [P, 16, PAIRS]), st.sb("nm", [P, 1])
    misc = Ring([st.ps("misc0", [P, 512])[:, :]])
    wide = Ring([st.ps(f"wide{i}", [P, 512])[:, :] for i in range(3)])
    half = Ring([st.ps(f"half{i}", [P, 512])[:, :] for i in range(2)])
    acc = Slot(st.ps("acc", [P, 512])[:, :])
    facc = Slot(st.ps("facc", [P, 512])[:, :])
    dmas = [SlotDma(st, f"in{i}") for i in range(2)]
    for s in bT.slots + rT.slots:
        s.free = [ve.do(ve.engine.memset, s.ap[:, :].bitcast(F32), 0.0)]
    m = ve.do(ve.engine.tensor_reduce, nm[:, :], T["nmax"][:, 0:groups], AX, ALU.min)
    ac.wait(m)
    shifted = ac.do(ac.engine.activation, shift[:, 0:groups], T["nmax"][:, 0:groups], ACT.Exp, scale=-1.0, bias=nm[:, :])
    ve.do(ve.engine.tensor_scalar, xeps[:, 0:groups], T["xsum"][:, 0:groups], EPS_KERNEL, None, ALU.mult)
    ve.wait(shifted)
    m = ve.do(ve.engine.tensor_tensor, ksum[:, 0:groups, :], T["ksum"][:, 0:groups, :], shift[:, 0:groups].unsqueeze(2).to_broadcast([P, groups, PAIRS]), ALU.mult)
    ve.wait(m)
    sums = ve.do(ve.engine.tensor_scalar, ksum[:, 0:groups, :], ksum[:, 0:groups, :], GROUP * EPS_KERNEL, None, ALU.add)

    def affine(q, v, gain, bias, *after):
        q.wait(*after)
        m = q.do(q.engine.tensor_tensor, v, v, T[gain][:, :].unsqueeze(1).to_broadcast([P, TILES, C]), ALU.mult)
        q.wait(m)
        return q.do(q.engine.tensor_tensor, v, v, T[bias][:, :].unsqueeze(1).to_broadcast([P, TILES, C]), ALU.add)

    def as_rows(ring, values, *after):
        yield from opened(bp)
        b = bp.next()
        ve.wait(b.free, *after)
        m = ve.do(ve.engine.tensor_copy, b.ap[:, :, 0:H1], values)
        yield
        ve.wait(m)
        split = m = ve.do(ve.engine.tensor_tensor, b.ap[:, :, H1:2 * H1], values, b.ap[:, :, 0:H1].bitcast(F32), ALU.subtract)
        yield from rest(1)
        yield from opened(misc)
        bank = misc.next()
        pe.wait(m, bank.free)
        for t in range(TILES):
            m = pe.do(pe.engine.transpose, bank.ap[0:2 * H1, t * P:(t + 1) * P], b.ap[:, t, :].bitcast(F32), ident[:, :], signal=t == TILES - 1)
        b.free = [m]
        yield from rest(1)
        yield from opened(ring)
        rows = ring.next()
        ac.wait(m, rows.free)
        rows.ready = ac.do(ac.engine.activation, rows.ap[0:2 * H1, :], bank.ap[0:2 * H1, :], ACT.Copy)
        rows.split = split
        bank.free = [rows.ready]
        yield from rest(2)
        return rows

    def one(g):
        yield from opened(cin)
        ci = cin.next()
        loaded = dmas[g % 2].start(ci.ap[:, :], scratch[g], ci.free)
        xg = X[:, g, :, :]
        h = norm.begin(xg, 1e-5)
        yield from rest(4)
        yield from opened(xn)
        x = xn.next()
        xv = group(x.ap[:, :])
        m = norm.apply(ve, xv, xg, h, x.free)
        yield from rest(3)
        yield from opened(misc)
        bank = misc.next()
        m = transpose_tiles(st, bank, xv, ident, C, m)
        yield
        yield from opened(pairs)
        pair = pairs.next()
        ready = evacuate_pair(st, pair, bank, m)
        yield from rest(3)
        gp.wait(loaded, sums)
        m = gp.do(gp.engine.tensor_scalar, ci.ap[:, :], ci.ap[:, :], shift[:, g:g + 1], xeps[:, g:g + 1], ALU.mult, ALU.add)
        yield from opened(den)
        dn = den.next()
        gp.wait(dn.free)
        dn.ready = gp.do(gp.engine.tensor_tensor, dn.ap[:, :, :], T["mask"][:, :, :],
                         ksum[:, g, :].unsqueeze(2).to_broadcast([P, PAIRS, STRIP]), ALU.mult)
        yield from opened(top)
        tp = top.next()
        yield from opened(dg)
        d_ = dg.next()
        ve.wait(tp.free, d_.free)
        for t in range(TILES):
            yield from opened(sq)
            s = sq.next()
            tile = [v[:, t * P:(t + 1) * P] for v in pair.ap]
            for side in range(2):
                cut = slice(side * 512, (side + 1) * 512)
                yield from opened(wide)
                bank = wide.next()
                pe.wait(ready, bank.free)
                m1 = matmul_pairs(pe, bank.ap, tile, [v[:, cut] for v in T["wq"]])
                ac.wait(m1, s.free)
                m1 = ac.do(ac.engine.activation, s.ap[:, cut], bank.ap, ACT.Square, scale=0.25)
                bank.free = [m1]
                yield from opened(wide)
                bank = wide.next()
                pe.wait(bank.free)
                m2 = matmul_pairs(pe, bank.ap, tile, [v[:, cut] for v in T["gq"]])
                ve.wait(m2)
                bank.free = [ve.do(ve.engine.tensor_reduce, tp.ap[:, t, side * 8:side * 8 + 8], heads_of(bank.ap), AX, ALU.max)]
                yield
            ve.wait(m1)
            m1 = ve.do(ve.engine.tensor_reduce, d_.ap[:, t, :], heads_of(s.ap[:, :]), AX, ALU.add)
            s.free = [m1]
        yield from opened(mem)
        mm = mem.next()
        for side in range(2):
            yield from opened(wide)
            w = wide.next()
            pe.wait(m, w.free)
            wv = w.ap.rearrange("p (c o) -> p c o", o=C)
            for hd in range(side * 8, side * 8 + 8):
                e = hd % 2 * M1
                m3 = pe.do(pe.engine.matmul, wv[e:e + M1, hd // 2 - side * 4, :], ci.ap[:, hd * M1:(hd + 1) * M1], T["vo"][:, hd, :], start=True, stop=True, signal=hd % 8 == 7)
            ac.wait(m3, mm.free)
            mm.ready = ac.do(ac.engine.activation, mm.ap[:, side * 4:side * 4 + 4, :], wv, ACT.Copy)
            w.free = [mm.ready]
            yield
        ci.free = [m3]
        yield from rest(2)
        ve.wait(m1)
        m = ve.do(ve.engine.scalar_tensor_tensor, tp.ap[:, :, :], tp.ap[:, :, :], -1.0, d_.ap[:, :, :], ALU.mult, ALU.subtract)
        bt = yield from as_rows(bT, tp.ap[:, :, :], m)
        tp.free, d_.free = [bt.split], [m]
        fs = []

        def denominators(part):
            for j in range(4):
                c = 4 * part + j
                pe.wait(fs[c].ready, dn.ready)
                m = pe.do(pe.engine.matmul, acc.ap[j * STRIP:(j + 1) * STRIP, :], dn.ap[:, c, :], fs[c].ap[:, :],
                          start=part == 0, stop=part == 1)
            return m

        for c in range(PAIRS):
            yield from opened(qf)
            f = qf.next()
            yield from opened(half)
            bk = half.next()
            pe.wait(bk.free, bt.ready)
            matmul_pairs(pe, bk.ap, [v[:, c * P:(c + 1) * P] for v in T["gq"]], pair.ap, stop=False, signal=False)
            m = pe.do(pe.engine.matmul, bk.ap, K["spread"][:, c, :], bt.ap[:, :], start=False, stop=True)
            yield
            ac.wait(m, f.free)
            a = ac.do(ac.engine.activation, f.ap[:, :], bk.ap, ACT.Exp)
            bk.free = [a]
            yield
            ve.wait(a)
            f.ready = ve.do(ve.engine.tensor_scalar, f.ap[:, :], f.ap[:, :], EPS_KERNEL, None, ALU.add)
            fs.append(f)
            yield
            if c == 5:
                while acc.held:
                    yield
                pe.wait(acc.claim().free)
                denominators(0)
        pair.free, bt.free = [m], [m]
        yield from rest(3)
        m = denominators(1)
        dn.free = [m]
        yield from opened(denT)
        dT = denT.next()
        yield
        ac.wait(m, dT.free)
        evacuated = m = ac.do(ac.engine.activation, dT.ap[:, :], acc.ap, ACT.Copy)
        yield from rest(2)
        yield from opened(misc)
        bank = misc.next()
        m = transpose_tiles(st, bank, group(dT.ap[:, :]), ident, C, m)
        dT.free = [m]
        yield from rest(2)
        yield from opened(rec)
        r = rec.next()
        ve.wait(m, r.free)
        m = ve.do(ve.engine.reciprocal, r.ap[:, :, :].rearrange("p t (j r) -> p t j r", j=4),
                  bank.ap.rearrange("p (t j r) -> p t j r", t=TILES, j=4)[:, :, :, 0:4])
        bank.free = [m]
        bt = yield from as_rows(rT, r.ap[:, :, :], m)
        r.free = [bt.split]

        def gather(c):
            pe.wait(fs[c].divided, mm.ready, evacuated)
            m = pe.do(pe.engine.matmul, acc.ap, mm.ap[:, c, :], fs[c].ap[:, :], start=c == 0, stop=c == PAIRS - 1)
            fs[c].free = [m]
            return m

        for c, f in enumerate(fs):
            yield from opened(half)
            bk = half.next()
            pe.wait(bt.ready, bk.free)
            spread = pe.do(pe.engine.matmul, bk.ap, K["spread"][:, 2 * (c % 4) + c // 4, :], bt.ap[:, :], start=True, stop=True)
            yield
            ve.wait(spread, f.ready)
            f.divided = ve.do(ve.engine.tensor_tensor, f.ap[:, :], f.ap[:, :], bk.ap, ALU.mult)
            bk.free = [f.divided]
            if c >= 1:
                gather(c - 1)
            yield
        bt.free = [spread]
        m = gather(PAIRS - 1)
        mm.free = [m]
        yield from opened(yT)
        y = yT.next()
        ac.wait(m, y.free)
        m = ac.do(ac.engine.activation, y.ap[:, :], acc.ap, ACT.Copy)
        acc.free = [m]
        yield
        yield from opened(misc)
        bank = misc.next()
        m = untranspose_tiles(st, bank, y.ap, ident, C, m)
        y.free = [m]
        yield from opened(y1)
        o = y1.next()
        ov = group(o.ap[:, :])
        yield from rest(1)
        ve.wait(m, o.free)
        m = ve.do(ve.engine.tensor_tensor, ov, group(bank.ap), xv, ALU.add)
        bank.free, x.free = [m], [m]
        h = norm.begin(ov, 1e-6, m)
        yield from rest(4)
        m = norm.apply(ve, ov, ov, h)
        yield
        m = affine(gp, ov, "ln1_g", "ln1_b", m)
        yield from rest(7)
        yield from opened(misc)
        bank = misc.next()
        m = transpose_tiles(st, bank, ov, ident, C, m)
        pair = pairs2.next()
        m = evacuate_pair(st, pair, bank, m)
        yield from rest(2)
        pe.wait(m)
        up = []

        def down():
            c, s = up.pop(0)
            pe.wait(s.ready)
            if c == 0:
                pe.wait(facc.free)
            m = pe.do(pe.engine.matmul, facc.ap, T["w2"][:, c, :], s.ap[:, :], start=c == 0, stop=c == DFF // P - 1)
            s.free = [m]
            return m

        while facc.held:
            yield
        facc.claim()
        for c in range(DFF // P):
            yield from opened(half)
            bk = half.next()
            pe.wait(bk.free)
            m = matmul_pairs(pe, bk.ap, [v[:, c * P:(c + 1) * P] for v in T["w1"]], pair.ap)
            last = m
            yield
            n, p, s = neg.next(), pos.next(), hid.next()
            ve.wait(m, n.free)
            m1 = ve.do(ve.engine.tensor_scalar, n.ap[:, :], bk.ap, T["b1"][:, c:c + 1], 0.0, ALU.add, ALU.min)
            ac.wait(m1, p.free)
            m = ac.do(ac.engine.activation, p.ap[:, :], bk.ap, ACT.Relu, bias=T["b1"][:, c:c + 1])
            bk.free = [m]
            m = ac.do(ac.engine.activation, n.ap[:, :], n.ap[:, :], ACT.Exp)
            ve.wait(m, s.free)
            s.ready = ve.do(ve.engine.scalar_tensor_tensor, s.ap[:, :], n.ap[:, :], -1.0, p.ap[:, :], ALU.add, ALU.add)
            n.free, p.free = [s.ready], [s.ready]
            up.append((c, s))
            if c >= 1:
                down()
            yield
        pair.free = [last]
        m = down()
        yield from opened(yT)
        y = yT.next()
        ac.wait(m, y.free)
        m = ac.do(ac.engine.activation, y.ap[:, :], facc.ap, ACT.Identity, bias=T["b2"][:, :])
        facc.free = [m]
        yield
        yield from opened(misc)
        bank = misc.next()
        m = untranspose_tiles(st, bank, y.ap, ident, C, m)
        y.free = [m]
        yield from opened(y2)
        r = y2.next()
        rv = group(r.ap[:, :])
        ve.wait(m, r.free)
        m = ve.do(ve.engine.tensor_tensor, rv, group(bank.ap), ov, ALU.add)
        bank.free, o.free = [m], [m]
        h = norm.begin(rv, 1e-6, m)
        yield from rest(4)
        m = norm.apply(ve, rv, rv, h)
        m = affine(gp, rv, "ln2_g", "ln2_b", m)
        yield from rest(5)
        ve.wait(m)
        r.free = [ve.do(ve.engine.tensor_tensor, xg, xg, rv, ALU.add)]
        yield

    staggered(one, groups, 3, 40)
    st.run()


def attn1(nc, ctx, name, X, T, K, groups, scratch):
    attn1_keys(nc, ctx, name + "k", X, T, K, groups, scratch)
    attn1_queries(nc, ctx, name + "q", X, T, K, groups, scratch)


def row(vector):
    return vector.rearrange("(a n) -> a n", a=1)


def constant_tensors(sb):
    return {"ident": sb("ident", [P, P]), "order": sb("order", [P, 16]), "minus_half": sb("minus_half", [P, 16]),
            "spread": sb("spread", [P, CHUNKS - 1, P], F32R)}


def constants(st, K):
    gp, ve = st.gp, st.ve
    select = lambda ap, **kw: gp.then(gp.engine.affine_select,
        out=ap, in_=ap, compare_op=ALU.not_equal, fill=1.0, **kw)
    gp.do(gp.engine.memset, K["ident"][:, :], 0.0)
    select(K["ident"][:, :], base=0, pattern=[[-1, P]], channel_multiplier=1)
    gp.do(gp.engine.memset, K["minus_half"][:, :], -0.5)
    for j in range(16):
        last = gp.do(gp.engine.memset, K["order"][:, j:j + 1], float(16 - j))
    raw = st.sb("spread_raw", [P, CHUNKS - 1, P])
    gp.do(gp.engine.memset, raw[:, :, :], 0.0)
    view = raw[:, :, :].rearrange("p c (e i) -> p c e i", e=2)
    for half in range(2):
        last = select(view, base=-EXPERTS * half, pattern=[[-2, CHUNKS - 1], [-1, 2], [0, INTER]], channel_multiplier=1)
    ve.wait(last)
    K["ready"] = [last, ve.do(ve.engine.tensor_copy, K["spread"][:, :, :], raw[:, :, :])]


def macaron(nc, d, out, groups):
    with ExitStack() as ctx:
        keep = lambda name, shape, dt=F32: ctx.enter_context(nc.sbuf_tensor(name, shape, dt))
        X = keep("X", [P, groups, TILES, C])
        K = constant_tensors(keep)
        layer0 = ExitStack()
        keep0 = lambda name, shape, dt=F32: layer0.enter_context(nc.sbuf_tensor(name, shape, dt))
        W = ffn0_tensors(keep0)
        A = attn0_tensors(keep0)
        st = Stage(nc, "setup", ctx)
        for g in range(0, groups, 2):
            lane = Loads(st, f"x{g}", st.ac)
            n = min(2, groups - g)
            lane.add(X[:, g:g + n, :, :].rearrange("p b t c -> p b (t c)"),
                     d["L0_attn_x"][g:g + n].rearrange("b (p t) c -> p b (t c)", p=P))
            st.ve.wait(lane.all())
        bank = Slot(st.ps("bank", [P, 512])[:, :])
        constants(st, K)
        ffn0_weights(st, d, W, K, bank)
        attn0_weights(st, d, A, K, bank)
        st.run()
        ffn0(nc, ctx, "ffnA", X, W, K, groups)
        attn0(nc, ctx, "att0", X, A, K, groups)
        ffn0(nc, ctx, "ffnB", X, W, K, groups)
        layer0.close()
        layer1 = ExitStack()
        keep1 = lambda name, shape, dt=F32: layer1.enter_context(nc.sbuf_tensor(name, shape, dt))
        V, T, scratch = setup1(nc, ctx, keep1, d, K)
        ffn1(nc, ctx, "ffnC", X, V, K, groups)
        attn1(nc, ctx, "att1", X, T, K, groups, scratch)
        ffn1(nc, ctx, "ffnD", X, V, K, groups)
        layer1.close()
        st = Stage(nc, "store", ctx)
        lane = Loads(st, "out")
        for g in range(0, groups, 2):
            n = min(2, groups - g)
            lane.add(out[g:g + n].rearrange("b (p t) c -> p b (t c)", p=P),
                     X[:, g:g + n, :, :].rearrange("p b t c -> p b (t c)"))
        st.sp.wait(lane.all())
        st.run()


NAMES = ["L0_attn_x", "L0_attn_qkv_w", "L0_attn_qkv_b", "L0_attn_proj_w", "L0_attn_proj_b",
         "L0_ffn_gate_w", "L0_ffn_gate_b", "L0_ffn_We1", "L0_ffn_be1", "L0_ffn_We2", "L0_ffn_be2",
         "L0_ffn_We3", "L0_ffn_be3", "L0_ffn_ws1", "L0_ffn_bs1", "L0_ffn_ws2", "L0_ffn_bs2",
         "L0_ffn_ws3", "L0_ffn_bs3", "L1_attn_Wq", "L1_attn_Wk", "L1_attn_Wv", "L1_attn_Wo",
         "L1_attn_proj", "L1_attn_W1", "L1_attn_b1", "L1_attn_W2", "L1_attn_b2", "L1_attn_ln1_g",
         "L1_attn_ln1_b", "L1_attn_ln2_g", "L1_attn_ln2_b", "L1_ffn_signatures_raw",
         "L1_ffn_knot_values", "L1_ffn_temperature", "L1_ffn_compress_w1", "L1_ffn_compress_b1",
         "L1_ffn_compress_w2", "L1_ffn_compress_b2", "L1_ffn_spline_w1", "L1_ffn_spline_b1",
         "L1_ffn_spline_w2", "L1_ffn_spline_b2", "L1_ffn_directions", "L1_ffn_norm_gamma",
         "L1_ffn_norm_beta", "L1_ffn_output_scale"]


def kernel(**inputs):
    import concourse.bacc as bacc
    from concourse.bass_utils import run_bass_kernel_spmd

    nc = bacc.Bacc("TRN2", target_bir_lowering=False, num_devices=1)
    arrays, dram = {}, {}
    for name in NAMES:
        arrays[name] = np.ascontiguousarray(inputs[name])
        dram[name] = nc.dram_tensor(name, arrays[name].shape, F32, kind="ExternalInput").ap()
    shape = arrays["L0_attn_x"].shape
    out = nc.dram_tensor("out", shape, F32, kind="ExternalOutput").ap()
    macaron(nc, dram, out, shape[0])
    result = run_bass_kernel_spmd(nc, [arrays], core_ids=[0])
    return result.results[0]["out"]
```
